# Optimizing a Trainium2 kernel written in Bass

```python
import numpy as np
import jax
import jax.numpy as jnp

def _softmax(x, axis=-1):
    return jax.nn.softmax(x, axis=axis)

def _gelu(x):
    return jax.nn.gelu(x, approximate=True)

def _silu(x):
    return jax.nn.silu(x)

def _sigmoid(x):
    return jax.nn.sigmoid(x)

def _layernorm(x, axis=-1, eps=1e-05):
    m = jnp.mean(x, axis=axis, keepdims=True)
    v = jnp.var(x, axis=axis, keepdims=True)
    return (x - m) / jnp.sqrt(v + eps)

def _scatter_add(tgt, idx, src, axis=0):
    return tgt.at[idx].add(src)

def _segment_sum(src, seg, n):
    return jax.ops.segment_sum(src, seg, n)
kernel_name = 'mk_decoder_preln_d2_seqx_r4_f13feb'

def setup_inputs(seed: int=0):
    np.random.seed(seed)
    _w = jnp.asarray

    def _rec_inputs():
        import jax
        import jax.numpy as jnp
        _rk = jax.random.key(seed)
        x = -0.000125 + 0.9999 * jax.random.normal(jax.random.fold_in(_rk, 1), (4, 512, 512), jnp.float32)
        _lenS = 512 - jax.random.randint(jax.random.fold_in(_rk, 7), (4,), 0, max(1, 512 // 4) + 1, jnp.int32)
        _lenS2 = 512 - jax.random.randint(jax.random.fold_in(_rk, 8), (4,), 0, max(1, 512 // 4) + 1, jnp.int32)
        itok_BxS_13_99985 = jax.random.randint(jax.random.fold_in(_rk, 11), (4, 512), 13, 99986, jnp.int32)
        _ctx_2048P = jax.random.normal(jax.random.fold_in(_rk, 12), (4, 16, 512), jnp.float32)
        _ctx_2048c = jax.random.dirichlet(jax.random.fold_in(_rk, 512), 0.3 * jnp.ones((16,), jnp.float32), (4, 512))
        _ctx_2048t = jnp.einsum('bsk,bkd->bsd', _ctx_2048c, _ctx_2048P)
        _ctx_2048t = _ctx_2048t * jax.lax.rsqrt(jnp.mean(jnp.square(_ctx_2048t)) + 1e-12) * 0.953939
        ctx_2048 = 6.82029e-06 + 0.0200006 * (_ctx_2048t + 0.3 * jax.random.normal(jax.random.fold_in(_rk, 612), (4, 512, 512), jnp.float32))
        _validS = jnp.arange(512)[None, :] < _lenS[:, None]
        _validS2 = jnp.arange(512)[None, :] < _lenS2[:, None]
        _causal = jnp.tril(jnp.ones((512, 512), dtype=bool))
        mask_BxS2_ik0 = jnp.where(jnp.broadcast_to(_validS2[:, :], (4, 512)), 0, 1).astype(jnp.int32)
        return (x, itok_BxS_13_99985, ctx_2048, mask_BxS2_ik0)
    x, itok_BxS_13_99985, ctx_2048, mask_BxS2_ik0 = _rec_inputs()

    def _L0_attn_setup():
        import jax, jax.numpy as jnp
        import numpy as np
        EMBED_DIM = 512
        NUM_HEADS = 16
        HEAD_DIM = EMBED_DIM // NUM_HEADS
        BASE = 10000.0

        def rotate_half(x):
            half = x.shape[-1] // 2
            x1, x2 = (x[..., :half], x[..., half:])
            return jnp.concatenate([-x2, x1], axis=-1)

        def apply_rope(x, base=BASE):
            S, Dh = (x.shape[-2], x.shape[-1])
            inv_freq = 1.0 / base ** (jnp.arange(0, Dh, 2, dtype=jnp.float32) / Dh)
            t = jnp.arange(S, dtype=jnp.float32)
            freqs = jnp.einsum('i,j->ij', t, inv_freq)
            emb = jnp.concatenate([freqs, freqs], axis=-1)
            return x * jnp.cos(emb) + rotate_half(x) * jnp.sin(emb)
        key = jax.random.key(seed)
        ks = jax.random.split(key, 9)
        B, S, D = (2, 512, EMBED_DIM)
        xavier = lambda k, shape: jax.random.uniform(k, shape, jnp.float32, -1.0, 1.0) * float(np.sqrt(6.0 / (shape[0] + shape[1])))
        return {'x': jax.random.normal(ks[0], (B, S, D), jnp.float32), 'q_w': xavier(ks[1], (D, D)), 'k_w': xavier(ks[2], (D, D)), 'v_w': xavier(ks[3], (D, D)), 'q_b': jnp.zeros((D,), jnp.float32), 'k_b': jnp.zeros((D,), jnp.float32), 'v_b': jnp.zeros((D,), jnp.float32), 'out_w': xavier(ks[4], (D, D)), 'out_b': jnp.zeros((D,), jnp.float32)}
    _L0_attn_all = _L0_attn_setup()
    _L0_attn_in = {k: v for k, v in _L0_attn_all.items() if k in ('q_w', 'k_w', 'v_w', 'q_b', 'k_b', 'v_b', 'out_w', 'out_b')}
    del _L0_attn_all

    def _L0_xattn_setup():
        import jax, jax.numpy as jnp
        import numpy as np
        B, S, D = (4, 1024, 512)
        E = 4
        F = 2048 // E
        VOCAB = 25000
        key = jax.random.key(seed)
        k1, k2, k3, k4, k5 = jax.random.split(key, 5)
        hidden_states = jax.random.normal(k1, (B, S, D), dtype=jnp.float32)
        token_ids = jax.random.randint(k2, (B, S), 0, VOCAB, dtype=jnp.int64)
        Wg = jax.random.normal(k3, (E, F, D), dtype=jnp.float32) * 0.02
        Wu = jax.random.normal(k4, (E, F, D), dtype=jnp.float32) * 0.02
        Wd = jax.random.normal(k5, (E, D, F), dtype=jnp.float32) * 0.02
        return {'hidden_states': hidden_states, 'token_ids': token_ids, 'Wg': Wg, 'Wu': Wu, 'Wd': Wd}
    _L0_xattn_all = _L0_xattn_setup()
    _L0_xattn_in = {k: v for k, v in _L0_xattn_all.items() if k in ()}
    del _L0_xattn_all

    def _L0_ffn_setup():
        import jax, jax.numpy as jnp
        import numpy as np
        DIM = 512
        INNER = 2048
        EPS_RMS = 1e-06
        EPS_Q = 1e-05

        def simple_rms_norm(x, dim):
            rms = jnp.sqrt(jnp.mean(x * x, axis=-1, keepdims=True) + EPS_RMS)
            return x / rms * dim ** (-0.5)

        def activation_quant(x):
            scale = 127.0 / jnp.clip(jnp.max(jnp.abs(x), axis=-1, keepdims=True), EPS_Q)
            return jnp.clip(jnp.round(x * scale), -128, 127) / scale

        def weight_quant(w):
            return jnp.sign(w) * jnp.mean(jnp.abs(w))

        def bit_linear(x, w, b, dim_in):
            x_norm = simple_rms_norm(x, dim_in)
            x_q = activation_quant(x_norm)
            w_q = weight_quant(w)
            return jnp.einsum('bsd,od->bso', x_q, w_q) + b
        key = jax.random.key(seed)
        k1, k2, k3, k4, k5 = jax.random.split(key, 5)
        bound1 = 1.0 / np.sqrt(DIM)
        bound2 = 1.0 / np.sqrt(INNER)
        return {'x': jax.random.normal(k1, (4, 512, DIM), dtype=jnp.float32), 'w1': jax.random.uniform(k2, (INNER, DIM), jnp.float32, -bound1, bound1), 'b1': jax.random.uniform(k3, (INNER,), jnp.float32, -bound1, bound1), 'w2': jax.random.uniform(k4, (DIM, INNER), jnp.float32, -bound2, bound2), 'b2': jax.random.uniform(k5, (DIM,), jnp.float32, -bound2, bound2)}
    _L0_ffn_all = _L0_ffn_setup()
    _L0_ffn_in = {k: v for k, v in _L0_ffn_all.items() if k in ('w1', 'b1', 'w2', 'b2')}
    del _L0_ffn_all

    def _L1_attn_setup():
        import jax, jax.numpy as jnp
        import numpy as np
        B, S, H = (2, 512, 512)
        NH = 16
        HD = H // NH
        SCALE = 1.0 / float(np.sqrt(HD))
        key = jax.random.key(seed)
        ks = jax.random.split(key, 5)
        hidden_states = jax.random.normal(ks[0], (B, S, H), dtype=jnp.float32)
        w_qkv = jax.random.normal(ks[1], (3 * H, H), dtype=jnp.float32) * (1.0 / np.sqrt(H))
        b_qkv = jax.random.normal(ks[2], (3 * H,), dtype=jnp.float32) * 0.01
        w_out = jax.random.normal(ks[3], (H, H), dtype=jnp.float32) * (1.0 / np.sqrt(H))
        b_out = jax.random.normal(ks[4], (H,), dtype=jnp.float32) * 0.01
        return {'hidden_states': hidden_states, 'w_qkv': w_qkv, 'b_qkv': b_qkv, 'w_out': w_out, 'b_out': b_out}
    _L1_attn_all = _L1_attn_setup()
    _L1_attn_in = {k: v for k, v in _L1_attn_all.items() if k in ('w_qkv', 'b_qkv', 'w_out', 'b_out')}
    del _L1_attn_all

    def _L1_xattn_setup():
        import jax, jax.numpy as jnp
        import numpy as np
        import math
        H = 512
        NH = 16
        HD = H // NH
        EPS_LN = 1e-05
        RES_SCALE_MAX = 0.3

        def _nan_clean(x, lim=10000.0):
            return jnp.nan_to_num(x, nan=0.0, posinf=lim, neginf=-lim)
        key = jax.random.key(seed)
        ks = jax.random.split(key, 12)
        B, S, T = (4, 512, 64)
        std = 1.0 / math.sqrt(H)
        return {'hidden_states': jax.random.normal(ks[0], (B, S, H), jnp.float32), 'audio_tokens': jax.random.normal(ks[1], (B, T, H), jnp.float32), 'attention_mask': jax.random.randint(ks[2], (B, T), 0, 2, jnp.int32), 'Wq': jax.random.normal(ks[3], (H, H), jnp.float32) * std, 'bq': jnp.zeros((H,), jnp.float32), 'Wk': jax.random.normal(ks[4], (H, H), jnp.float32) * std, 'bk': jnp.zeros((H,), jnp.float32), 'Wv': jax.random.normal(ks[5], (H, H), jnp.float32) * std, 'bv': jnp.zeros((H,), jnp.float32), 'Wo': jax.random.normal(ks[6], (H, H), jnp.float32) * std, 'bo': jnp.zeros((H,), jnp.float32), 'ln_gamma': jnp.ones((H,), jnp.float32), 'ln_beta': jnp.zeros((H,), jnp.float32), 'residual_scale': jnp.float32(0.05)}
    _L1_xattn_all = _L1_xattn_setup()
    _L1_xattn_in = {k: v for k, v in _L1_xattn_all.items() if k in ('Wq', 'bq', 'Wk', 'bk', 'Wv', 'bv', 'Wo', 'bo', 'ln_gamma', 'ln_beta', 'residual_scale')}
    del _L1_xattn_all

    def _L1_ffn_setup():
        import jax, jax.numpy as jnp
        import numpy as np
        FP8_MAX = 448.0
        SCALE_EPS = 1e-07
        key = jax.random.key(seed)
        k1, k2, k3 = jax.random.split(key, 3)
        in_f, out_f = (512, 512)
        x = jax.random.normal(k1, (4, 1024, in_f), dtype=jnp.float32)
        w_fp32 = jax.random.normal(k2, (out_f, in_f), dtype=jnp.float32) * (1.0 / np.sqrt(in_f))
        weight = w_fp32.astype(jnp.float8_e4m3fn).astype(jnp.float32)
        weight_scale = jnp.ones((), dtype=jnp.float32)
        bound = 1.0 / np.sqrt(in_f)
        bias = jax.random.uniform(k3, (out_f,), dtype=jnp.float32, minval=-bound, maxval=bound)
        return {'x': x, 'weight': weight, 'weight_scale': weight_scale, 'bias': bias}
    _L1_ffn_all = _L1_ffn_setup()
    _L1_ffn_in = {k: v for k, v in _L1_ffn_all.items() if k in ('weight', 'weight_scale', 'bias')}
    del _L1_ffn_all
    return {'x': x, 'itok_BxS_13_99985': itok_BxS_13_99985, 'ctx_2048': ctx_2048, 'mask_BxS2_ik0': mask_BxS2_ik0, 'L0_attn_q_w': _L0_attn_in['q_w'], 'L0_attn_k_w': _L0_attn_in['k_w'], 'L0_attn_v_w': _L0_attn_in['v_w'], 'L0_attn_q_b': _L0_attn_in['q_b'], 'L0_attn_k_b': _L0_attn_in['k_b'], 'L0_attn_v_b': _L0_attn_in['v_b'], 'L0_attn_out_w': _L0_attn_in['out_w'], 'L0_attn_out_b': _L0_attn_in['out_b'], 'L0_ffn_w1': _L0_ffn_in['w1'], 'L0_ffn_b1': _L0_ffn_in['b1'], 'L0_ffn_w2': _L0_ffn_in['w2'], 'L0_ffn_b2': _L0_ffn_in['b2'], 'L1_attn_w_qkv': _L1_attn_in['w_qkv'], 'L1_attn_b_qkv': _L1_attn_in['b_qkv'], 'L1_attn_w_out': _L1_attn_in['w_out'], 'L1_attn_b_out': _L1_attn_in['b_out'], 'L1_xattn_Wq': _L1_xattn_in['Wq'], 'L1_xattn_bq': _L1_xattn_in['bq'], 'L1_xattn_Wk': _L1_xattn_in['Wk'], 'L1_xattn_bk': _L1_xattn_in['bk'], 'L1_xattn_Wv': _L1_xattn_in['Wv'], 'L1_xattn_bv': _L1_xattn_in['bv'], 'L1_xattn_Wo': _L1_xattn_in['Wo'], 'L1_xattn_bo': _L1_xattn_in['bo'], 'L1_xattn_ln_gamma': _L1_xattn_in['ln_gamma'], 'L1_xattn_ln_beta': _L1_xattn_in['ln_beta'], 'L1_xattn_residual_scale': _L1_xattn_in['residual_scale'], 'L1_ffn_weight': _L1_ffn_in['weight'], 'L1_ffn_weight_scale': _L1_ffn_in['weight_scale'], 'L1_ffn_bias': _L1_ffn_in['bias']}

def reference(x, itok_BxS_13_99985, ctx_2048, mask_BxS2_ik0, L0_attn_q_w, L0_attn_k_w, L0_attn_v_w, L0_attn_q_b, L0_attn_k_b, L0_attn_v_b, L0_attn_out_w, L0_attn_out_b, L0_ffn_w1, L0_ffn_b1, L0_ffn_w2, L0_ffn_b2, L1_attn_w_qkv, L1_attn_b_qkv, L1_attn_w_out, L1_attn_b_out, L1_xattn_Wq, L1_xattn_bq, L1_xattn_Wk, L1_xattn_bk, L1_xattn_Wv, L1_xattn_bv, L1_xattn_Wo, L1_xattn_bo, L1_xattn_ln_gamma, L1_xattn_ln_beta, L1_xattn_residual_scale, L1_ffn_weight, L1_ffn_weight_scale, L1_ffn_bias):
    import jax
    import jax.numpy as jnp

    def _L0_attn_ref(x, q_w, k_w, v_w, q_b, k_b, v_b, out_w, out_b):
        import jax, jax.numpy as jnp
        import numpy as np
        EMBED_DIM = 512
        NUM_HEADS = 16
        HEAD_DIM = EMBED_DIM // NUM_HEADS
        BASE = 10000.0

        def rotate_half(x):
            half = x.shape[-1] // 2
            x1, x2 = (x[..., :half], x[..., half:])
            return jnp.concatenate([-x2, x1], axis=-1)

        def apply_rope(x, base=BASE):
            S, Dh = (x.shape[-2], x.shape[-1])
            inv_freq = 1.0 / base ** (jnp.arange(0, Dh, 2, dtype=jnp.float32) / Dh)
            t = jnp.arange(S, dtype=jnp.float32)
            freqs = jnp.einsum('i,j->ij', t, inv_freq)
            emb = jnp.concatenate([freqs, freqs], axis=-1)
            return x * jnp.cos(emb) + rotate_half(x) * jnp.sin(emb)
        B, S, D = x.shape
        H, Dh = (NUM_HEADS, HEAD_DIM)
        scaling = Dh ** (-0.5)
        q = (x @ q_w.T + q_b).reshape(B, S, H, Dh).transpose(0, 2, 1, 3)
        k = (x @ k_w.T + k_b).reshape(B, S, H, Dh).transpose(0, 2, 1, 3)
        v = (x @ v_w.T + v_b).reshape(B, S, H, Dh).transpose(0, 2, 1, 3)
        q = apply_rope(q)
        k = apply_rope(k)
        attn = jnp.einsum('bhqd,bhkd->bhqk', q, k) * scaling
        probs = jax.nn.softmax(attn, axis=-1)
        out = jnp.einsum('bhqk,bhkd->bhqd', probs, v)
        out = out.transpose(0, 2, 1, 3).reshape(B, S, D)
        return out @ out_w.T + out_b

    def _L0_xattn_ref(hidden_states, token_ids, Wg, Wu, Wd):
        import jax, jax.numpy as jnp
        import numpy as np
        B, S, D = (4, 1024, 512)
        E = 4
        F = 2048 // E
        VOCAB = 25000
        tokens_per_expert = VOCAB // E
        tid = jnp.clip(token_ids, 0, VOCAB - 1)
        expert_ids = jnp.minimum(tid // tokens_per_expert, E - 1)
        out = jnp.zeros_like(hidden_states)
        for e in range(E):
            g = jax.nn.silu(jnp.einsum('bsd,fd->bsf', hidden_states, Wg[e]))
            u = jnp.einsum('bsd,fd->bsf', hidden_states, Wu[e])
            y = jnp.einsum('bsf,df->bsd', g * u, Wd[e])
            out = jnp.where((expert_ids == e)[..., None], y, out)
        return out

    def _L0_ffn_ref(x, w1, b1, w2, b2):
        import jax, jax.numpy as jnp
        import numpy as np
        DIM = 512
        INNER = 2048
        EPS_RMS = 1e-06
        EPS_Q = 1e-05

        def simple_rms_norm(x, dim):
            rms = jnp.sqrt(jnp.mean(x * x, axis=-1, keepdims=True) + EPS_RMS)
            return x / rms * dim ** (-0.5)

        def activation_quant(x):
            scale = 127.0 / jnp.clip(jnp.max(jnp.abs(x), axis=-1, keepdims=True), EPS_Q)
            return jnp.clip(jnp.round(x * scale), -128, 127) / scale

        def weight_quant(w):
            return jnp.sign(w) * jnp.mean(jnp.abs(w))

        def bit_linear(x, w, b, dim_in):
            x_norm = simple_rms_norm(x, dim_in)
            x_q = activation_quant(x_norm)
            w_q = weight_quant(w)
            return jnp.einsum('bsd,od->bso', x_q, w_q) + b
        h = bit_linear(x, w1, b1, DIM)
        h = jax.nn.gelu(h, approximate=False)
        return bit_linear(h, w2, b2, INNER)

    def _L1_attn_ref(hidden_states, w_qkv, b_qkv, w_out, b_out):
        import jax, jax.numpy as jnp
        import numpy as np
        B, S, H = (2, 512, 512)
        NH = 16
        HD = H // NH
        SCALE = 1.0 / float(np.sqrt(HD))
        b, s, _ = hidden_states.shape
        qkv = jnp.einsum('bsh,oh->bso', hidden_states, w_qkv) + b_qkv
        qkv = qkv.reshape(b, s, 3, NH, HD).transpose(2, 0, 3, 1, 4)
        q, k, v = (qkv[0], qkv[1], qkv[2])
        scores = jnp.einsum('bnqd,bnkd->bnqk', q, k) * SCALE
        attn = jax.nn.softmax(scores, axis=-1)
        out = jnp.einsum('bnqk,bnkd->bnqd', attn, v)
        out = out.transpose(0, 2, 1, 3).reshape(b, s, H)
        return jnp.einsum('bsh,oh->bso', out, w_out) + b_out

    def _L1_xattn_ref(hidden_states, audio_tokens, attention_mask, Wq, bq, Wk, bk, Wv, bv, Wo, bo, ln_gamma, ln_beta, residual_scale):
        import jax, jax.numpy as jnp
        import numpy as np
        import math
        H = 512
        NH = 16
        HD = H // NH
        EPS_LN = 1e-05
        RES_SCALE_MAX = 0.3

        def _nan_clean(x, lim=10000.0):
            return jnp.nan_to_num(x, nan=0.0, posinf=lim, neginf=-lim)
        B, S, _ = hidden_states.shape
        T = audio_tokens.shape[1]
        hs = _nan_clean(hidden_states).astype(jnp.float32)
        at = _nan_clean(audio_tokens).astype(jnp.float32)

        def proj(x, W, b, L):
            y = x @ W.T + b
            return y.reshape(B, L, NH, HD).transpose(0, 2, 1, 3)
        q = _nan_clean(proj(hs, Wq, bq, S))
        k = _nan_clean(proj(at, Wk, bk, T))
        v = _nan_clean(proj(at, Wv, bv, T))
        scale = max(math.sqrt(HD), 1e-08)
        scores = jnp.einsum('bhsd,bhtd->bhst', q, k) / scale
        scores = jnp.clip(scores, -50.0, 50.0)
        scores = jnp.nan_to_num(scores, nan=0.0, posinf=50.0, neginf=-50.0)
        attend = (attention_mask.astype(jnp.float32) > 0.5)[:, None, None, :]
        scores = jnp.where(attend, scores, -10000.0)
        scores = jnp.clip(scores, -50.0, 50.0)
        probs = jax.nn.softmax(scores, axis=-1)
        probs = jnp.nan_to_num(probs, nan=0.0, posinf=1.0, neginf=0.0)
        probs = probs / (probs.sum(axis=-1, keepdims=True) + 1e-08)
        ctx = jnp.einsum('bhst,bhtd->bhsd', probs, v)
        ctx = ctx.transpose(0, 2, 1, 3).reshape(B, S, H)
        delta = _nan_clean(ctx @ Wo.T + bo)
        rs = jnp.clip(residual_scale, 0.0, RES_SCALE_MAX)
        delta = rs * delta
        mu = delta.mean(axis=-1, keepdims=True)
        var = jnp.mean((delta - mu) ** 2, axis=-1, keepdims=True)
        delta = (delta - mu) / jnp.sqrt(var + EPS_LN) * ln_gamma + ln_beta
        return delta

    def _L1_ffn_ref(x, weight, weight_scale, bias):
        import jax, jax.numpy as jnp
        import numpy as np
        FP8_MAX = 448.0
        SCALE_EPS = 1e-07
        scale = jnp.maximum(jnp.max(jnp.abs(x)) / FP8_MAX, SCALE_EPS)
        x_q = (x / scale).astype(jnp.float8_e4m3fn).astype(jnp.float32)
        w = weight * weight_scale
        out = jnp.einsum('bsi,oi->bso', x_q, w) + bias
        return out
    x = x + _L0_attn_ref(_layernorm(x, axis=-1), L0_attn_q_w, L0_attn_k_w, L0_attn_v_w, L0_attn_q_b, L0_attn_k_b, L0_attn_v_b, L0_attn_out_w, L0_attn_out_b)
    x = x + _L0_xattn_ref(_layernorm(x, axis=-1), itok_BxS_13_99985, ctx_2048, ctx_2048, ctx_2048)
    x = x + _L0_ffn_ref(_layernorm(x, axis=-1), L0_ffn_w1, L0_ffn_b1, L0_ffn_w2, L0_ffn_b2)
    x = x + _L1_attn_ref(_layernorm(x, axis=-1), L1_attn_w_qkv, L1_attn_b_qkv, L1_attn_w_out, L1_attn_b_out)
    x = x + _L1_xattn_ref(_layernorm(x, axis=-1), ctx_2048, mask_BxS2_ik0, L1_xattn_Wq, L1_xattn_bq, L1_xattn_Wk, L1_xattn_bk, L1_xattn_Wv, L1_xattn_bv, L1_xattn_Wo, L1_xattn_bo, L1_xattn_ln_gamma, L1_xattn_ln_beta, L1_xattn_residual_scale)
    x = x + _L1_ffn_ref(_layernorm(x, axis=-1), L1_ffn_weight, L1_ffn_weight_scale, L1_ffn_bias)
    return x

_drawn_inputs = setup_inputs


def setup_inputs(seed=0):
    import zlib

    import numpy as np

    out = dict(_drawn_inputs(seed))
    spreads = {'L0_attn_q_b': (0.0, 0.404),
     'L0_attn_k_b': (0.0, 0.395),
     'L0_attn_v_b': (0.0, 0.1),
     'L0_attn_out_b': (0.0, 0.1),
     'L1_xattn_bq': (0.0, 2.0),
     'L1_xattn_bk': (0.0, 2.0),
     'L1_xattn_bv': (0.0, 0.1),
     'L1_xattn_bo': (0.0, 0.1),
     'L1_xattn_ln_gamma': (1.0, 0.2),
     'L1_xattn_ln_beta': (0.0, 0.1)}
    factors = {'L0_ffn_w1': 3.826,
     'L0_ffn_b1': 3.253,
     'L0_ffn_w2': 2.898,
     'L1_attn_b_qkv': 3.163,
     'L1_attn_b_out': 3.631,
     'L1_xattn_Wq': 8.0,
     'L1_xattn_Wk': 8.0,
     'L1_ffn_bias': 200.0}
    for name, (base, spread) in spreads.items():
        noise = np.random.default_rng([zlib.crc32(name.encode()), seed]).standard_normal(out[name].shape)
        drawn = base * np.exp(spread * noise) if base else spread * noise
        out[name] = jnp.asarray(drawn.astype(out[name].dtype))
    for name, factor in factors.items():
        out[name] = (out[name] * factor).astype(out[name].dtype)
    return out
```

```python
from contextlib import ExitStack

import concourse.bass as bass
from concourse import mybir

P = 128
NB = 4
S = 512
D = 512
NH = 16
HD = D // NH
T = S // P
C = D // P
HG = P // HD
NE = 4
INNER = 2048
NI = INNER // P
WSCALE = 64.0
MSCALE = 64.0
ARENA = 27 * 1024 + 640
EPS = 1e-5
MAGIC = 1.5 * 2.0 ** 23
VOCAB_PER_EXPERT = 25000 // NE

ALU = mybir.AluOpType
ACT = mybir.ActivationFunctionType
AX = mybir.AxisListType
F32 = mybir.dt.float32
F16 = mybir.dt.float16
I32 = mybir.dt.int32
RMAX = bass.bass_isa.ReduceOp.max
RADD = bass.bass_isa.ReduceOp.add
SOFTMAX_SCALE = HD ** -0.5


def tile3(ap):
    return ap.rearrange("p (c t) -> p c t", t=P)


class Chain:

    def __init__(self, phase, sem, per, b):
        self.at, self.sem, self.per, self.base, self.n = phase.at, sem, per, b * per, 0

    def put(self, ins):
        ins.then_inc(self.sem, 1)
        self.n += 1

    def wait(self, eng):
        eng.wait_ge(*self.at(self.sem, self.base + self.n))

    def close(self):
        assert self.n == self.per, (self.sem, self.n, self.per)


class Machine:

    def __init__(self, nc, ctx, io):
        self.nc, self.ctx, self.io = nc, ctx, io
        sb = lambda name, shape, dt: ctx.enter_context(nc.sbuf_tensor(name, shape, dt))
        self.x = sb("x", [P, NB * T, D], F32)
        self.xn = sb("xn", [P, T, D], F32)
        self.xt = sb("xt", [P, 2, C, S], F16)
        self.w = sb("w", [P, 4, 2, C, D], F16)
        self.raw = sb("raw", [P, 2, C, D], F32)
        self.arena = sb("arena", [P, ARENA], F32)
        self.ident = sb("ident", [P, P], F32)
        self.ident16 = sb("ident16", [P, P], F16)
        self.mhalf = sb("mhalf", [P, T], F32)
        self.carrier = sb("carrier", [P, 1], F32)
        self.eps = sb("eps", [P, T], F32)
        self.stats = sb("stats", [P, T, 6], F32)
        self.mv = sb("mv", [P, T, 2], F32)
        self.rstd = sb("rstd", [P, T], F32)
        self.ps = ctx.enter_context(nc.psum_tensor("ps", [P, 8, 512], F32))
        self.phase_end = ctx.enter_context(nc.semaphore("phase_end"))
        self.sems, self.count = {}, {}
        self.used = 0

    def sem(self, name, total):
        if name not in self.sems:
            self.sems[name] = self.ctx.enter_context(self.nc.semaphore(name))
            self.count[name] = 1
        self.taken.append(name)
        assert self.taken.count(name) == 1, name
        self.start[name] = self.count[name]
        self.count[name] += total
        return self.sems[name]

    def next_phase(self):
        self.used, self.taken, self.start = 0, [], {}
        return self.start

    def take(self, n, dt=F32):
        words = (n + 1) // 2 if dt == F16 else n
        a = self.arena[:, self.used:self.used + words]
        self.used += words
        assert self.used <= ARENA, self.used
        return a if dt == F32 else a.bitcast(dt)

    def barrier(self, eng, k):
        eng.drain().then_inc(self.phase_end, 1)
        eng.wait_ge(self.phase_end, 5 * (k + 1))


def counter(start):
    return lambda sem, n: (sem, start[sem.name] + n)


def slot(ap, i):
    return ap[:, bass.ds(i, 1), :].rearrange("p a n -> p (a n)")


class Norm:

    def __init__(self, m, name, calls):
        self.m = m
        self.sums = m.sem(f"{name}_bn_sums", calls * T)
        self.moments = m.sem(f"{name}_moments", calls * T)
        self.rstd_ready = m.sem(f"{name}_rstd_ready", calls)
        self.eps_added = m.sem(f"{name}_eps_added", calls)
        self.xn_ready = m.sem(f"{name}_xn_ready", calls * T)
        self.at = counter(m.start)

    def dve(self, v, b, src, dst):
        m = self.m
        for i in range(T):
            v.bn_stats(m.stats[:, i, :], src(i)).then_inc(self.sums, 1)
        v.wait_ge(*self.at(self.sums, b * T + T))
        v.memset(m.carrier[:], 0.0)
        for i in range(T):
            v.bn_aggr(m.mv[:, i, :], m.stats[:, i, :]).then_inc(self.moments, 1)
        v.wait_ge(*self.at(self.moments, b * T + T))
        v.wait_ge(*self.at(self.rstd_ready, b + 1))
        for i in range(T):
            v.tensor_scalar(dst(i), src(i), m.mv[:, i, 0:1], m.rstd[:, i:i + 1],
                            ALU.subtract, ALU.mult).then_inc(self.xn_ready, 1)

    def pool(self, g, b):
        m = self.m
        g.wait_ge(*self.at(self.moments, b * T + T))
        g.tensor_tensor(m.rstd[:], m.mv[:, :, 1:2].rearrange("p t a -> p (t a)"), m.eps[:],
                        ALU.add).then_inc(self.eps_added, 1)
        g.wait_ge(*self.at(self.eps_added, b + 1))
        g.tensor_tensor(m.rstd[:], m.rstd[:], m.mhalf[:], ALU.pow).then_inc(self.rstd_ready, 1)


class Phase:
    def __init__(self, m, name):
        self.m, self.name = m, name
        self.at = counter(m.next_phase())
        self.io = m.io

    def sem(self, name, total):
        return self.m.sem(name, total)

    def sems(self, name, n, total):
        return [self.sem(f"{name}{i}", total) for i in range(n)]

    def pe(self, pe): pass
    def act(self, act): pass
    def dve(self, v): pass
    def pool(self, g): pass
    def sp(self, sp): pass


class Start(Phase):

    def __init__(self, m):
        super().__init__(m, "start")
        self.loaded = [self.sem("x_loaded", 16), self.sem("const_loaded", 16)]
        self.norm = Norm(m, "norm", 1)
        self.consts = self.sem("consts_done", 2)

    def sp(self, sp):
        m = self.m
        sp.dma_start(m.x[:], self.io["x"].rearrange("b (t p) d -> p (b t) d", p=P)).then_inc(self.loaded[0], 16)
        sp.dma_start(m.ident[:], self.io["ident"]).then_inc(self.loaded[1], 16)
        sp.wait_ge(*self.at(self.loaded[0], 16))
        sp.wait_ge(*self.at(self.loaded[1], 16))

    def pool(self, g):
        g.memset(self.m.mhalf[:], -0.5).then_inc(self.consts, 1)
        g.memset(self.m.eps[:], EPS).then_inc(self.consts, 1)
        g.wait_ge(*self.at(self.consts, 2))
        self.norm.pool(g, 0)

    def dve(self, v):
        m = self.m
        v.wait_ge(*self.at(self.loaded[1], 16))
        v.tensor_copy(m.ident16[:], m.ident[:])
        v.wait_ge(*self.at(self.loaded[0], 16))
        self.norm.dve(v, 0, lambda i: m.x[:, i, :], lambda i: m.xn[:, i, :])


class Weights(Phase):

    def __init__(self, m, name, mats):
        super().__init__(m, name)
        self.mats = mats
        n = len(mats)
        self.raw_loaded = [self.sem(f"raw_loaded{k}", 16 * ((n - k + 1) // 2)) for k in range(2)]
        self.high_done, self.low_done = self.sem("high_done", n), self.sem("low_done", n)

    def sp(self, sp):
        for n, a in enumerate(self.mats):
            if n >= 2:
                sp.wait_ge(*self.at(self.low_done, n - 1))
            sp.dma_start(self.m.raw[:, n % 2], a.rearrange("(c p) o -> p c o", p=P)).then_inc(self.raw_loaded[n % 2], 16)
        for k in range(min(2, len(self.mats))):
            sp.wait_ge(*self.at(self.raw_loaded[k], 16 * ((len(self.mats) - k + 1) // 2)))

    def act(self, act):
        m = self.m
        for n in range(len(self.mats)):
            act.wait_ge(*self.at(self.raw_loaded[n % 2], 16 * (n // 2 + 1)))
            act.activation(m.w[:, n, 0], m.raw[:, n % 2], ACT.Copy, scale=WSCALE).then_inc(self.high_done, 1)

    def dve(self, v):
        m = self.m
        for n in range(len(self.mats)):
            v.wait_ge(*self.at(self.high_done, n + 1))
            v.scalar_tensor_tensor(out=m.w[:, n, 1].rearrange("p c o -> p (c o)"),
                                   in0=m.raw[:, n % 2].rearrange("p c o -> p (c o)"), scalar=WSCALE,
                                   in1=m.w[:, n, 0].rearrange("p c o -> p (c o)"),
                                   op0=ALU.mult, op1=ALU.subtract).then_inc(self.low_done, 1)


def three_passes(pe, out, left, right, cl, cr, start=True, stop=True):
    n = len(cl)
    for k in range(n):
        for a, (l, r) in enumerate(((0, 0), (0, 1), (1, 0))):
            last = pe.matmul(out, left[l](cl[k]), right[r](cr[k]), start=start and k == 0 and a == 0,
                             stop=stop and k == n - 1 and a == 2)
    return last


class Attention(Phase):

    def __init__(self, m, name, q_bias, k_bias, v_bias, out_bias, rope=False, cross=False):
        super().__init__(m, name)
        self.rope, self.cross = rope, cross
        self.biases = (k_bias, q_bias)
        self.v_bias, self.out_bias = v_bias, out_bias
        take = m.take
        self.qst = take(NH * S, F16).rearrange("p (h t) -> p h t", h=NH)
        self.kst = take(NH * S, F16).rearrange("p (h t) -> p h t", h=NH)
        self.qf = take(4 * C * S, F16).rearrange("p (w a c t) -> p w a c t", w=2, a=2, c=C)
        self.v = take(T * D).rearrange("p (t d) -> p t d", t=T)
        self.pt = take(2 * HG * S).rearrange("p (n t) -> p n t", n=2)
        self.ct = take(2 * C * S, F16).rearrange("p (a c t) -> p a c t", a=2, c=C)
        self.qb = take(2 * S).rearrange("p (n t) -> p n t", n=2)
        if rope:
            self.t1 = take(2 * S).rearrange("p (n t) -> p n t", n=2)
            self.t2 = take(S)
            self.qr = take(2 * S).rearrange("p (n t) -> p n t", n=2)
            self.cos, self.sin, self.rot = take(S), take(S), take(P)
        self.ctxn, self.rden = take(S), take(S)
        self.vb, self.ob = take(D), take(D)
        self.pb = take(2 * C)
        self.mx = take(HG * T)
        self.mt = take(P, F16)
        self.ones = take(HD)
        if cross:
            self.cth = m.raw[:, 1].rearrange("p c o -> p (c o)").bitcast(F16).rearrange("p (a c t) -> p a c t", a=2, c=C)
            self.delta = take(T * D).rearrange("p (t d) -> p t d", t=T)
            self.gamma, self.beta = take(D), take(D)
            self.rs, self.rs64 = take(1), take(1)
            self.mask, self.hi = take(NB * T, I32), take(NB * T)
            self.raw_loaded, self.audio_high, self.audio_low = self.sem("raw_loaded0", 16 * NB), self.sem("audio_high", NB), self.sem("audio_low", NB)
            self.clipped = self.sem("clipped", NB * NH)
            self.dnorm = Norm(m, "delta", NB)
            self.scaled = self.sem("gamma_applied", NB * T)
        seq = [("xt", i) for i in range(T)]
        if rope:
            for c in range(2 * C):
                seq.append(("proj", c))
                if c:
                    seq.append(("rot", c - 1))
            seq.append(("rot", 2 * C - 1))
        else:
            seq += [("proj", c) for c in range(2 * C)]
        seq += [("v", i) for i in range(T)] + [("out", i) for i in range(T)]
        self.seq = seq
        self.place = {it: (n % 4, n // 4) for n, it in enumerate(seq)}
        self.uses = len(seq) // 4
        assert len(seq) % 4 == 0
        u = NB * self.uses
        self.bank_full, self.bank_free = self.sems("bank_full", 4, u), self.sems("bank_free", 4, u)
        u = 0 if cross else NB * self.ROWS * C // 2
        self.row_full, self.row_free = self.sems("rowmax_full", 2, u), self.sems("rowmax_free", 2, u)
        self.norm = Norm(m, "norm", NB)
        s = self.sem
        self.xt_high, self.fh, self.fl = s("xt_high", NB * T), s("qk_high", NB * 2 * C), s("qk_low", NB * 2 * C)
        self.kdma, self.qdma, self.mdma = s("k_stacked", NB * 12 * 16), s("q_stacked", NB * 12 * 16), s("max_stacked", 0 if cross else NB * C * 16)
        self.t1_ready, self.rotated = s("cos_part", rope * NB * 2 * C), s("rotated", NB * (2 * C if rope else T if cross else 0))
        self.st_full, self.exp_done, self.pv_done = (s(n, NB * NH) for n in ("scores_full", "exp_done", "pv_done"))
        self.ctx_free, self.rden_done, self.ch, self.cl = (s(n, NB * C) for n in ("ctx_free", "rden_done", "ctx_high", "ctx_low"))
        self.bias_added = s("bias_added", NB * T)
        self.nconst = 16 * (4 + 3 * rope + 4 * cross)
        self.const, self.consts_done = s("const_loaded", self.nconst), s("consts_done", 2 + 5 * cross)

    def wait_free(self, eng, item, b):
        k, u = self.place[item]
        eng.wait_ge(*self.at(self.bank_free[k], b * self.uses + u))

    def wait_full(self, eng, item, b):
        k, u = self.place[item]
        eng.wait_ge(*self.at(self.bank_full[k], b * self.uses + u + 1))

    def wait_read(self, eng, item, b):
        k, u = self.place[item]
        eng.wait_ge(*self.at(self.bank_free[k], b * self.uses + u + 1))

    def bank(self, item):
        return self.m.ps[:, self.place[item][0], :]

    ROWS = HG * T + 1

    def row(self, g, j):
        n = self.ROWS * g + j
        return n % 2, n // 2

    def row_free_wait(self, eng, g, j, b, read=0):
        k, u = self.row(g, j)
        eng.wait_ge(*self.at(self.row_free[k], b * (self.ROWS * C // 2) + u + read))

    def row_full_wait(self, eng, g, j, b):
        k, u = self.row(g, j)
        eng.wait_ge(*self.at(self.row_full[k], b * (self.ROWS * C // 2) + u + 1))

    SHARE = [range(0, 6), range(6, 11), range(11, 16), range(0)]

    def sp(self, sp):
        m, io = self.m, self.io
        row = lambda a: a.rearrange("(a n) -> a n", a=1).broadcast_to([P, D])
        loads = [(self.vb, row(self.v_bias)), (self.ob, row(self.out_bias)),
                 (self.pb[:, 0:C], self.biases[0]),
                 (self.pb[:, C:2 * C], self.biases[1])]
        if self.rope:
            loads += [(self.cos, io["rope_cos"]), (self.sin, io["rope_sin"]), (self.rot, io["rope_rot"])]
        if self.cross:
            loads += [(self.gamma, row(io["L1_xattn_ln_gamma"])), (self.beta, row(io["L1_xattn_ln_beta"])),
                      (self.rs, io["L1_xattn_residual_scale"].rearrange("(a n) -> a n", a=1).broadcast_to([P, 1])),
                      (self.mask, io["mask_cols"])]
        for dst, src in loads:
            sp.dma_start(dst, src).then_inc(self.const, 16)
        sp.wait_ge(*self.at(self.const, 16 * len(loads)))
        with sp.Fori(0, NB) as b:
            if self.cross:
                sp.wait_ge(*self.at(self.audio_low, b))
                sp.dma_start(m.raw[:, 0],
                             io["ctxT"][bass.ds(b * D, D), :].rearrange("(c p) o -> p c o", p=P)).then_inc(self.raw_loaded, 16)
            for w, stack, parts, sem, need in ((0, self.kst, (0, 0, 1), self.kdma, C), (1, self.qst, (0, 1, 0), self.qdma, 2 * C)):
                sp.wait_ge(*self.at(self.fl, b * 2 * C + need))
                for r, part in enumerate(parts):
                    for j in range(HG):
                        sp.dma_start(stack[HD * r:HD * (r + 1)].rearrange("p (c j) t -> p c j t", j=HG)[:, :, j, :],
                                     self.qf[HD * j:HD * (j + 1), w, part]).then_inc(sem, 16)
            if not self.cross:
                for g in range(C):
                    self.row_free_wait(sp, g, self.ROWS - 1, b, read=1)
                    sp.dma_start(self.qst[3 * HD:3 * HD + 1, HG * g:HG * (g + 1), :].rearrange("p h t -> p (h t)"),
                                 self.mt[0:HG * T, :]).then_inc(self.mdma, 16)

    def scores_rows(self):
        return 3 * HD if self.cross else 3 * HD + 1

    def pe_rowmax(self, pe, g, js, b):
        for j in js:
            head, t = HG * g + j // T, j % T
            self.row_free_wait(pe, g, j, b)
            pe.matmul(self.m.ps[:, 4 + self.row(g, j)[0], :], self.qst[0:3 * HD, head, t * P:(t + 1) * P],
                      self.kst[0:3 * HD, head, :], start=True, stop=True).then_inc(self.row_full[self.row(g, j)[0]], 1)

    def pe_turn_max(self, pe, g, b):
        self.row_free_wait(pe, g, self.ROWS - 2, b, read=1)
        self.row_free_wait(pe, g, self.ROWS - 1, b)
        k = self.row(g, self.ROWS - 1)[0]
        pe.transpose(self.m.ps[0:HG * T, 4 + k, 0:P], self.mx, self.m.ident[:]).then_inc(self.row_full[k], 1)

    def pe_values(self, pe, u, b):
        g, kb = divmod(u, T)
        pe.wait_ge(*self.at(self.exp_done, b * NH + u + 1))
        if kb == 0:
            pe.wait_ge(*self.at(self.ctx_free, b * C + g))
        for bank, left in ((6, lambda j: self.v[:, kb, HD * (HG * g + j):HD * (HG * g + j + 1)]), (7, lambda j: self.ones)):
            for j in range(HG):
                last = pe.matmul(self.m.ps[HD * j:HD * (j + 1), bank, :], left(j),
                                 self.pt[:, u % 2, j * S:(j + 1) * S], start=kb == 0, stop=kb == T - 1,
                                 tile_position=(0, HD * j))
        last.then_inc(self.pv_done, 1)

    def pe(self, pe):
        m = self.m
        xt = [lambda c: m.xt[:, 0, c, :], lambda c: m.xt[:, 1, c, :]]
        pe.wait_ge(*self.at(self.const, self.nconst))
        pe.wait_ge(*self.at(self.consts_done, 2 + self.cross * 5))
        with pe.Fori(0, NB) as b:
            rowmax_started = False
            for item in self.seq:
                kind, i = item
                if kind == "out":
                    if i == 0:
                        self.pe_heads(pe, b)
                    pe.wait_ge(*self.at(self.exp_done, b * NH + NH))
                self.wait_free(pe, item, b)
                out = self.bank(item)
                if kind == "xt":
                    if i == 0:
                        pe.wait_ge(*self.at(self.norm.xn_ready, b * T))
                    for c in range(C):
                        last = pe.transpose(out[:, c * P:(c + 1) * P], m.xn[:, i, c * P:(c + 1) * P], m.ident[:])
                elif kind == "proj":
                    if i == 0:
                        self.wait_read(pe, ("xt", T - 1), b)
                        if self.cross:
                            pe.wait_ge(*self.at(self.audio_low, b + 1))
                    w = i // C
                    c0 = (i % C) * P
                    src = xt if i >= C or not self.cross else [lambda c: self.cth[:, 0, c, :], lambda c: self.cth[:, 1, c, :]]
                    last = three_passes(pe, out, [lambda c: m.w[:, w, 0, c, c0:c0 + P], lambda c: m.w[:, w, 1, c, c0:c0 + P]],
                                        src, range(C), range(C))
                elif kind == "rot":
                    self.wait_read(pe, ("proj", i), b)
                    last = pe.matmul(out, self.rot, self.qb[:, i % 2, :], start=True, stop=True)
                elif kind == "v":
                    a = self.cth if self.cross else m.xt
                    last = three_passes(pe, out, [lambda c: a[:, 0, c, i * P:(i + 1) * P], lambda c: a[:, 1, c, i * P:(i + 1) * P]],
                                        [lambda c: m.w[:, 2, 0, c, :], lambda c: m.w[:, 2, 1, c, :]], range(C), range(C))
                else:
                    if i == 0:
                        pe.wait_ge(*self.at(self.cl, b * C + C))
                    last = three_passes(pe, out, [lambda c: self.ct[:, 0, c, i * P:(i + 1) * P], lambda c: self.ct[:, 1, c, i * P:(i + 1) * P]],
                                        [lambda c: m.w[:, 3, 0, c, :], lambda c: m.w[:, 3, 1, c, :]], range(C), range(C))
                last.then_inc(self.bank_full[self.place[item][0]], 1)
                if kind == "v" and not self.cross:
                    if i == 0:
                        pe.wait_ge(*self.at(self.kdma, (b + 1) * 16 * 12))
                        pe.wait_ge(*self.at(self.qdma, (b + 1) * 16 * 12))
                    self.pe_rowmax(pe, 0, range(T * i, T * (i + 1)), b)

    def pe_heads(self, pe, b):
        if self.cross:
            pe.wait_ge(*self.at(self.kdma, (b + 1) * 16 * 12))
            pe.wait_ge(*self.at(self.qdma, (b + 1) * 16 * 12))
        else:
            self.pe_turn_max(pe, 0, b)
        for i in range(T):
            self.wait_read(pe, ("v", i), b)
        R = self.scores_rows()
        for u in range(NH):
            g, kb = divmod(u, T)
            pe.wait_ge(*self.at(self.clipped if self.cross else self.exp_done, b * NH + u))
            if kb == 0 and not self.cross:
                pe.wait_ge(*self.at(self.mdma, (b * C + g + 1) * 16))
            for j in range(HG):
                last = pe.matmul(self.m.ps[:, j, :], self.kst[0:R, HG * g + j, kb * P:(kb + 1) * P],
                                 self.qst[0:R, HG * g + j, :], start=True, stop=True)
            last.then_inc(self.st_full, 1)
            if not self.cross and g + 1 < C:
                self.pe_rowmax(pe, g + 1, self.SHARE[kb], b)
                if kb == T - 1:
                    self.pe_turn_max(pe, g + 1, b)
            if u:
                self.pe_values(pe, u - 1, b)
        self.pe_values(pe, NH - 1, b)

    def act(self, act):
        m = self.m
        act.wait_ge(*self.at(self.const, self.nconst))
        act.wait_ge(*self.at(self.consts_done, 2 + self.cross * 5))
        descale = 1.0 / WSCALE
        with act.Fori(0, NB) as b:
            if self.cross:
                act.wait_ge(*self.at(self.raw_loaded, b * 16 + 16))
                act.wait_ge(*self.at(self.pv_done, b * NH))
                act.activation(self.cth[:, 0], m.raw[:, 0], ACT.Copy, scale=WSCALE).then_inc(self.audio_high, 1)
            for item in self.seq:
                kind, i = item
                if kind == "xt":
                    self.wait_full(act, item, b)
                    act.activation(m.xt[:, 0, :, i * P:(i + 1) * P], tile3(self.bank(item)), ACT.Copy).then_inc(self.xt_high, 1)
                elif kind == "proj":
                    self.wait_full(act, item, b)
                    if self.rope:
                        act.wait_ge(*self.at(self.t1_ready, b * 2 * C + max(i - 1, 0)))
                        if i >= 2:
                            self.wait_full(act, ("rot", i - 2), b)
                        elif i == 0:
                            act.wait_ge(*self.at(self.exp_done, b * NH))
                    else:
                        act.wait_ge(*self.at(self.fl, b * 2 * C + max(i - 1, 0)))
                    s = descale if i >= C or not self.cross else descale / WSCALE
                    act.activation(self.qb[:, i % 2, :], self.bank(item), ACT.Identity, scale=s,
                                   bias=self.pb[:, i:i + 1]).then_inc(self.bank_free[self.place[item][0]], 1)
            for u in range(NH):
                if self.cross:
                    act.wait_ge(*self.at(self.clipped, b * NH + u + 1))
                    src = self.pt[:, u % 2, :]
                else:
                    act.wait_ge(*self.at(self.st_full, b * NH + u + 1))
                    act.wait_ge(*self.at(self.pv_done, b * NH + max(u - 1, 0)))
                    src = m.ps[:, 0:4, :].rearrange("p a t -> p (a t)")
                act.activation(self.pt[:, u % 2, :], src, ACT.Exp, scale=SOFTMAX_SCALE).then_inc(self.exp_done, 1)

    def dve_rowmax(self, v, g, js, b):
        for j in js:
            k = self.row(g, j)[0]
            self.row_full_wait(v, g, j, b)
            v.tensor_reduce(self.mx[:, j:j + 1], self.m.ps[:, 4 + k, :], AX.X, ALU.max).then_inc(self.row_free[k], 1)

    def dve_turn_max(self, v, g, b):
        j = self.ROWS - 1
        k = self.row(g, j)[0]
        self.row_full_wait(v, g, j, b)
        v.wait_ge(*self.at(self.mdma, (b * C + g) * 16))
        v.tensor_scalar(self.mt[0:HG * T, :], self.m.ps[0:HG * T, 4 + k, 0:P], 1.0 / MSCALE, None,
                        ALU.mult).then_inc(self.row_free[k], 1)

    def dve_context(self, v, g, b):
        v.wait_ge(*self.at(self.pv_done, b * NH + T * (g + 1)))
        v.reciprocal(self.rden, self.m.ps[:, 7, :]).then_inc(self.rden_done, 1)
        v.wait_ge(*self.at(self.rden_done, b * C + g + 1))
        v.wait_ge(*self.at(self.cl, b * C + g))
        v.tensor_tensor(self.ctxn, self.m.ps[:, 6, :], self.rden, ALU.mult).then_inc(self.ctx_free, 1)
        v.wait_ge(*self.at(self.ctx_free, b * C + g + 1))
        v.tensor_copy(self.ct[:, 0, g, :], self.ctxn).then_inc(self.ch, 1)

    def dve(self, v):
        m = self.m
        n = self.nconst
        v.memset(self.ones, 1.0).then_inc(self.consts_done, 1)
        v.memset(self.kst[3 * HD:3 * HD + 1].rearrange("p h t -> p (h t)"), -MSCALE).then_inc(self.consts_done, 1)
        v.wait_ge(*self.at(self.const, n))
        if self.cross:
            top = 50.0 / SOFTMAX_SCALE
            v.tensor_scalar(self.hi, self.mask, 0.5, 2.0 * top, ALU.is_gt, ALU.mult).then_inc(self.consts_done, 1)
            v.tensor_scalar(self.rs, self.rs, 0.0, 0.3, ALU.max, ALU.min).then_inc(self.consts_done, 1)
            v.wait_ge(*self.at(self.consts_done, 4))
            v.tensor_scalar(self.hi, self.hi, -top, None, ALU.add).then_inc(self.consts_done, 1)
            v.tensor_scalar(self.rs64, self.rs, 1.0 / WSCALE, None, ALU.mult).then_inc(self.consts_done, 1)
            v.tensor_scalar(self.ob, self.ob, self.rs, None, ALU.mult).then_inc(self.consts_done, 1)
            v.wait_ge(*self.at(self.consts_done, 7))
        with v.Fori(0, NB) as b:
            if self.cross:
                v.wait_ge(*self.at(self.audio_high, b + 1))
                v.scalar_tensor_tensor(out=self.cth[:, 1].rearrange("p c t -> p (c t)"), in0=m.raw[:, 0].rearrange("p c t -> p (c t)"),
                                       scalar=WSCALE, in1=self.cth[:, 0].rearrange("p c t -> p (c t)"),
                                       op0=ALU.mult, op1=ALU.subtract).then_inc(self.audio_low, 1)
            for item in self.seq:
                kind, i = item
                k = self.place[item][0]
                if kind == "xt":
                    v.wait_ge(*self.at(self.xt_high, b * T + i + 1))
                    v.tensor_tensor(m.xt[:, 1, :, i * P:(i + 1) * P], tile3(self.bank(item)), m.xt[:, 0, :, i * P:(i + 1) * P],
                                    ALU.subtract).then_inc(self.bank_free[k], 1)
                elif kind == "proj" and not self.rope:
                    self.wait_read(v, item, b)
                    v.tensor_copy(self.qf[:, i // C, 0, i % C, :], self.qb[:, i % 2, :]).then_inc(self.fh, 1)
                elif kind == "rot":
                    self.wait_full(v, item, b)
                    v.wait_ge(*self.at(self.rotated, b * 2 * C + i))
                    v.tensor_tensor(self.t2, self.bank(item), self.sin, ALU.mult).then_inc(self.bank_free[k], 1)
                    self.wait_read(v, item, b)
                    v.wait_ge(*self.at(self.t1_ready, b * 2 * C + i + 1))
                    v.wait_ge(*self.at(self.fl, b * 2 * C + max(i - 1, 0)))
                    v.tensor_tensor(self.qr[:, i % 2, :], self.t1[:, i % 2, :], self.t2, ALU.add).then_inc(self.rotated, 1)
                    v.wait_ge(*self.at(self.rotated, b * 2 * C + i + 1))
                    v.tensor_copy(self.qf[:, i // C, 0, i % C, :], self.qr[:, i % 2, :]).then_inc(self.fh, 1)
                elif kind == "v":
                    self.wait_full(v, item, b)
                    v.scalar_tensor_tensor(out=self.v[:, i, :], in0=self.bank(item),
                                           scalar=1.0 / WSCALE / (WSCALE if self.cross else 1.0),
                                           in1=self.vb, op0=ALU.mult, op1=ALU.add).then_inc(self.bank_free[k], 1)
                    if not self.cross:
                        self.dve_rowmax(v, 0, range(T * i, T * (i + 1)), b)
                elif kind == "out" and i == 0:
                    self.dve_heads(v, b)
                if kind == "out":
                    self.wait_full(v, item, b)
                    if self.cross:
                        v.scalar_tensor_tensor(out=self.delta[:, i, :], in0=self.bank(item), scalar=self.rs64, in1=self.ob,
                                               op0=ALU.mult, op1=ALU.add).then_inc(self.bank_free[k], 1)
                    else:
                        v.wait_ge(*self.at(self.bias_added, b * T + i + 1))
                        xs = slot(m.x, b * T + i)
                        v.scalar_tensor_tensor(out=xs, in0=self.bank(item), scalar=1.0 / WSCALE, in1=xs,
                                               op0=ALU.mult, op1=ALU.add).then_inc(self.bank_free[k], 1)
            for i in range(T):
                self.wait_read(v, ("out", i), b)
            if self.cross:
                self.dnorm.dve(v, b, lambda i: self.delta[:, i, :], lambda i: self.delta[:, i, :])
                for i in range(T):
                    v.wait_ge(*self.at(self.scaled, b * T + i + 1))
                    xs = slot(m.x, b * T + i)
                    v.tensor_tensor(xs, xs, self.delta[:, i, :], ALU.add).then_inc(self.rotated, 1)
                v.wait_ge(*self.at(self.rotated, b * T + T))

    def dve_heads(self, v, b):
        m = self.m
        if not self.cross:
            self.dve_turn_max(v, 0, b)
        for u in range(NH):
            g, kb = divmod(u, T)
            if self.cross:
                v.wait_ge(*self.at(self.st_full, b * NH + u + 1))
                v.wait_ge(*self.at(self.pv_done, b * NH + max(u - 1, 0)))
                v.tensor_scalar(self.pt[:, u % 2, :], m.ps[:, 0:4, :].rearrange("p a t -> p (a t)"),
                                slot_col(self.hi, b * T + kb), -50.0 / SOFTMAX_SCALE, ALU.min, ALU.max).then_inc(self.clipped, 1)
            elif g + 1 < C:
                self.dve_rowmax(v, g + 1, self.SHARE[kb], b)
                if kb == T - 1:
                    self.dve_turn_max(v, g + 1, b)
            if kb == (1 if self.cross else 0) and g:
                self.dve_context(v, g - 1, b)
            if u == NH - 2:
                nb = (b + 1) % NB
                self.norm.dve(v, b, lambda i: slot(m.x, nb * T + i), lambda i: m.xn[:, i, :])
        self.dve_context(v, C - 1, b)

    def pool_context(self, g, c, b):
        g.wait_ge(*self.at(self.ch, b * C + c + 1))
        g.tensor_tensor(self.ct[:, 1, c, :], self.ctxn, self.ct[:, 0, c, :], ALU.subtract).then_inc(self.cl, 1)

    def pool(self, g):
        m = self.m
        g.wait_ge(*self.at(self.const, self.nconst))
        g.wait_ge(*self.at(self.consts_done, 2 + self.cross * 5))
        with g.Fori(0, NB) as b:
            g.wait_ge(*self.at(self.norm.xn_ready, b * T))
            for i in range(2 * C):
                if self.rope:
                    self.wait_read(g, ("proj", i), b)
                    g.wait_ge(*self.at(self.rotated, b * 2 * C + max(i - 1, 0)))
                    g.tensor_tensor(self.t1[:, i % 2, :], self.qb[:, i % 2, :], self.cos, ALU.mult).then_inc(self.t1_ready, 1)
                if self.rope:
                    if i:
                        self.pool_low(g, i - 1, b)
                else:
                    self.pool_low(g, i, b)
            if self.rope:
                self.pool_low(g, 2 * C - 1, b)
            for i in range(T):
                xs = slot(m.x, b * T + i)
                g.tensor_tensor(xs, xs, self.beta if self.cross else self.ob, ALU.add).then_inc(self.bias_added, 1)
            for c in range(C - 1):
                self.pool_context(g, c, b)
            self.norm.pool(g, b)
            self.pool_context(g, C - 1, b)
            if self.cross:
                self.dnorm.pool(g, b)
                g.wait_ge(*self.at(self.bias_added, b * T + T))
                for i in range(T):
                    g.wait_ge(*self.at(self.dnorm.xn_ready, b * T + i + 1))
                    g.tensor_tensor(self.delta[:, i, :], self.delta[:, i, :], self.gamma, ALU.mult).then_inc(self.scaled, 1)

    def pool_low(self, g, i, b):
        src = self.qr if self.rope else self.qb
        g.wait_ge(*self.at(self.fh, b * 2 * C + i + 1))
        g.tensor_tensor(self.qf[:, i // C, 1, i % C, :], src[:, i % 2, :], self.qf[:, i // C, 0, i % C, :],
                        ALU.subtract).then_inc(self.fl, 1)


def slot_col(ap, i):
    return ap[:, bass.ds(i, 1)]


def flat(ap):
    return ap.rearrange("p a b -> p (a b)")


class Experts(Phase):

    def __init__(self, m, name):
        super().__init__(m, name)
        take = m.take
        self.mask = take(NE * NB * S, F16).rearrange("p (e t) -> p e t", e=NE)
        self.ids = m.raw[:, 0].rearrange("p c o -> p (c o)").bitcast(I32)
        self.mx = take(2 * NE * C * S, F16).rearrange("p (a e n) -> p a e n", a=2, e=NE)
        self.ma = take(2 * C * NE * S, F16).rearrange("p (a f e t) -> p a f e t", a=2, f=C, e=NE)
        self.gate = take(2 * S).rearrange("p (n t) -> p n t", n=2)
        self.a = take(2 * S).rearrange("p (n t) -> p n t", n=2)
        self.ahl = take(2 * S, F16).rearrange("p (a t) -> p a t", a=2)
        s = self.sem
        self.ids_loaded, self.masks = s("ids_loaded", 16), s("masks_made", 2 * NE - 2)
        self.norm = Norm(m, "norm", NB)
        self.bank_full, self.bank_free = self.sems("bank_full", 4, NB * 2), self.sems("bank_free", 4, NB * 2)
        self.y_full, self.y_free = self.sems("y_full", 4, NB), self.sems("y_free", 4, NB)
        self.xt_high, self.mx_done, self.gated = s("xt_high", NB * T), s("inputs_masked", NB * 2 * NE), s("silu_done", NB * C)
        self.a_split, self.ma_done = s("act_split", NB * 2 * C), s("act_masked", NB * 2 * C)

    def sp(self, sp):
        sp.dma_start(self.ids, self.io["itok"].rearrange("(a n) -> a n", a=1).broadcast_to([P, NB * S])).then_inc(self.ids_loaded, 16)
        sp.wait_ge(*self.at(self.ids_loaded, 16))

    def pe(self, pe):
        m = self.m
        with pe.Fori(0, NB) as b:
            for i in range(T):
                pe.wait_ge(*self.at(self.bank_free[i], b * 2))
                if i == 0:
                    pe.wait_ge(*self.at(self.norm.xn_ready, b * T))
                for c in range(C):
                    last = pe.transpose(m.ps[:, i, c * P:(c + 1) * P], m.xn[:, i, c * P:(c + 1) * P], m.ident[:])
                last.then_inc(self.bank_full[i], 1)
            for f in range(C):
                pe.wait_ge(*self.at(self.bank_free[f], b * 2 + 1))
                for e in range(NE):
                    if f == 0:
                        pe.wait_ge(*self.at(self.mx_done, b * 2 * NE + 2 * (e + 1)))
                    last = three_passes(pe, m.ps[:, f, :], [lambda c: m.w[:, e, 0, c, f * P:(f + 1) * P], lambda c: m.w[:, e, 1, c, f * P:(f + 1) * P]],
                                        [lambda c: self.mx[:, 0, e, c * S:(c + 1) * S], lambda c: self.mx[:, 1, e, c * S:(c + 1) * S]],
                                        range(C), range(C), start=e == 0, stop=e == NE - 1)
                last.then_inc(self.bank_full[f], 1)
            for f in range(C):
                pe.wait_ge(*self.at(self.ma_done, b * 2 * C + 2 * (f + 1)))
                for i in range(T):
                    if f == 0:
                        pe.wait_ge(*self.at(self.y_free[i], b))
                    for e in range(NE):
                        last = three_passes(pe, m.ps[:, 4 + i, :], [lambda f: self.ma[:, 0, f, e, i * P:(i + 1) * P], lambda f: self.ma[:, 1, f, e, i * P:(i + 1) * P]],
                                            [lambda f: m.w[:, e, 0, f, :], lambda f: m.w[:, e, 1, f, :]], [f], [f],
                                            start=f == 0 and e == 0, stop=f == C - 1 and e == NE - 1)
                    if f == C - 1:
                        last.then_inc(self.y_full[i], 1)

    def act(self, act):
        m = self.m
        with act.Fori(0, NB) as b:
            for i in range(T):
                act.wait_ge(*self.at(self.bank_full[i], b * 2 + 1))
                act.activation(m.xt[:, 0, :, i * P:(i + 1) * P], tile3(m.ps[:, i, :]), ACT.Copy).then_inc(self.xt_high, 1)
            for f in range(C):
                act.wait_ge(*self.at(self.bank_full[f], b * 2 + 2))
                act.wait_ge(*self.at(self.ma_done, b * 2 * C + 2 * max(f - 1, 0)))
                act.activation(self.gate[:, f % 2, :], m.ps[:, f, :], ACT.Silu, scale=1.0 / WSCALE).then_inc(self.gated, 1)

    def dve(self, v):
        m = self.m
        v.wait_ge(*self.at(self.ids_loaded, 16))
        k = VOCAB_PER_EXPERT
        v.tensor_scalar(self.mask[:, 0, :], self.ids, float(k), None, ALU.is_lt).then_inc(self.masks, 1)
        for e in range(1, NE):
            v.tensor_scalar(self.mask[:, e, :], self.ids, float(e * k), None, ALU.is_ge).then_inc(self.masks, 1)
        v.wait_ge(*self.at(self.masks, NE))
        for e in range(1, NE - 1):
            v.scalar_tensor_tensor(out=self.mask[:, e, :], in0=self.ids, scalar=float((e + 1) * k), in1=self.mask[:, e, :],
                                   op0=ALU.is_lt, op1=ALU.mult).then_inc(self.masks, 1)
        v.wait_ge(*self.at(self.masks, 2 * NE - 2))
        with v.Fori(0, NB) as b:
            for i in range(T):
                v.wait_ge(*self.at(self.xt_high, b * T + i + 1))
                v.tensor_tensor(m.xt[:, 1, :, i * P:(i + 1) * P], tile3(m.ps[:, i, :]), m.xt[:, 0, :, i * P:(i + 1) * P],
                                ALU.subtract).then_inc(self.bank_free[i], 1)
            for i in range(T):
                v.wait_ge(*self.at(self.bank_free[i], b * 2 + 1))
            for e in range(NE):
                own = self.mask[:, e:e + 1, bass.ds(b * S, S)].broadcast_to([P, C, S])
                for a in range(2):
                    v.tensor_tensor(self.mx[:, a, e, :].rearrange("p (c t) -> p c t", c=C), m.xt[:, a, :, :], own,
                                    ALU.mult).then_inc(self.mx_done, 1)
            for f in range(C):
                v.wait_ge(*self.at(self.gated, b * C + f + 1))
                v.wait_ge(*self.at(self.a_split, b * 2 * C + 2 * f))
                v.scalar_tensor_tensor(out=self.a[:, f % 2, :], in0=m.ps[:, f, :], scalar=1.0 / WSCALE, in1=self.gate[:, f % 2, :],
                                       op0=ALU.mult, op1=ALU.mult).then_inc(self.bank_free[f], 1)
                v.wait_ge(*self.at(self.bank_free[f], b * 2 + 2))
                v.wait_ge(*self.at(self.ma_done, b * 2 * C + 2 * f))
                v.tensor_copy(self.ahl[:, 0, :], self.a[:, f % 2, :]).then_inc(self.a_split, 1)
                v.wait_ge(*self.at(self.a_split, b * 2 * C + 2 * f + 1))
                v.tensor_tensor(self.ahl[:, 1, :], self.a[:, f % 2, :], self.ahl[:, 0, :], ALU.subtract).then_inc(self.a_split, 1)
                for a in range(2):
                    if a:
                        v.wait_ge(*self.at(self.a_split, b * 2 * C + 2 * f + 2))
                    v.tensor_tensor(self.ma[:, a, f], self.ahl[:, a:a + 1, :].broadcast_to([P, NE, S]),
                                    self.mask[:, :, bass.ds(b * S, S)], ALU.mult).then_inc(self.ma_done, 1)
            nb = (b + 1) % NB
            self.norm.dve(v, b, lambda i: slot(m.x, nb * T + i), lambda i: m.xn[:, i, :])
            for i in range(T):
                v.wait_ge(*self.at(self.y_full[i], b + 1))
                xs = slot(m.x, b * T + i)
                v.scalar_tensor_tensor(out=xs, in0=m.ps[:, 4 + i, :], scalar=1.0 / WSCALE, in1=xs,
                                       op0=ALU.mult, op1=ALU.add).then_inc(self.y_free[i], 1)
            for i in range(T):
                v.wait_ge(*self.at(self.y_free[i], b + 1))

    def pool(self, g):
        with g.Fori(0, NB) as b:
            self.norm.pool(g, b)


class BitMlp(Phase):

    def __init__(self, m, name):
        super().__init__(m, name)
        take = m.take
        self.b1, self.b2 = take(INNER), take(D)
        self.h = take(3 * INNER).rearrange("p (n f) -> p n f", n=3)
        self.q2 = take(2 * INNER, F16).rearrange("p (n f) -> p n f", n=2)
        self.q2t = take(2 * INNER, F16).rearrange("p (n f) -> p n f", n=2)
        self.junk = take(INNER)
        self.q1f = take(T * D).rearrange("p (t d) -> p t d", t=T)
        self.q1 = take(T * D, F16).rearrange("p (t d) -> p t d", t=T)
        self.ms, self.am, self.r, self.top, self.inv, self.f, self.alpha = (take(2 * T) for _ in range(7))
        self.negmean, self.absum, self.absum2 = take(2), take(8), take(2)
        self.signs = m.w[:].rearrange("p n a c o -> p (n a c o)")
        s = self.sem
        self.raw_loaded, self.const = self.sems("raw_loaded", 2, 16 * 4), s("const_loaded", 32)
        self.pos_done, self.sign_done, self.abs_done = s("positive", 8), s("signs_made", 8), s("abs_summed", 8)
        self.abs2, self.allred, self.mean_done = s("abs_totalled", 1), s("abs_all", 1), s("means_ready", 1)
        self.norm = Norm(m, "norm", NB)
        self.bank_full, self.bank_free = self.sems("bank_full", 4, NB * 5), self.sems("bank_free", 4, NB * 5)
        self.t_full, self.t_free = self.sems("turn_full", 2, NB * T), self.sems("turn_free", 2, NB * T)
        self.y_full, self.y_free = self.sems("y_full", 2, NB * 2), self.sems("y_free", 2, NB * 2)
        self.per = 3 + 1 + 5 + 2 * T + T * (1 + 1 + 5 + 2)
        self.chain, self.power, self.powered = s("chain", NB * self.per), s("power_wanted", NB * (T + 1)), s("power_ready", NB * (T + 1))
        self.q1_done, self.gelu_done, self.ss_done, self.q2_done = (s(n, NB * T) for n in ("q1_done", "gelu_done", "squares_summed", "q2_done"))
        self.bias_added = s("bias_added", NB * T)

    def sp(self, sp):
        io, m = self.io, self.m
        row = lambda a, n: a.rearrange("(a n) -> a n", a=1).broadcast_to([P, n])
        sp.dma_start(self.b1, row(io["L0_ffn_b1"], INNER)).then_inc(self.const, 16)
        sp.dma_start(self.b2, row(io["L0_ffn_b2"], D)).then_inc(self.const, 16)
        for n in range(8):
            if n >= 2:
                sp.wait_ge(*self.at(self.sign_done, n - 1))
                sp.wait_ge(*self.at(self.abs_done, n - 1))
            src = (io["L0_ffn_w1T"][n * P:(n + 1) * P, :].rearrange("p (c o) -> p c o", c=C) if n < 4 else
                   io["L0_ffn_w2T"][(n - 4) * D:(n - 3) * D, :].rearrange("(c p) o -> p c o", p=P))
            sp.dma_start(m.raw[:, n % 2], src).then_inc(self.raw_loaded[n % 2], 16)
        sp.wait_ge(*self.at(self.const, 32))

    def pe(self, pe):
        m = self.m
        sg = self.signs
        pe.wait_ge(*self.at(self.sign_done, 8))
        with pe.Fori(0, NB) as b:
            for i in range(T):
                pe.wait_ge(*self.at(self.q1_done, b * T + i + 1))
                pe.wait_ge(*self.at(self.bank_free[i], b * 5))
                for c in range(C):
                    last = pe.transpose(m.ps[:, i, 0:256].bitcast(F16)[:, c * P:(c + 1) * P], self.q1[:, i, c * P:(c + 1) * P], m.ident16[:])
                last.then_inc(self.bank_full[i], 1)
            for st in range(T + 2):
                i = st
                if i < T:
                    pe.wait_ge(*self.at(self.bank_free[i], b * 5 + 1))
                    for n in range(4):
                        pe.wait_ge(*self.at(self.bank_free[n], b * 5 + 1 + i))
                        for c in range(C):
                            last = pe.matmul(m.ps[:, n, :], m.xt[:, 0, c, i * P:(i + 1) * P],
                                             sg[:, c * INNER + n * 512:c * INNER + (n + 1) * 512], start=c == 0, stop=c == C - 1)
                        last.then_inc(self.bank_full[n], 1)
                i = st - 2
                if i >= 0:
                    pe.wait_ge(*self.at(self.q2_done, b * T + i + 1))
                    for k in range(2):
                        pe.wait_ge(*self.at(self.t_free[k], b * T + i))
                        for c in range(8):
                            last = pe.transpose(m.ps[:, 4 + k, :].bitcast(F16)[:, c * P:(c + 1) * P],
                                                self.q2[:, i % 2, (8 * k + c) * P:(8 * k + c + 1) * P], m.ident16[:])
                        last.then_inc(self.t_full[k], 1)
                    pe.wait_ge(*self.at(self.y_free[i % 2], b * 2 + i // 2))
                    for c in range(NI):
                        if c % 8 == 0:
                            pe.wait_ge(*self.at(self.t_free[c // 8], b * T + i + 1))
                        last = pe.matmul(m.ps[:, 6 + i % 2, :], self.q2t[:, i % 2, c * P:(c + 1) * P],
                                         sg[:, C * INNER + c * D:C * INNER + (c + 1) * D], start=c == 0, stop=c == NI - 1)
                    last.then_inc(self.y_full[i % 2], 1)

    def act(self, act):
        m = self.m
        for n in range(8):
            act.wait_ge(*self.at(self.raw_loaded[n % 2], 16 * (n // 2 + 1)))
            if n:
                act.wait_ge(*self.at(self.abs_done, n))
            act.activation(self.junk, flat(m.raw[:, n % 2]), ACT.Abs, accum_out=self.absum[:, n:n + 1]).then_inc(self.abs_done, 1)
        with act.Fori(0, NB) as b:
            for i in range(T):
                act.wait_ge(*self.at(self.bank_full[i], b * 5 + 1))
                act.activation(m.xt[:, 0, :, i * P:(i + 1) * P], tile3(m.ps[:, i, 0:256].bitcast(F16)), ACT.Copy).then_inc(self.bank_free[i], 1)
            for st in range(T + 2):
                i = st
                if i < T:
                    act.wait_ge(*self.at(self.bank_free[3], b * 5 + 2 + i))
                    act.activation(self.h[:, i % 3, :], self.h[:, i % 3, :], ACT.Gelu).then_inc(self.gelu_done, 1)
                    act.wait_ge(*self.at(self.gelu_done, b * T + i + 1))
                    act.wait_ge(*self.at(self.ss_done, b * T + i))
                    if i == 0:
                        act.wait_ge(*self.at(self.abs_done, 8))
                    act.activation(self.junk, self.h[:, i % 3, :], ACT.Square,
                                   accum_out=self.ms[:, T + i:T + i + 1]).then_inc(self.ss_done, 1)
                i = st - 2
                if i >= 0:
                    for k in range(2):
                        act.wait_ge(*self.at(self.t_full[k], b * T + i + 1))
                        act.activation(self.q2t[:, i % 2, k * 1024:(k + 1) * 1024], m.ps[:, 4 + k, :].bitcast(F16), ACT.Copy).then_inc(self.t_free[k], 1)

    def row_factors(self, v, ch, cols, dim, which, powers):
        ch.wait(v)
        v.wait_ge(*self.at(self.powered, powers))
        c = cols
        d = dim ** -0.5
        ch.put(v.scalar_tensor_tensor(out=self.top[:, c], in0=self.r[:, c], scalar=d, in1=self.am[:, c], op0=ALU.mult, op1=ALU.mult))
        ch.wait(v)
        ch.put(v.tensor_scalar(self.top[:, c], self.top[:, c], 1e-5, None, ALU.max))
        ch.wait(v)
        ch.put(v.reciprocal(self.inv[:, c], self.top[:, c]))
        ch.put(v.tensor_scalar(self.alpha[:, c], self.top[:, c], self.negmean[:, which:which + 1], 1.0 / 127.0, ALU.mult, ALU.mult))
        ch.wait(v)
        ch.put(v.scalar_tensor_tensor(out=self.f[:, c], in0=self.inv[:, c], scalar=127.0 * d, in1=self.r[:, c], op0=ALU.mult, op1=ALU.mult))
        ch.wait(v)

    def quantise(self, v, ch, src, tmp, dst, factor, done):
        ch.put(v.tensor_scalar(tmp, src, factor, 127.0, ALU.mult, ALU.min))
        ch.wait(v)
        ch.put(v.tensor_scalar(tmp, tmp, -128.0, MAGIC, ALU.max, ALU.add))
        ch.wait(v)
        v.tensor_scalar(dst, tmp, -MAGIC, None, ALU.add).then_inc(done, 1)

    def dve(self, v):
        m = self.m
        for n in range(8):
            v.wait_ge(*self.at(self.raw_loaded[n % 2], 16 * (n // 2 + 1)))
            if n:
                v.wait_ge(*self.at(self.sign_done, n))
            v.tensor_scalar(self.h[:, 0, :], flat(m.raw[:, n % 2]), 0.0, None, ALU.is_gt).then_inc(self.pos_done, 1)
            v.wait_ge(*self.at(self.pos_done, n + 1))
            v.scalar_tensor_tensor(out=self.signs[:, n * INNER:(n + 1) * INNER], in0=flat(m.raw[:, n % 2]), scalar=0.0,
                                   in1=self.h[:, 0, :], op0=ALU.is_lt, op1=ALU.subtract).then_inc(self.sign_done, 1)
        v.wait_ge(*self.at(self.abs_done, 8))
        v.wait_ge(*self.at(self.sign_done, 8))
        v.tensor_reduce(self.absum2, self.absum.rearrange("p (a n) -> p a n", a=2), AX.X, ALU.add).then_inc(self.abs2, 1)
        v.wait_ge(*self.at(self.allred, 1))
        v.tensor_scalar(self.negmean, self.negmean, -1.0 / (INNER * D), None, ALU.mult).then_inc(self.mean_done, 1)
        v.wait_ge(*self.at(self.mean_done, 1))
        v.wait_ge(*self.at(self.const, 32))
        with v.Fori(0, NB) as b:
            ch = Chain(self, self.chain, self.per, b)
            c4 = slice(0, T)
            ch.wait(v)
            ch.put(v.tensor_reduce(self.am[:, c4], m.xn[:], AX.X, ALU.max, apply_absolute_value=True))
            var = m.mv[:, :, 1:2].rearrange("p t a -> p (t a)")
            ch.put(v.tensor_tensor(self.ms[:, c4], var, m.rstd[:], ALU.mult))
            ch.wait(v)
            ch.put(v.tensor_tensor(self.ms[:, c4], self.ms[:, c4], m.rstd[:], ALU.mult))
            ch.wait(v)
            ch.put(v.tensor_scalar(self.r[:, c4], self.ms[:, c4], 1e-6, None, ALU.add))
            ch.wait(v)
            v.tensor_copy(self.f[:, c4], self.r[:, c4]).then_inc(self.power, 1)
            v.wait_ge(*self.at(self.power, b * (T + 1) + 1))
            self.row_factors(v, ch, c4, D, 0, b * (T + 1) + 1)
            for i in range(T):
                self.quantise(v, ch, m.xn[:, i, :], self.q1f[:, i, :], self.q1[:, i, :], self.f[:, i:i + 1], self.q1_done)
            for st in range(T + 2):
                i = st
                if i < T:
                    if i == 3:
                        v.wait_ge(*self.at(self.q2_done, b * T + 1))
                    for n in range(4):
                        v.wait_ge(*self.at(self.bank_full[n], b * 5 + 2 + i))
                        v.scalar_tensor_tensor(out=self.h[:, i % 3, n * 512:(n + 1) * 512], in0=m.ps[:, n, :], scalar=self.alpha[:, i:i + 1],
                                               in1=self.b1[:, n * 512:(n + 1) * 512], op0=ALU.mult, op1=ALU.add).then_inc(self.bank_free[n], 1)
                i = st - 1
                if 0 <= i < T:
                    col = slice(T + i, T + i + 1)
                    v.wait_ge(*self.at(self.gelu_done, b * T + i + 1))
                    ch.put(v.tensor_reduce(self.am[:, col], self.h[:, i % 3, :], AX.X, ALU.max, apply_absolute_value=True))
                    v.wait_ge(*self.at(self.ss_done, b * T + i + 1))
                    ch.put(v.tensor_scalar(self.r[:, col], self.ms[:, col], 1.0 / INNER, 1e-6, ALU.mult, ALU.add))
                    ch.wait(v)
                    v.tensor_copy(self.f[:, col], self.r[:, col]).then_inc(self.power, 1)
                    v.wait_ge(*self.at(self.power, b * (T + 1) + i + 2))
                    self.row_factors(v, ch, col, INNER, 1, b * (T + 1) + i + 2)
                    self.quantise(v, ch, self.h[:, i % 3, :], self.h[:, i % 3, :], self.q2[:, i % 2, :], self.f[:, T + i:T + i + 1], self.q2_done)
                i = st - 2
                if i >= 0:
                    v.wait_ge(*self.at(self.y_full[i % 2], b * 2 + i // 2 + 1))
                    v.wait_ge(*self.at(self.bias_added, b * T + i + 1))
                    xs = slot(m.x, b * T + i)
                    v.scalar_tensor_tensor(out=xs, in0=m.ps[:, 6 + i % 2, :], scalar=self.alpha[:, T + i:T + i + 1], in1=xs,
                                           op0=ALU.mult, op1=ALU.add).then_inc(self.y_free[i % 2], 1)
                if st == T - 1:
                    v.wait_ge(*self.at(self.q1_done, b * T + T))
                    nb = (b + 1) % NB
                    self.norm.dve(v, b, lambda i: slot(m.x, nb * T + i), lambda i: m.xn[:, i, :])
            for k in range(2):
                v.wait_ge(*self.at(self.y_free[k], b * 2 + 2))
            v.wait_ge(*self.at(self.norm.xn_ready, b * T + T))
            v.wait_ge(*self.at(self.q2_done, b * T + T))
            ch.close()

    def pool(self, g):
        m = self.m
        g.wait_ge(*self.at(self.abs2, 1))
        g.partition_all_reduce(self.negmean, self.absum2, P, RADD).then_inc(self.allred, 1)
        g.wait_ge(*self.at(self.const, 32))

        def inverse_root(k, b, cols):
            g.wait_ge(*self.at(self.power, b * (T + 1) + k + 1))
            g.tensor_tensor(self.r[:, cols], self.f[:, cols], m.mhalf[:, 0:cols.stop - cols.start], ALU.pow).then_inc(self.powered, 1)

        with g.Fori(0, NB) as b:
            g.wait_ge(*self.at(self.norm.xn_ready, b * T))
            inverse_root(0, b, slice(0, T))
            for i in range(T):
                xs = slot(m.x, b * T + i)
                g.tensor_tensor(xs, xs, self.b2, ALU.add).then_inc(self.bias_added, 1)
            for i in range(3):
                inverse_root(1 + i, b, slice(T + i, T + i + 1))
                if i == 2:
                    self.norm.pool(g, b)
            inverse_root(T, b, slice(2 * T - 1, 2 * T))


class Fp8Linear(Phase):

    def __init__(self, m, name):
        super().__init__(m, name)
        take = m.take
        self.y = take(NB * T * D).rearrange("p (t d) -> p t d", t=NB * T)
        self.v = take(2 * T * D).rearrange("p (n d) -> p n d", n=2)
        self.p2 = take(2 * T * D).rearrange("p (n d) -> p n d", n=2)
        self.q = take(2 * T * D, F16).rearrange("p (n d) -> p n d", n=2)
        self.bias = take(D)
        self.am, self.top, self.ws, self.ws64 = take(NB), take(4), take(1), take(1)
        s = self.sem
        self.const, self.wdone, self.normed, self.peak = s("const_loaded", 48), s("weight_split", 3), Norm(m, "norm", NB), s("peaks", NB + 1)
        self.allred, self.scale, self.chain, self.q_done = s("peak_all", 1), s("scale_ready", 3), s("chain", 4 * NB), s("q_done", NB)
        self.bank_full, self.bank_free = self.sems("bank_full", 4, NB), self.sems("bank_free", 4, NB)
        self.y_full, self.y_free = self.sems("y_full", 4, NB), self.sems("y_free", 4, NB)
        self.bias_added, self.stored = s("bias_added", NB * T), s("stored", 16 * NB * T)

    def sp(self, sp):
        io, m = self.io, self.m
        row = lambda a, n: a.rearrange("(a n) -> a n", a=1).broadcast_to([P, n])
        sp.dma_start(m.raw[:, 0], io["L1_ffn_weightT"].rearrange("(c p) o -> p c o", p=P)).then_inc(self.const, 16)
        sp.dma_start(self.bias, row(io["L1_ffn_bias"], D)).then_inc(self.const, 16)
        sp.dma_start(self.ws, row(io["L1_ffn_weight_scale"], 1)).then_inc(self.const, 16)
        sp.wait_ge(*self.at(self.const, 48))
        with sp.Fori(0, NB) as b:
            for i in range(T):
                sp.wait_ge(*self.at(self.y_free[i], b + 1))
                sp.dma_start(io["out"][bass.ds(b, 1), i * P:(i + 1) * P, :].rearrange("b p d -> p (b d)"),
                             slot(m.x, b * T + i)).then_inc(self.stored, 16)
        sp.wait_ge(*self.at(self.stored, 16 * NB * T))

    def pe(self, pe):
        m = self.m
        pe.wait_ge(*self.at(self.wdone, 3))
        with pe.Fori(0, NB) as b:
            pe.wait_ge(*self.at(self.q_done, b + 1))
            for i in range(T):
                pe.wait_ge(*self.at(self.bank_free[i], b))
                for c in range(C):
                    last = pe.transpose(m.ps[:, i, 0:256].bitcast(F16)[:, c * P:(c + 1) * P],
                                        self.q[:, 0, i * D + c * P:i * D + (c + 1) * P], m.ident16[:])
                last.then_inc(self.bank_full[i], 1)
            for i in range(T):
                pe.wait_ge(*self.at(self.bank_free[i], b + 1))
                pe.wait_ge(*self.at(self.y_free[i], b))
                for c in range(C):
                    for a in range(2):
                        last = pe.matmul(m.ps[:, 4 + i, :], m.xt[:, 0, c, i * P:(i + 1) * P], m.w[:, 0, a, c, :],
                                         start=c == 0 and a == 0, stop=c == C - 1 and a == 1)
                last.then_inc(self.y_full[i], 1)

    def act(self, act):
        m = self.m
        with act.Fori(0, NB) as b:
            for i in range(T):
                act.wait_ge(*self.at(self.bank_full[i], b + 1))
                act.activation(m.xt[:, 0, :, i * P:(i + 1) * P], tile3(m.ps[:, i, 0:256].bitcast(F16)), ACT.Copy).then_inc(self.bank_free[i], 1)

    def dve(self, v):
        m = self.m
        v.wait_ge(*self.at(self.const, 48))
        v.tensor_scalar(self.ws64, self.ws, WSCALE, None, ALU.mult).then_inc(self.scale, 1)
        v.wait_ge(*self.at(self.scale, 1))
        v.tensor_scalar(flat(m.raw[:, 1]), flat(m.raw[:, 0]), self.ws64, None, ALU.mult).then_inc(self.wdone, 1)
        v.wait_ge(*self.at(self.wdone, 1))
        v.tensor_copy(flat(m.w[:, 0, 0]), flat(m.raw[:, 1])).then_inc(self.wdone, 1)
        v.wait_ge(*self.at(self.wdone, 2))
        v.tensor_tensor(flat(m.w[:, 0, 1]), flat(m.raw[:, 1]), flat(m.w[:, 0, 0]), ALU.subtract).then_inc(self.wdone, 1)
        with v.Fori(0, NB) as b:
            self.normed.dve(v, b, lambda i: slot(m.x, b * T + i), lambda i: slot(self.y, b * T + i))
            v.wait_ge(*self.at(self.normed.xn_ready, b * T + T))
            v.tensor_reduce(slot_col(self.am, b), self.y[:, bass.ds(b * T, T), :].rearrange("p t d -> p (t d)"), AX.X, ALU.max,
                            apply_absolute_value=True).then_inc(self.peak, 1)
        v.wait_ge(*self.at(self.peak, NB))
        v.tensor_reduce(self.top[:, 0:1], self.am, AX.X, ALU.max).then_inc(self.peak, 1)
        v.wait_ge(*self.at(self.allred, 1))
        v.tensor_scalar(self.top[:, 2:3], self.top[:, 1:2], 1.0 / 448.0, 1e-7, ALU.mult, ALU.max).then_inc(self.scale, 1)
        v.wait_ge(*self.at(self.scale, 2))
        v.reciprocal(self.top[:, 3:4], self.top[:, 2:3]).then_inc(self.scale, 1)
        v.wait_ge(*self.at(self.scale, 3))
        val, pw = self.v[:, 0, :], self.p2[:, 0, :]
        with v.Fori(0, NB) as b:
            ch = Chain(self, self.chain, 4, b)
            v.wait_ge(*self.at(self.q_done, b))
            ch.put(v.tensor_scalar(val, self.y[:, bass.ds(b * T, T), :].rearrange("p t d -> p (t d)"), self.top[:, 3:4], None, ALU.mult))
            ch.wait(v)
            ch.put(v.tensor_scalar(pw.bitcast(I32), val.bitcast(I32), 0x7F800000, None, ALU.bitwise_and))
            ch.wait(v)
            ch.put(v.tensor_scalar(pw, pw, 2.0 ** -6, 1.5 * 2.0 ** 20, ALU.max, ALU.mult))
            ch.wait(v)
            ch.put(v.tensor_tensor(val, val, pw, ALU.add))
            ch.wait(v)
            for i in range(T):
                v.wait_ge(*self.at(self.bank_full[i], b))
            v.tensor_tensor(self.q[:, 0, :], val, pw, ALU.subtract).then_inc(self.q_done, 1)
            ch.close()
            for i in range(T):
                v.wait_ge(*self.at(self.y_full[i], b + 1))
                v.wait_ge(*self.at(self.bias_added, b * T + i + 1))
                xs = slot(m.x, b * T + i)
                v.scalar_tensor_tensor(out=xs, in0=m.ps[:, 4 + i, :], scalar=1.0 / WSCALE, in1=xs,
                                       op0=ALU.mult, op1=ALU.add).then_inc(self.y_free[i], 1)

    def pool(self, g):
        m = self.m
        g.wait_ge(*self.at(self.const, 48))
        with g.Fori(0, NB) as b:
            self.normed.pool(g, b)
        g.wait_ge(*self.at(self.peak, NB + 1))
        g.partition_all_reduce(self.top[:, 1:2], self.top[:, 0:1], P, RMAX).then_inc(self.allred, 1)
        with g.Fori(0, NB) as b:
            for i in range(T):
                xs = slot(m.x, b * T + i)
                g.tensor_tensor(xs, xs, self.bias, ALU.add).then_inc(self.bias_added, 1)


class Finish(Phase):

    def __init__(self, m):
        super().__init__(m, "finish")
        self.stored = self.sem("stored", 16)

    def sp(self, sp):
        sp.dma_start(self.io["out"].rearrange("b (t p) d -> p (b t) d", p=P), self.m.x[:]).then_inc(self.stored, 16)
        sp.wait_ge(*self.at(self.stored, 16))


def program(nc, io, stages):
    with ExitStack() as ctx:
        m = Machine(nc, ctx, io)
        phases = stages(m, io)
        block = ctx.enter_context(nc.Block())

        @block.tensor
        def _(pe):
            m.barrier(pe, 0)
            for k, ph in enumerate(phases):
                ph.pe(pe)
                m.barrier(pe, k + 1)

        @block.scalar
        def _(act):
            m.barrier(act, 0)
            for k, ph in enumerate(phases):
                ph.act(act)
                m.barrier(act, k + 1)

        @block.vector
        def _(v):
            m.barrier(v, 0)
            for k, ph in enumerate(phases):
                ph.dve(v)
                m.barrier(v, k + 1)

        @block.gpsimd
        def _(g):
            m.barrier(g, 0)
            for k, ph in enumerate(phases):
                ph.pool(g)
                m.barrier(g, k + 1)

        @block.sync
        def _(sp):
            for sem in m.sems.values():
                sp.sem_inc(sem, 1)
            m.barrier(sp, 0)
            for k, ph in enumerate(phases):
                ph.sp(sp)
                m.barrier(sp, k + 1)


def decoder(nc, io):
    def stages(m, t):
        qkv = t["L1_attn_w_qkvT"]
        return [Start(m),
                Weights(m, "w_attn0", [t["L0_attn_k_wT"], t["L0_attn_q_wT"], t["L0_attn_v_wT"], t["L0_attn_out_wT"]]),
                Attention(m, "attn0", t["L0_attn_q_b_cols"], t["L0_attn_k_b_cols"], t["L0_attn_v_b"], t["L0_attn_out_b"], rope=True),
                Weights(m, "w_experts", [t["ctxT"][e * D:(e + 1) * D, :] for e in range(NE)]),
                Experts(m, "experts"),
                BitMlp(m, "bit"),
                Weights(m, "w_attn1", [qkv[:, D:2 * D], qkv[:, 0:D], qkv[:, 2 * D:3 * D], t["L1_attn_w_outT"]]),
                Attention(m, "attn1", t["L1_attn_q_b_cols"], t["L1_attn_k_b_cols"], t["L1_attn_v_b"], t["L1_attn_b_out"]),
                Weights(m, "w_xattn", [t["L1_xattn_WkT"], t["L1_xattn_WqT"], t["L1_xattn_WvT"], t["L1_xattn_WoT"]]),
                Attention(m, "xattn", t["L1_xattn_bq_cols"], t["L1_xattn_bk_cols"], t["L1_xattn_bv"], t["L1_xattn_bo"], cross=True),
                Fp8Linear(m, "fp8")]
    program(nc, io, stages)


def layout(inputs):
    import numpy as np
    a = {k: np.ascontiguousarray(v) for k, v in inputs.items()}
    for k in ("L0_attn_q_w", "L0_attn_k_w", "L0_attn_v_w", "L0_attn_out_w", "L0_ffn_w1", "L0_ffn_w2", "L1_attn_w_qkv",
              "L1_attn_w_out", "L1_xattn_Wq", "L1_xattn_Wk", "L1_xattn_Wv", "L1_xattn_Wo", "L1_ffn_weight"):
        a[k + "T"] = np.ascontiguousarray(a.pop(k).T)
    a["ctxT"] = np.ascontiguousarray(a.pop("ctx_2048").transpose(0, 2, 1)).reshape(NB * D, S)
    for k in ("L1_xattn_residual_scale", "L1_ffn_weight_scale"):
        a[k] = a[k].reshape(1)
    cols = lambda v: np.ascontiguousarray(v.reshape(-1, P).T)
    b1 = a["L1_attn_b_qkv"]
    a["L1_attn_q_b_cols"], a["L1_attn_k_b_cols"], a["L1_attn_v_b"] = cols(b1[0:D]), cols(b1[D:2 * D]), np.ascontiguousarray(b1[2 * D:])
    for k in ("L0_attn_q_b", "L0_attn_k_b", "L1_xattn_bq", "L1_xattn_bk"):
        a[k + "_cols"] = cols(a.pop(k))
    a["mask_cols"] = cols(a.pop("mask_BxS2_ik0"))
    a["itok"] = a.pop("itok_BxS_13_99985").reshape(-1)
    a["ident"] = np.eye(P, dtype=np.float32)
    half = HD // 2
    inv = (np.float32(1.0) / np.float32(10000.0) ** (np.arange(0, HD, 2, dtype=np.float32) / np.float32(HD))).astype(np.float32)
    angle = (np.arange(S, dtype=np.float32)[None, :] * inv[:, None]).astype(np.float32)
    angle = np.tile(angle, (2 * HG, 1))
    a["rope_cos"], a["rope_sin"] = np.cos(angle).astype(np.float32), np.sin(angle).astype(np.float32)
    rot = np.zeros((P, P), np.float32)
    for o in range(P):
        first = o % HD < half
        rot[o + half if first else o - half, o] = -1.0 if first else 1.0
    a["rope_rot"] = rot
    return a


def kernel(**inputs):
    import concourse.bacc as bacc
    from concourse import mybir as _mybir
    from concourse.bass_utils import run_bass_kernel_spmd as run

    nc = bacc.Bacc("TRN2", target_bir_lowering=False, num_devices=1)
    arrays = layout(inputs)
    io = {k: nc.dram_tensor(f"in_{k}", v.shape, _mybir.dt.from_np(v.dtype), kind="ExternalInput").ap() for k, v in arrays.items()}
    io["out"] = nc.dram_tensor("out", (NB, S, D), F32, kind="ExternalOutput").ap()
    decoder(nc, io)
    r = run(nc, [{f"in_{k}": v for k, v in arrays.items()}], core_ids=[0])
    return r.results[0]["out"]
```

```python
from contextlib import ExitStack

import concourse.bass as bass
from concourse import mybir

P = 128
NB = 4
S = 512
D = 512
NH = 16
HD = D // NH
T = S // P
C = D // P
HG = P // HD
NE = 4
INNER = 2048
NI = INNER // P
WSCALE = 64.0
MSCALE = 64.0
ARENA = 27 * 1024 + 640
EPS = 1e-5
MAGIC = 1.5 * 2.0 ** 23
VOCAB_PER_EXPERT = 25000 // NE

ALU = mybir.AluOpType
ACT = mybir.ActivationFunctionType
AX = mybir.AxisListType
F32 = mybir.dt.float32
F16 = mybir.dt.float16
I32 = mybir.dt.int32
RMAX = bass.bass_isa.ReduceOp.max
RADD = bass.bass_isa.ReduceOp.add
SOFTMAX_SCALE = HD ** -0.5


def tile3(ap):
    return ap.rearrange("p (c t) -> p c t", t=P)


class Chain:

    def __init__(self, phase, sem, per, b):
        self.at, self.sem, self.per, self.base, self.n = phase.at, sem, per, b * per, 0

    def put(self, ins):
        ins.then_inc(self.sem, 1)
        self.n += 1

    def wait(self, eng):
        eng.wait_ge(*self.at(self.sem, self.base + self.n))

    def close(self):
        assert self.n == self.per, (self.sem, self.n, self.per)


class Machine:

    def __init__(self, nc, ctx, io):
        self.nc, self.ctx, self.io = nc, ctx, io
        sb = lambda name, shape, dt: ctx.enter_context(nc.sbuf_tensor(name, shape, dt))
        self.x = sb("x", [P, NB * T, D], F32)
        self.xn = sb("xn", [P, T, D], F32)
        self.xt = sb("xt", [P, 2, C, S], F16)
        self.w = sb("w", [P, 4, 2, C, D], F16)
        self.raw = sb("raw", [P, 2, C, D], F32)
        self.arena = sb("arena", [P, ARENA], F32)
        self.ident = sb("ident", [P, P], F32)
        self.ident16 = sb("ident16", [P, P], F16)
        self.mhalf = sb("mhalf", [P, T], F32)
        self.carrier = sb("carrier", [P, 1], F32)
        self.eps = sb("eps", [P, T], F32)
        self.stats = sb("stats", [P, T, 6], F32)
        self.mv = sb("mv", [P, T, 2], F32)
        self.rstd = sb("rstd", [P, T], F32)
        self.ps = ctx.enter_context(nc.psum_tensor("ps", [P, 8, 512], F32))
        self.phase_end = ctx.enter_context(nc.semaphore("phase_end"))
        self.sems, self.count = {}, {}
        self.used = 0

    def sem(self, name, total):
        if name not in self.sems:
            self.sems[name] = self.ctx.enter_context(self.nc.semaphore(name))
            self.count[name] = 1
        self.taken.append(name)
        assert self.taken.count(name) == 1, name
        self.start[name] = self.count[name]
        self.count[name] += total
        return self.sems[name]

    def next_phase(self):
        self.used, self.taken, self.start = 0, [], {}
        return self.start

    def take(self, n, dt=F32):
        words = (n + 1) // 2 if dt == F16 else n
        a = self.arena[:, self.used:self.used + words]
        self.used += words
        assert self.used <= ARENA, self.used
        return a if dt == F32 else a.bitcast(dt)

    def barrier(self, eng, k):
        eng.drain().then_inc(self.phase_end, 1)
        eng.wait_ge(self.phase_end, 5 * (k + 1))


def counter(start):
    return lambda sem, n: (sem, start[sem.name] + n)


def slot(ap, i):
    return ap[:, bass.ds(i, 1), :].rearrange("p a n -> p (a n)")


class Norm:

    def __init__(self, m, name, calls):
        self.m = m
        self.sums = m.sem(f"{name}_bn_sums", calls * T)
        self.moments = m.sem(f"{name}_moments", calls * T)
        self.rstd_ready = m.sem(f"{name}_rstd_ready", calls)
        self.eps_added = m.sem(f"{name}_eps_added", calls)
        self.xn_ready = m.sem(f"{name}_xn_ready", calls * T)
        self.at = counter(m.start)

    def dve_moments(self, v, b, src):
        m = self.m
        for i in range(T):
            v.bn_stats(m.stats[:, i, :], src(i)).then_inc(self.sums, 1)
        v.wait_ge(*self.at(self.sums, b * T + T))
        v.memset(m.carrier[:], 0.0)
        for i in range(T):
            v.bn_aggr(m.mv[:, i, :], m.stats[:, i, :]).then_inc(self.moments, 1)

    def dve_apply(self, v, b, src, dst):
        m = self.m
        v.wait_ge(*self.at(self.moments, b * T + T))
        v.wait_ge(*self.at(self.rstd_ready, b + 1))
        for i in range(T):
            v.tensor_scalar(dst(i), src(i), m.mv[:, i, 0:1], m.rstd[:, i:i + 1],
                            ALU.subtract, ALU.mult).then_inc(self.xn_ready, 1)

    def dve(self, v, b, src, dst):
        self.dve_moments(v, b, src)
        self.dve_apply(v, b, src, dst)

    def pool(self, g, b):
        m = self.m
        g.wait_ge(*self.at(self.moments, b * T + T))
        g.tensor_tensor(m.rstd[:], m.mv[:, :, 1:2].rearrange("p t a -> p (t a)"), m.eps[:],
                        ALU.add).then_inc(self.eps_added, 1)
        g.wait_ge(*self.at(self.eps_added, b + 1))
        g.tensor_tensor(m.rstd[:], m.rstd[:], m.mhalf[:], ALU.pow).then_inc(self.rstd_ready, 1)


class Phase:
    def __init__(self, m, name):
        self.m, self.name = m, name
        self.at = counter(m.next_phase())
        self.io = m.io

    def sem(self, name, total):
        return self.m.sem(name, total)

    def sems(self, name, n, total):
        return [self.sem(f"{name}{i}", total) for i in range(n)]

    def pe(self, pe): pass
    def act(self, act): pass
    def dve(self, v): pass
    def pool(self, g): pass
    def sp(self, sp): pass


class Start(Phase):

    def __init__(self, m):
        super().__init__(m, "start")
        self.loaded = [self.sem("x_loaded", 16), self.sem("const_loaded", 16)]
        self.norm = Norm(m, "norm", 1)
        self.consts = self.sem("consts_done", 2)

    def sp(self, sp):
        m = self.m
        sp.dma_start(m.x[:], self.io["x"].rearrange("b (t p) d -> p (b t) d", p=P)).then_inc(self.loaded[0], 16)
        sp.dma_start(m.ident[:], self.io["ident"]).then_inc(self.loaded[1], 16)
        sp.wait_ge(*self.at(self.loaded[0], 16))
        sp.wait_ge(*self.at(self.loaded[1], 16))

    def pool(self, g):
        g.memset(self.m.mhalf[:], -0.5).then_inc(self.consts, 1)
        g.memset(self.m.eps[:], EPS).then_inc(self.consts, 1)
        g.wait_ge(*self.at(self.consts, 2))
        self.norm.pool(g, 0)

    def dve(self, v):
        m = self.m
        v.wait_ge(*self.at(self.loaded[1], 16))
        v.tensor_copy(m.ident16[:], m.ident[:])
        v.wait_ge(*self.at(self.loaded[0], 16))
        self.norm.dve(v, 0, lambda i: m.x[:, i, :], lambda i: m.xn[:, i, :])


class Weights(Phase):

    def __init__(self, m, name, mats):
        super().__init__(m, name)
        self.mats = mats
        n = len(mats)
        self.raw_loaded = [self.sem(f"raw_loaded{k}", 16 * ((n - k + 1) // 2)) for k in range(2)]
        self.high_done, self.low_done = self.sem("high_done", n), self.sem("low_done", n)

    def sp(self, sp):
        for n, a in enumerate(self.mats):
            if n >= 2:
                sp.wait_ge(*self.at(self.low_done, n - 1))
            sp.dma_start(self.m.raw[:, n % 2], a.rearrange("(c p) o -> p c o", p=P)).then_inc(self.raw_loaded[n % 2], 16)
        for k in range(min(2, len(self.mats))):
            sp.wait_ge(*self.at(self.raw_loaded[k], 16 * ((len(self.mats) - k + 1) // 2)))

    def act(self, act):
        m = self.m
        for n in range(len(self.mats)):
            act.wait_ge(*self.at(self.raw_loaded[n % 2], 16 * (n // 2 + 1)))
            act.activation(m.w[:, n, 0], m.raw[:, n % 2], ACT.Copy, scale=WSCALE).then_inc(self.high_done, 1)

    def dve(self, v):
        m = self.m
        for n in range(len(self.mats)):
            v.wait_ge(*self.at(self.high_done, n + 1))
            v.scalar_tensor_tensor(out=m.w[:, n, 1].rearrange("p c o -> p (c o)"),
                                   in0=m.raw[:, n % 2].rearrange("p c o -> p (c o)"), scalar=WSCALE,
                                   in1=m.w[:, n, 0].rearrange("p c o -> p (c o)"),
                                   op0=ALU.mult, op1=ALU.subtract).then_inc(self.low_done, 1)


def three_passes(pe, out, left, right, cl, cr, start=True, stop=True):
    n = len(cl)
    for k in range(n):
        for a, (l, r) in enumerate(((0, 0), (0, 1), (1, 0))):
            last = pe.matmul(out, left[l](cl[k]), right[r](cr[k]), start=start and k == 0 and a == 0,
                             stop=stop and k == n - 1 and a == 2)
    return last


class Attention(Phase):

    NPROJ = 2 * C
    HALVES = 2

    def __init__(self, m, name, q_bias, k_bias, v_bias, out_bias, rope=False, cross=False):
        super().__init__(m, name)
        self.rope, self.cross = rope, cross
        self.biases = (k_bias, q_bias)
        self.v_bias, self.out_bias = v_bias, out_bias
        take = m.take
        self.qst = take(NH * S, F16).rearrange("p (h t) -> p h t", h=NH)
        self.kst = take(NH * S, F16).rearrange("p (h t) -> p h t", h=NH)
        self.qf = take(4 * C * S, F16).rearrange("p (w a c t) -> p w a c t", w=2, a=2, c=C)
        self.v = take(T * D).rearrange("p (t d) -> p t d", t=T)
        self.pt = take(2 * HG * S).rearrange("p (n t) -> p n t", n=2)
        self.ct = take(2 * C * S, F16).rearrange("p (a c t) -> p a c t", a=2, c=C)
        self.qb = take(2 * S).rearrange("p (n t) -> p n t", n=2)
        if rope:
            self.t1 = take(2 * S).rearrange("p (n t) -> p n t", n=2)
            self.t2 = take(S)
            self.qr = take(2 * S).rearrange("p (n t) -> p n t", n=2)
            self.cos, self.sin, self.rot = take(S), take(S), take(P)
        self.ctxn, self.sums = take(S), take(S)
        self.vb, self.ob = take(D), take(D)
        self.pb = take(2 * C)
        self.mx = take(HG * T)
        self.mt = take(P, F16)
        self.ones = take(HD)
        s = self.sem
        if cross:
            self.cth = m.raw[:, 1].rearrange("p c o -> p (c o)").bitcast(F16).rearrange("p (a c t) -> p a c t", a=2, c=C)
            self.delta = take(T * D).rearrange("p (t d) -> p t d", t=T)
            self.gamma, self.beta = take(D), take(D)
            self.rs, self.rs64 = take(1), take(1)
            self.mask, self.hi = take(NB * T, I32), take(NB * T)
            self.raw_loaded, self.audio_high, self.audio_low = s("raw_loaded0", 16 * (NB + 1)), s("audio_high", NB + 1), s("audio_low", NB + 1)
            self.clipped = self.sems("clipped", 2, NB * NH)
            self.dnorm = Norm(m, "delta", NB)
        seq = []
        for n in range(self.NPROJ):
            seq.append(("proj", n))
            if rope and n:
                seq.append(("rot", n - 1))
        if rope:
            seq.append(("rot", self.NPROJ - 1))
        seq += [("v", i) for i in range(T)] + [("out", i) for i in range(T)]
        self.place = {it: (n % 4, n // 4) for n, it in enumerate(seq)}
        self.uses = len(seq) // 4
        assert len(seq) % 4 == 0 and self.place["v", 0][0] == 0
        u = NB * self.uses
        self.bank_full, self.bank_free = self.sems("bank_full", 4, u), self.sems("bank_free", 4, u)
        self.row_items = (0 if cross else self.ROWS * C) + T
        u = T // 2 + NB * self.row_items // 2
        self.row_full, self.row_free = self.sems("rowmax_full", 2, u), self.sems("rowmax_free", 2, u)
        self.norm = Norm(m, "norm", NB)
        self.xt_high, self.fh, self.fl = s("xt_high", (NB + 1) * T), s("qk_high", NB * self.NPROJ), s("qk_low", NB * self.NPROJ)
        self.stacked = self.sems("stacked", 2, NB * 24 * 16)
        self.mdma = s("max_stacked", 0 if cross else NB * C * 16)
        self.t1_ready, self.rotated = s("cos_part", rope * NB * self.NPROJ), s("rotated", rope * NB * self.NPROJ)
        self.st_full, self.exp_done = self.sems("scores_full", 2, NB * NH), self.sems("exp_done", 2, NB * NH)
        self.pv_done, self.ctx_free, self.inverted = s("pv_done", NB * NH), s("ctx_free", NB * C * 2), s("sums_inverted", NB * C * 4)
        self.normed, self.ch, self.cl = (s(n, NB * C) for n in ("ctx_normed", "ctx_high", "ctx_low"))
        self.bias_added, self.scaled = s("bias_added", NB * T), s("gamma_applied", cross * NB * T)
        self.x_done = s("x_done", cross * NB * T)
        self.nconst = 16 * (4 + 3 * rope + 4 * cross)
        self.const, self.consts_done = s("const_loaded", self.nconst), s("consts_done", 2 + 5 * cross)

    def wait_free(self, eng, item, b):
        k, u = self.place[item]
        eng.wait_ge(*self.at(self.bank_free[k], b * self.uses + u))

    def wait_full(self, eng, item, b):
        k, u = self.place[item]
        eng.wait_ge(*self.at(self.bank_full[k], b * self.uses + u + 1))

    def wait_read(self, eng, item, b):
        k, u = self.place[item]
        eng.wait_ge(*self.at(self.bank_free[k], b * self.uses + u + 1))

    def bank(self, item):
        return self.m.ps[:, self.place[item][0], :]

    def proj_of(self, n):
        return n // 2 % 2, 2 * (n // 4) + n % 2

    ROWS = HG * T + 1

    def row(self, g, j):
        n = self.ROWS * g + j
        return n % 2, n // 2

    def xt_row(self, i):
        n = self.row_items - T + i
        return n % 2, n // 2

    def row_wait(self, eng, sem, place, b, done):
        k, u = place
        eng.wait_ge(*self.at(sem[k], u % (T // 2) + done if b is None else T // 2 + b * (self.row_items // 2) + u + done))

    def row_bank(self, place):
        return self.m.ps[:, 4 + place[0], :]

    WITH_V = [(2, 1, 2, 1), (1, 1, 2, 1), (1, 2, 1, 1), (0, 0, 0, 0)]
    WITH_UNIT = [(2, 1, 1, 1, 1), (1, 1, 1, 1, 1), (2, 1, 1, 1, 0), (0, 0, 0, 0, 0)]

    def first(self, table, i):
        return sum(sum(r) for r in table[:i])

    def sp(self, sp):
        m, io = self.m, self.io
        row = lambda a: a.rearrange("(a n) -> a n", a=1).broadcast_to([P, D])
        loads = [(self.vb, row(self.v_bias)), (self.ob, row(self.out_bias)),
                 (self.pb[:, 0:C], self.biases[0]),
                 (self.pb[:, C:2 * C], self.biases[1])]
        if self.rope:
            loads += [(self.cos, io["rope_cos"]), (self.sin, io["rope_sin"]), (self.rot, io["rope_rot"])]
        if self.cross:
            loads += [(self.gamma, row(io["L1_xattn_ln_gamma"])), (self.beta, row(io["L1_xattn_ln_beta"])),
                      (self.rs, io["L1_xattn_residual_scale"].rearrange("(a n) -> a n", a=1).broadcast_to([P, 1])),
                      (self.mask, io["mask_cols"])]
        if self.cross:
            sp.dma_start(m.raw[:, 0], io["ctxT"][0:D, :].rearrange("(c p) o -> p c o", p=P)).then_inc(self.raw_loaded, 16)
        for dst, src in loads:
            sp.dma_start(dst, src).then_inc(self.const, 16)
        sp.wait_ge(*self.at(self.const, 16 * len(loads)))
        with sp.Fori(0, NB) as b:
            if self.cross:
                nb = (b + 1) % NB
                sp.wait_ge(*self.at(self.audio_low, b + 1))
                sp.dma_start(m.raw[:, 0],
                             io["ctxT"][bass.ds(nb * D, D), :].rearrange("(c p) o -> p c o", p=P)).then_inc(self.raw_loaded, 16)
            for half in range(2):
                for w, stack, parts in ((0, self.kst, (0, 0, 1)), (1, self.qst, (0, 1, 0))):
                    sp.wait_ge(*self.at(self.fl, b * self.NPROJ + 4 * half + 2 * (w + 1)))
                    for r, part in enumerate(parts):
                        for j in range(HG):
                            sp.dma_start(stack[HD * r:HD * (r + 1)].rearrange("p (c j) t -> p c j t", j=HG)[:, 2 * half:2 * half + 2, j, :],
                                         self.qf[HD * j:HD * (j + 1), w, part, 2 * half:2 * half + 2]).then_inc(self.stacked[half], 16)
            if not self.cross:
                for g in range(C):
                    self.row_wait(sp, self.row_free, self.row(g, self.ROWS - 1), b, 1)
                    sp.dma_start(self.qst[3 * HD:3 * HD + 1, HG * g:HG * (g + 1), :].rearrange("p h t -> p (h t)"),
                                 self.mt[0:HG * T, :]).then_inc(self.mdma, 16)
        if self.cross:
            sp.wait_ge(*self.at(self.raw_loaded, 16 * (NB + 1)))

    def scores_rows(self):
        return 3 * HD if self.cross else 3 * HD + 1

    def pe_rowmax(self, pe, g, js, b):
        for j in js:
            head, t = HG * g + j // T, j % T
            at = self.row(g, j)
            self.row_wait(pe, self.row_free, at, b, 0)
            pe.matmul(self.row_bank(at), self.qst[0:3 * HD, head, t * P:(t + 1) * P],
                      self.kst[0:3 * HD, head, :], start=True, stop=True).then_inc(self.row_full[at[0]], 1)

    def pe_turn_max(self, pe, g, b):
        self.row_wait(pe, self.row_free, self.row(g, self.ROWS - 2), b, 1)
        at = self.row(g, self.ROWS - 1)
        self.row_wait(pe, self.row_free, at, b, 0)
        pe.transpose(self.row_bank(at)[0:HG * T, 0:P], self.mx, self.m.ident[:]).then_inc(self.row_full[at[0]], 1)

    def pe_turn_x(self, pe, i, b):
        m = self.m
        at = self.xt_row(i)
        self.row_wait(pe, self.row_free, at, b, 0)
        if i == 0 and b is not None:
            pe.wait_ge(*self.at(self.norm.xn_ready, b * T + T))
        for c in range(C):
            last = pe.transpose(self.row_bank(at)[:, c * P:(c + 1) * P], m.xn[:, i, c * P:(c + 1) * P], m.ident[:])
        last.then_inc(self.row_full[at[0]], 1)

    def pe_values(self, pe, u, b, ones):
        g, kb = divmod(u, T)
        if not ones:
            for h in range(2):
                pe.wait_ge(*self.at(self.exp_done[h], b * NH + u + 1))
            if kb == 0:
                pe.wait_ge(*self.at(self.ctx_free, (b * C + g) * 2))
        for j in range(HG):
            left = self.ones if ones else self.v[:, kb, HD * (HG * g + j):HD * (HG * g + j + 1)]
            last = pe.matmul(self.m.ps[HD * j:HD * (j + 1), 7 if ones else 6, :], left,
                             self.pt[:, u % 2, j * S:(j + 1) * S], start=kb == 0, stop=kb == T - 1,
                             tile_position=(0, HD * j))
        if ones:
            last.then_inc(self.pv_done, 1)

    def pe_proj(self, pe, n, b):
        m = self.m
        w, chunk = self.proj_of(n)
        item, c0 = ("proj", n), chunk * P
        src = self.cth if self.cross and w == 0 else m.xt
        self.wait_free(pe, item, b)
        three_passes(pe, self.bank(item), [lambda c: m.w[:, w, 0, c, c0:c0 + P], lambda c: m.w[:, w, 1, c, c0:c0 + P]],
                     [lambda c: src[:, 0, c, :], lambda c: src[:, 1, c, :]], range(C), range(C)).then_inc(self.bank_full[self.place[item][0]], 1)

    def pe_rotate(self, pe, n, b):
        item = ("rot", n)
        self.wait_free(pe, item, b)
        self.wait_read(pe, ("proj", n), b)
        pe.matmul(self.bank(item), self.rot, self.qb[:, n % 2, :], start=True, stop=True).then_inc(self.bank_full[self.place[item][0]], 1)

    def pe(self, pe):
        m = self.m
        pe.wait_ge(*self.at(self.const, self.nconst))
        pe.wait_ge(*self.at(self.consts_done, 2 + self.cross * 5))
        for i in range(T):
            self.pe_turn_x(pe, i, None)
        with pe.Fori(0, NB) as b:
            for k in range(2):
                pe.wait_ge(*self.at(self.row_free[k], T // 2 + b * (self.row_items // 2)))
            if self.cross:
                pe.wait_ge(*self.at(self.audio_low, b + 1))
            for n in range(self.NPROJ):
                self.pe_proj(pe, n, b)
                if self.rope and n:
                    self.pe_rotate(pe, n - 1, b)
            if self.rope:
                self.pe_rotate(pe, self.NPROJ - 1, b)
            a = self.cth if self.cross else m.xt
            for i in range(T):
                item = ("v", i)
                self.wait_free(pe, item, b)
                j = self.first(self.WITH_V, i)
                for c in range(C):
                    last = three_passes(pe, self.bank(item), [lambda c: a[:, 0, c, i * P:(i + 1) * P], lambda c: a[:, 1, c, i * P:(i + 1) * P]],
                                        [lambda c: m.w[:, 2, 0, c, :], lambda c: m.w[:, 2, 1, c, :]], [c], [c], start=c == 0, stop=c == C - 1)
                    if c == C - 1:
                        last.then_inc(self.bank_full[self.place[item][0]], 1)
                    if not self.cross:
                        if i == 0 and c == 0:
                            pe.wait_ge(*self.at(self.stacked[0], (b + 1) * 24 * 16))
                        self.pe_rowmax(pe, 0, range(j, j + self.WITH_V[i][c]), b)
                        j += self.WITH_V[i][c]
                        if i == T - 1 and c == 1:
                            self.pe_turn_max(pe, 0, b)
            self.pe_heads(pe, b)
            for c in range(C):
                if c == 0:
                    pe.wait_ge(*self.at(self.cl, b * C + C - 1))
                if c == C - 1:
                    pe.wait_ge(*self.at(self.cl, b * C + C))
                for i in range(T):
                    item = ("out", i)
                    if c == 0:
                        self.wait_free(pe, item, b)
                    last = three_passes(pe, self.bank(item), [lambda c: self.ct[:, 0, c, i * P:(i + 1) * P], lambda c: self.ct[:, 1, c, i * P:(i + 1) * P]],
                                        [lambda c: m.w[:, 3, 0, c, :], lambda c: m.w[:, 3, 1, c, :]], [c], [c], start=c == 0, stop=c == C - 1)
                    if c == C - 1:
                        last.then_inc(self.bank_full[self.place[item][0]], 1)

    def pe_heads(self, pe, b):
        if self.cross:
            pe.wait_ge(*self.at(self.stacked[0], (b + 1) * 24 * 16))
        R = self.scores_rows()
        for u in range(NH):
            g, kb = divmod(u, T)
            if u == T:
                pe.wait_ge(*self.at(self.stacked[1], (b + 1) * 24 * 16))
            slots, j = self.WITH_UNIT[kb], self.first(self.WITH_UNIT, kb)
            for step in range(5):
                if not self.cross and g + 1 < C:
                    self.pe_rowmax(pe, g + 1, range(j, j + slots[step]), b)
                    j += slots[step]
                    if kb == T - 1 and step == 0:
                        self.pe_turn_max(pe, g + 1, b)
                if step == 0 and kb == 0 and not self.cross:
                    pe.wait_ge(*self.at(self.mdma, (b * C + g + 1) * 16))
                if step < 2:
                    h = step
                    if u == 0:
                        for i in (2 * h, 2 * h + 1):
                            self.wait_read(pe, ("v", i), b)
                    else:
                        pe.wait_ge(*self.at((self.clipped if self.cross else self.exp_done)[h], b * NH + u))
                    for j4 in (2 * h, 2 * h + 1):
                        last = pe.matmul(self.m.ps[:, j4, :], self.kst[0:R, HG * g + j4, kb * P:(kb + 1) * P],
                                         self.qst[0:R, HG * g + j4, :], start=True, stop=True)
                    last.then_inc(self.st_full[h], 1)
                elif step < 4 and u:
                    self.pe_values(pe, u - 1, b, ones=step == 3)
                elif step == 4 and g == C - 1:
                    self.pe_turn_x(pe, kb, b)
        for i in range(T):
            self.wait_read(pe, ("v", i), b)
        self.pe_values(pe, NH - 1, b, ones=False)
        self.pe_values(pe, NH - 1, b, ones=True)

    def act_turn_x(self, act, i, b):
        at = self.xt_row(i)
        self.row_wait(act, self.row_full, at, b, 1)
        act.activation(self.m.xt[:, 0, :, i * P:(i + 1) * P], tile3(self.row_bank(at)), ACT.Copy).then_inc(self.xt_high, 1)

    def act_audio(self, act, n):
        act.wait_ge(*self.at(self.raw_loaded, n * 16 + 16))
        act.activation(self.cth[:, 0], self.m.raw[:, 0], ACT.Copy, scale=WSCALE).then_inc(self.audio_high, 1)

    def act_context(self, act, g, b):
        act.wait_ge(*self.at(self.pv_done, b * NH + T * (g + 1)))
        act.wait_ge(*self.at(self.cl, b * C + g))
        act.activation(self.sums, self.m.ps[:, 7, :], ACT.Copy).then_inc(self.ctx_free, 1)
        act.activation(self.ctxn, self.m.ps[:, 6, :], ACT.Copy).then_inc(self.ctx_free, 1)

    def act_context_high(self, act, g, b):
        act.wait_ge(*self.at(self.normed, b * C + g + 1))
        act.activation(self.ct[:, 0, g, :], self.ctxn, ACT.Copy).then_inc(self.ch, 1)

    def act(self, act):
        act.wait_ge(*self.at(self.const, self.nconst))
        act.wait_ge(*self.at(self.consts_done, 2 + self.cross * 5))
        descale = 1.0 / WSCALE
        if self.cross:
            self.act_audio(act, 0)
        for i in range(T):
            self.act_turn_x(act, i, None)
        with act.Fori(0, NB) as b:
            for n in range(self.NPROJ):
                item = ("proj", n)
                w, c = self.proj_of(n)
                self.wait_full(act, item, b)
                if self.rope:
                    act.wait_ge(*self.at(self.t1_ready, b * self.NPROJ + max(n - 1, 0)))
                    if n >= 2:
                        self.wait_full(act, ("rot", n - 2), b)
                    elif n == 0:
                        act.wait_ge(*self.at(self.exp_done[0], b * NH))
                else:
                    act.wait_ge(*self.at(self.fl, b * self.NPROJ + max(n - 1, 0)))
                s = descale if w or not self.cross else descale / WSCALE
                act.activation(self.qb[:, n % 2, :], self.bank(item), ACT.Identity, scale=s,
                               bias=self.pb[:, C * w + c:C * w + c + 1]).then_inc(self.bank_free[self.place[item][0]], 1)
                if not self.rope:
                    self.wait_read(act, item, b)
                    act.activation(self.qf[:, w, 0, c, :], self.qb[:, n % 2, :], ACT.Copy).then_inc(self.fh, 1)
            for u in range(NH):
                g, kb = divmod(u, T)
                for h in range(2):
                    out = self.pt[:, u % 2, 2 * h * S:(2 * h + 2) * S]
                    if self.cross:
                        act.wait_ge(*self.at(self.clipped[h], b * NH + u + 1))
                        src = out
                    else:
                        act.wait_ge(*self.at(self.st_full[h], b * NH + u + 1))
                        act.wait_ge(*self.at(self.pv_done, b * NH + max(u - 1, 0)))
                        src = flat(self.m.ps[:, 2 * h:2 * h + 2, :])
                    act.activation(out, src, ACT.Exp, scale=SOFTMAX_SCALE).then_inc(self.exp_done[h], 1)
                if kb == 0 and g:
                    self.act_context(act, g - 1, b)
                if kb == 2 and g:
                    self.act_context_high(act, g - 1, b)
                if g == C - 1:
                    self.act_turn_x(act, kb, b)
                    if kb == 1 and self.cross:
                        self.act_audio(act, b + 1)
            self.act_context(act, C - 1, b)
            self.act_context_high(act, C - 1, b)

    def dve_rowmax(self, v, g, js, b):
        for j in js:
            at = self.row(g, j)
            self.row_wait(v, self.row_full, at, b, 1)
            v.tensor_reduce(self.mx[:, j:j + 1], self.row_bank(at), AX.X, ALU.max).then_inc(self.row_free[at[0]], 1)

    def dve_turn_max(self, v, g, b):
        at = self.row(g, self.ROWS - 1)
        self.row_wait(v, self.row_full, at, b, 1)
        v.wait_ge(*self.at(self.mdma, (b * C + g) * 16))
        v.tensor_scalar(self.mt[0:HG * T, :], self.row_bank(at)[0:HG * T, 0:P], 1.0 / MSCALE, None,
                        ALU.mult).then_inc(self.row_free[at[0]], 1)

    def dve_turn_x(self, v, i, b):
        m = self.m
        at = self.xt_row(i)
        v.wait_ge(*self.at(self.xt_high, (i if b is None else (b + 1) * T + i) + 1))
        v.tensor_tensor(m.xt[:, 1, :, i * P:(i + 1) * P], tile3(self.row_bank(at)), m.xt[:, 0, :, i * P:(i + 1) * P],
                        ALU.subtract).then_inc(self.row_free[at[0]], 1)

    def dve_invert(self, v, g, k, b):
        v.wait_ge(*self.at(self.ctx_free, (b * C + g) * 2 + 1))
        part = self.sums[:, k * P:(k + 1) * P]
        v.reciprocal(part, part).then_inc(self.inverted, 1)

    def dve_audio(self, v, n):
        m = self.m
        v.wait_ge(*self.at(self.audio_high, n + 1))
        v.scalar_tensor_tensor(out=self.cth[:, 1].rearrange("p c t -> p (c t)"), in0=m.raw[:, 0].rearrange("p c t -> p (c t)"),
                               scalar=WSCALE, in1=self.cth[:, 0].rearrange("p c t -> p (c t)"),
                               op0=ALU.mult, op1=ALU.subtract).then_inc(self.audio_low, 1)

    def dve(self, v):
        m = self.m
        n = self.nconst
        v.memset(self.ones, 1.0).then_inc(self.consts_done, 1)
        v.memset(self.kst[3 * HD:3 * HD + 1].rearrange("p h t -> p (h t)"), -MSCALE).then_inc(self.consts_done, 1)
        v.wait_ge(*self.at(self.const, n))
        if self.cross:
            top = 50.0 / SOFTMAX_SCALE
            v.tensor_scalar(self.hi, self.mask, 0.5, 2.0 * top, ALU.is_gt, ALU.mult).then_inc(self.consts_done, 1)
            v.tensor_scalar(self.rs, self.rs, 0.0, 0.3, ALU.max, ALU.min).then_inc(self.consts_done, 1)
            v.wait_ge(*self.at(self.consts_done, 4))
            v.tensor_scalar(self.hi, self.hi, -top, None, ALU.add).then_inc(self.consts_done, 1)
            v.tensor_scalar(self.rs64, self.rs, 1.0 / WSCALE, None, ALU.mult).then_inc(self.consts_done, 1)
            v.tensor_scalar(self.ob, self.ob, self.rs, None, ALU.mult).then_inc(self.consts_done, 1)
            v.wait_ge(*self.at(self.consts_done, 7))
            self.dve_audio(v, 0)
        for i in range(T):
            self.dve_turn_x(v, i, None)
        with v.Fori(0, NB) as b:
            if self.rope:
                for n in range(self.NPROJ):
                    self.dve_rotate(v, n, b)
            for i in range(T):
                item = ("v", i)
                j = self.first(self.WITH_V, i)
                if not self.cross:
                    self.dve_rowmax(v, 0, range(j, j + sum(self.WITH_V[i])), b)
                    if i == T - 1:
                        self.dve_turn_max(v, 0, b)
                self.wait_full(v, item, b)
                v.scalar_tensor_tensor(out=self.v[:, i, :], in0=self.bank(item),
                                       scalar=1.0 / WSCALE / (WSCALE if self.cross else 1.0),
                                       in1=self.vb, op0=ALU.mult, op1=ALU.add).then_inc(self.bank_free[self.place[item][0]], 1)
            self.dve_heads(v, b)
            for i in range(T):
                item = ("out", i)
                self.wait_full(v, item, b)
                if self.cross:
                    v.scalar_tensor_tensor(out=self.delta[:, i, :], in0=self.bank(item), scalar=self.rs64, in1=self.ob,
                                           op0=ALU.mult, op1=ALU.add).then_inc(self.bank_free[self.place[item][0]], 1)
                else:
                    v.wait_ge(*self.at(self.bias_added, b * T + i + 1))
                    xs = slot(m.x, b * T + i)
                    v.scalar_tensor_tensor(out=xs, in0=self.bank(item), scalar=1.0 / WSCALE, in1=xs,
                                           op0=ALU.mult, op1=ALU.add).then_inc(self.bank_free[self.place[item][0]], 1)
            for i in range(T):
                self.wait_read(v, ("out", i), b)
            if self.cross:
                self.dve_delta(v, b)

    def dve_rotate(self, v, n, b):
        item = ("rot", n)
        w, c = self.proj_of(n)
        self.wait_full(v, item, b)
        v.wait_ge(*self.at(self.rotated, b * self.NPROJ + n))
        v.tensor_tensor(self.t2, self.bank(item), self.sin, ALU.mult).then_inc(self.bank_free[self.place[item][0]], 1)
        self.wait_read(v, item, b)
        v.wait_ge(*self.at(self.t1_ready, b * self.NPROJ + n + 1))
        v.wait_ge(*self.at(self.fl, b * self.NPROJ + max(n - 1, 0)))
        v.tensor_tensor(self.qr[:, n % 2, :], self.t1[:, n % 2, :], self.t2, ALU.add).then_inc(self.rotated, 1)
        v.wait_ge(*self.at(self.rotated, b * self.NPROJ + n + 1))
        v.tensor_copy(self.qf[:, w, 0, c, :], self.qr[:, n % 2, :]).then_inc(self.fh, 1)

    def dve_delta(self, v, b):
        m = self.m
        self.dnorm.dve_moments(v, b, lambda i: self.delta[:, i, :])
        v.wait_ge(*self.at(self.dnorm.moments, b * T + T))
        for i in range(T):
            d = self.delta[:, i, :]
            v.scalar_tensor_tensor(out=d, in0=d, scalar=m.mv[:, i, 0:1], in1=self.gamma,
                                   op0=ALU.subtract, op1=ALU.mult).then_inc(self.scaled, 1)
        v.wait_ge(*self.at(self.dnorm.rstd_ready, b + 1))
        v.wait_ge(*self.at(self.bias_added, b * T + T))
        v.wait_ge(*self.at(self.scaled, b * T + T))
        for i in range(T):
            xs = slot(m.x, b * T + i)
            v.scalar_tensor_tensor(out=xs, in0=self.delta[:, i, :], scalar=m.rstd[:, i:i + 1], in1=xs,
                                   op0=ALU.mult, op1=ALU.add).then_inc(self.x_done, 1)
        v.wait_ge(*self.at(self.x_done, b * T + T))

    def dve_heads(self, v, b):
        m = self.m
        for u in range(NH):
            g, kb = divmod(u, T)
            if u == NH - T:
                nb = (b + 1) % NB
                self.norm.dve_apply(v, b, lambda i: slot(m.x, nb * T + i), lambda i: m.xn[:, i, :])
            if self.cross:
                for h in range(2):
                    v.wait_ge(*self.at(self.st_full[h], b * NH + u + 1))
                    v.wait_ge(*self.at(self.pv_done, b * NH + max(u - 1, 0)))
                    v.tensor_scalar(self.pt[:, u % 2, 2 * h * S:(2 * h + 2) * S], flat(m.ps[:, 2 * h:2 * h + 2, :]),
                                    slot_col(self.hi, b * T + kb), -50.0 / SOFTMAX_SCALE, ALU.min, ALU.max).then_inc(self.clipped[h], 1)
                    if g and kb in (1, 2):
                        self.dve_invert(v, g - 1, 2 * (kb - 1) + h, b)
            elif g + 1 < C:
                j = self.first(self.WITH_UNIT, kb)
                for n in range(sum(self.WITH_UNIT[kb])):
                    self.dve_rowmax(v, g + 1, [j + n], b)
                    if g and kb == 1 and n < 4:
                        self.dve_invert(v, g - 1, n, b)
                if kb == T - 1:
                    self.dve_turn_max(v, g + 1, b)
            elif kb == 1:
                for n in range(4):
                    self.dve_invert(v, g - 1, n, b)
            if g == C - 1:
                self.dve_turn_x(v, kb, b)
                if self.cross and kb == T - 2:
                    self.dve_audio(v, b + 1)
            if u == NH - T - 1:
                nb = (b + 1) % NB
                self.norm.dve_moments(v, b, lambda i: slot(m.x, nb * T + i))
        for n in range(4):
            self.dve_invert(v, C - 1, n, b)

    def pool_context(self, g, c, b):
        g.wait_ge(*self.at(self.inverted, (b * C + c + 1) * 4))
        g.wait_ge(*self.at(self.ctx_free, (b * C + c + 1) * 2))
        g.tensor_tensor(self.ctxn, self.ctxn, self.sums, ALU.mult).then_inc(self.normed, 1)
        g.wait_ge(*self.at(self.ch, b * C + c + 1))
        g.tensor_tensor(self.ct[:, 1, c, :], self.ctxn, self.ct[:, 0, c, :], ALU.subtract).then_inc(self.cl, 1)

    def pool(self, g):
        m = self.m
        g.wait_ge(*self.at(self.const, self.nconst))
        g.wait_ge(*self.at(self.consts_done, 2 + self.cross * 5))
        with g.Fori(0, NB) as b:
            g.wait_ge(*self.at(self.norm.xn_ready, b * T))
            for n in range(self.NPROJ):
                if self.rope:
                    self.wait_read(g, ("proj", n), b)
                    g.wait_ge(*self.at(self.rotated, b * self.NPROJ + max(n - 1, 0)))
                    g.tensor_tensor(self.t1[:, n % 2, :], self.qb[:, n % 2, :], self.cos, ALU.mult).then_inc(self.t1_ready, 1)
                    if n:
                        self.pool_low(g, n - 1, b)
                else:
                    self.pool_low(g, n, b)
            if self.rope:
                self.pool_low(g, self.NPROJ - 1, b)
            for i in range(T):
                xs = slot(m.x, b * T + i)
                g.tensor_tensor(xs, xs, self.beta if self.cross else self.ob, ALU.add).then_inc(self.bias_added, 1)
            for c in range(C):
                if c == C - 2:
                    self.norm.pool(g, b)
                self.pool_context(g, c, b)
            if self.cross:
                self.dnorm.pool(g, b)

    def pool_low(self, g, n, b):
        src = self.qr if self.rope else self.qb
        w, c = self.proj_of(n)
        g.wait_ge(*self.at(self.fh, b * self.NPROJ + n + 1))
        g.tensor_tensor(self.qf[:, w, 1, c, :], src[:, n % 2, :], self.qf[:, w, 0, c, :],
                        ALU.subtract).then_inc(self.fl, 1)


def slot_col(ap, i):
    return ap[:, bass.ds(i, 1)]


def flat(ap):
    return ap.rearrange("p a b -> p (a b)")


class Experts(Phase):

    def __init__(self, m, name):
        super().__init__(m, name)
        take = m.take
        self.mask = take(NE * NB * S, F16).rearrange("p (e t) -> p e t", e=NE)
        self.ids = m.raw[:, 0].rearrange("p c o -> p (c o)").bitcast(I32)
        self.mx = take(2 * NE * C * S, F16).rearrange("p (a e n) -> p a e n", a=2, e=NE)
        self.ma = take(2 * C * NE * S, F16).rearrange("p (a f e t) -> p a f e t", a=2, f=C, e=NE)
        self.gate = take(2 * S).rearrange("p (n t) -> p n t", n=2)
        self.a = take(2 * S).rearrange("p (n t) -> p n t", n=2)
        self.ahl = take(2 * S, F16).rearrange("p (a t) -> p a t", a=2)
        s = self.sem
        self.ids_loaded, self.masks = s("ids_loaded", 16), s("masks_made", 2 * NE - 2)
        self.norm = Norm(m, "norm", NB)
        self.bank_full, self.bank_free = self.sems("bank_full", 4, NB * 2), self.sems("bank_free", 4, NB * 2)
        self.y_full, self.y_free = self.sems("y_full", 4, NB), self.sems("y_free", 4, NB)
        self.xt_high, self.mx_done, self.gated = s("xt_high", NB * T), s("inputs_masked", NB * 2 * NE), s("silu_done", NB * C)
        self.a_split, self.ma_done = s("act_split", NB * 2 * C), s("act_masked", NB * 2 * C)

    def sp(self, sp):
        sp.dma_start(self.ids, self.io["itok"].rearrange("(a n) -> a n", a=1).broadcast_to([P, NB * S])).then_inc(self.ids_loaded, 16)
        sp.wait_ge(*self.at(self.ids_loaded, 16))

    def pe(self, pe):
        m = self.m
        with pe.Fori(0, NB) as b:
            for i in range(T):
                pe.wait_ge(*self.at(self.bank_free[i], b * 2))
                if i == 0:
                    pe.wait_ge(*self.at(self.norm.xn_ready, b * T))
                for c in range(C):
                    last = pe.transpose(m.ps[:, i, c * P:(c + 1) * P], m.xn[:, i, c * P:(c + 1) * P], m.ident[:])
                last.then_inc(self.bank_full[i], 1)
            for f in range(C):
                pe.wait_ge(*self.at(self.bank_free[f], b * 2 + 1))
                for e in range(NE):
                    if f == 0:
                        pe.wait_ge(*self.at(self.mx_done, b * 2 * NE + 2 * (e + 1)))
                    last = three_passes(pe, m.ps[:, f, :], [lambda c: m.w[:, e, 0, c, f * P:(f + 1) * P], lambda c: m.w[:, e, 1, c, f * P:(f + 1) * P]],
                                        [lambda c: self.mx[:, 0, e, c * S:(c + 1) * S], lambda c: self.mx[:, 1, e, c * S:(c + 1) * S]],
                                        range(C), range(C), start=e == 0, stop=e == NE - 1)
                last.then_inc(self.bank_full[f], 1)
            for f in range(C):
                pe.wait_ge(*self.at(self.ma_done, b * 2 * C + 2 * (f + 1)))
                for i in range(T):
                    if f == 0:
                        pe.wait_ge(*self.at(self.y_free[i], b))
                    for e in range(NE):
                        last = three_passes(pe, m.ps[:, 4 + i, :], [lambda f: self.ma[:, 0, f, e, i * P:(i + 1) * P], lambda f: self.ma[:, 1, f, e, i * P:(i + 1) * P]],
                                            [lambda f: m.w[:, e, 0, f, :], lambda f: m.w[:, e, 1, f, :]], [f], [f],
                                            start=f == 0 and e == 0, stop=f == C - 1 and e == NE - 1)
                    if f == C - 1:
                        last.then_inc(self.y_full[i], 1)

    def act(self, act):
        m = self.m
        with act.Fori(0, NB) as b:
            for i in range(T):
                act.wait_ge(*self.at(self.bank_full[i], b * 2 + 1))
                act.activation(m.xt[:, 0, :, i * P:(i + 1) * P], tile3(m.ps[:, i, :]), ACT.Copy).then_inc(self.xt_high, 1)
            for f in range(C):
                act.wait_ge(*self.at(self.bank_full[f], b * 2 + 2))
                act.wait_ge(*self.at(self.ma_done, b * 2 * C + 2 * max(f - 1, 0)))
                act.activation(self.gate[:, f % 2, :], m.ps[:, f, :], ACT.Silu, scale=1.0 / WSCALE).then_inc(self.gated, 1)

    def dve(self, v):
        m = self.m
        v.wait_ge(*self.at(self.ids_loaded, 16))
        k = VOCAB_PER_EXPERT
        v.tensor_scalar(self.mask[:, 0, :], self.ids, float(k), None, ALU.is_lt).then_inc(self.masks, 1)
        for e in range(1, NE):
            v.tensor_scalar(self.mask[:, e, :], self.ids, float(e * k), None, ALU.is_ge).then_inc(self.masks, 1)
        v.wait_ge(*self.at(self.masks, NE))
        for e in range(1, NE - 1):
            v.scalar_tensor_tensor(out=self.mask[:, e, :], in0=self.ids, scalar=float((e + 1) * k), in1=self.mask[:, e, :],
                                   op0=ALU.is_lt, op1=ALU.mult).then_inc(self.masks, 1)
        v.wait_ge(*self.at(self.masks, 2 * NE - 2))
        with v.Fori(0, NB) as b:
            for i in range(T):
                v.wait_ge(*self.at(self.xt_high, b * T + i + 1))
                v.tensor_tensor(m.xt[:, 1, :, i * P:(i + 1) * P], tile3(m.ps[:, i, :]), m.xt[:, 0, :, i * P:(i + 1) * P],
                                ALU.subtract).then_inc(self.bank_free[i], 1)
            for i in range(T):
                v.wait_ge(*self.at(self.bank_free[i], b * 2 + 1))
            for e in range(NE):
                own = self.mask[:, e:e + 1, bass.ds(b * S, S)].broadcast_to([P, C, S])
                for a in range(2):
                    v.tensor_tensor(self.mx[:, a, e, :].rearrange("p (c t) -> p c t", c=C), m.xt[:, a, :, :], own,
                                    ALU.mult).then_inc(self.mx_done, 1)
            for f in range(C):
                v.wait_ge(*self.at(self.gated, b * C + f + 1))
                v.wait_ge(*self.at(self.a_split, b * 2 * C + 2 * f))
                v.scalar_tensor_tensor(out=self.a[:, f % 2, :], in0=m.ps[:, f, :], scalar=1.0 / WSCALE, in1=self.gate[:, f % 2, :],
                                       op0=ALU.mult, op1=ALU.mult).then_inc(self.bank_free[f], 1)
                v.wait_ge(*self.at(self.bank_free[f], b * 2 + 2))
                v.wait_ge(*self.at(self.ma_done, b * 2 * C + 2 * f))
                v.tensor_copy(self.ahl[:, 0, :], self.a[:, f % 2, :]).then_inc(self.a_split, 1)
                v.wait_ge(*self.at(self.a_split, b * 2 * C + 2 * f + 1))
                v.tensor_tensor(self.ahl[:, 1, :], self.a[:, f % 2, :], self.ahl[:, 0, :], ALU.subtract).then_inc(self.a_split, 1)
                for a in range(2):
                    if a:
                        v.wait_ge(*self.at(self.a_split, b * 2 * C + 2 * f + 2))
                    v.tensor_tensor(self.ma[:, a, f], self.ahl[:, a:a + 1, :].broadcast_to([P, NE, S]),
                                    self.mask[:, :, bass.ds(b * S, S)], ALU.mult).then_inc(self.ma_done, 1)
            nb = (b + 1) % NB
            self.norm.dve(v, b, lambda i: slot(m.x, nb * T + i), lambda i: m.xn[:, i, :])
            for i in range(T):
                v.wait_ge(*self.at(self.y_full[i], b + 1))
                xs = slot(m.x, b * T + i)
                v.scalar_tensor_tensor(out=xs, in0=m.ps[:, 4 + i, :], scalar=1.0 / WSCALE, in1=xs,
                                       op0=ALU.mult, op1=ALU.add).then_inc(self.y_free[i], 1)
            for i in range(T):
                v.wait_ge(*self.at(self.y_free[i], b + 1))

    def pool(self, g):
        with g.Fori(0, NB) as b:
            self.norm.pool(g, b)


class BitMlp(Phase):

    def __init__(self, m, name):
        super().__init__(m, name)
        take = m.take
        self.b1, self.b2 = take(INNER), take(D)
        self.h = take(3 * INNER).rearrange("p (n f) -> p n f", n=3)
        self.q2 = take(2 * INNER, F16).rearrange("p (n f) -> p n f", n=2)
        self.q2t = take(2 * INNER, F16).rearrange("p (n f) -> p n f", n=2)
        self.junk = take(INNER)
        self.q1f = take(T * D).rearrange("p (t d) -> p t d", t=T)
        self.q1 = take(T * D, F16).rearrange("p (t d) -> p t d", t=T)
        self.ms, self.am, self.r, self.top, self.inv, self.f, self.alpha = (take(2 * T) for _ in range(7))
        self.negmean, self.absum, self.absum2 = take(2), take(8), take(2)
        self.signs = m.w[:].rearrange("p n a c o -> p (n a c o)")
        s = self.sem
        self.raw_loaded, self.const = self.sems("raw_loaded", 2, 16 * 4), s("const_loaded", 32)
        self.pos_done, self.sign_done, self.abs_done = s("positive", 8), s("signs_made", 8), s("abs_summed", 8)
        self.abs2, self.allred, self.mean_done = s("abs_totalled", 1), s("abs_all", 1), s("means_ready", 1)
        self.norm = Norm(m, "norm", NB)
        self.bank_full, self.bank_free = self.sems("bank_full", 4, NB * 5), self.sems("bank_free", 4, NB * 5)
        self.t_full, self.t_free = self.sems("turn_full", 2, NB * T), self.sems("turn_free", 2, NB * T)
        self.y_full, self.y_free = self.sems("y_full", 2, NB * 2), self.sems("y_free", 2, NB * 2)
        self.per = 3 + 1 + 5 + 2 * T + T * (1 + 1 + 5 + 2)
        self.chain, self.power, self.powered = s("chain", NB * self.per), s("power_wanted", NB * (T + 1)), s("power_ready", NB * (T + 1))
        self.q1_done, self.gelu_done, self.ss_done, self.q2_done = (s(n, NB * T) for n in ("q1_done", "gelu_done", "squares_summed", "q2_done"))
        self.bias_added = s("bias_added", NB * T)

    def sp(self, sp):
        io, m = self.io, self.m
        row = lambda a, n: a.rearrange("(a n) -> a n", a=1).broadcast_to([P, n])
        sp.dma_start(self.b1, row(io["L0_ffn_b1"], INNER)).then_inc(self.const, 16)
        sp.dma_start(self.b2, row(io["L0_ffn_b2"], D)).then_inc(self.const, 16)
        for n in range(8):
            if n >= 2:
                sp.wait_ge(*self.at(self.sign_done, n - 1))
                sp.wait_ge(*self.at(self.abs_done, n - 1))
            src = (io["L0_ffn_w1T"][n * P:(n + 1) * P, :].rearrange("p (c o) -> p c o", c=C) if n < 4 else
                   io["L0_ffn_w2T"][(n - 4) * D:(n - 3) * D, :].rearrange("(c p) o -> p c o", p=P))
            sp.dma_start(m.raw[:, n % 2], src).then_inc(self.raw_loaded[n % 2], 16)
        sp.wait_ge(*self.at(self.const, 32))

    def pe(self, pe):
        m = self.m
        sg = self.signs
        pe.wait_ge(*self.at(self.sign_done, 8))
        with pe.Fori(0, NB) as b:
            for i in range(T):
                pe.wait_ge(*self.at(self.q1_done, b * T + i + 1))
                pe.wait_ge(*self.at(self.bank_free[i], b * 5))
                for c in range(C):
                    last = pe.transpose(m.ps[:, i, 0:256].bitcast(F16)[:, c * P:(c + 1) * P], self.q1[:, i, c * P:(c + 1) * P], m.ident16[:])
                last.then_inc(self.bank_full[i], 1)
            for st in range(T + 2):
                i = st
                if i < T:
                    pe.wait_ge(*self.at(self.bank_free[i], b * 5 + 1))
                    for n in range(4):
                        pe.wait_ge(*self.at(self.bank_free[n], b * 5 + 1 + i))
                        for c in range(C):
                            last = pe.matmul(m.ps[:, n, :], m.xt[:, 0, c, i * P:(i + 1) * P],
                                             sg[:, c * INNER + n * 512:c * INNER + (n + 1) * 512], start=c == 0, stop=c == C - 1)
                        last.then_inc(self.bank_full[n], 1)
                i = st - 2
                if i >= 0:
                    pe.wait_ge(*self.at(self.q2_done, b * T + i + 1))
                    for k in range(2):
                        pe.wait_ge(*self.at(self.t_free[k], b * T + i))
                        for c in range(8):
                            last = pe.transpose(m.ps[:, 4 + k, :].bitcast(F16)[:, c * P:(c + 1) * P],
                                                self.q2[:, i % 2, (8 * k + c) * P:(8 * k + c + 1) * P], m.ident16[:])
                        last.then_inc(self.t_full[k], 1)
                    pe.wait_ge(*self.at(self.y_free[i % 2], b * 2 + i // 2))
                    for c in range(NI):
                        if c % 8 == 0:
                            pe.wait_ge(*self.at(self.t_free[c // 8], b * T + i + 1))
                        last = pe.matmul(m.ps[:, 6 + i % 2, :], self.q2t[:, i % 2, c * P:(c + 1) * P],
                                         sg[:, C * INNER + c * D:C * INNER + (c + 1) * D], start=c == 0, stop=c == NI - 1)
                    last.then_inc(self.y_full[i % 2], 1)

    def act(self, act):
        m = self.m
        for n in range(8):
            act.wait_ge(*self.at(self.raw_loaded[n % 2], 16 * (n // 2 + 1)))
            if n:
                act.wait_ge(*self.at(self.abs_done, n))
            act.activation(self.junk, flat(m.raw[:, n % 2]), ACT.Abs, accum_out=self.absum[:, n:n + 1]).then_inc(self.abs_done, 1)
        with act.Fori(0, NB) as b:
            for i in range(T):
                act.wait_ge(*self.at(self.bank_full[i], b * 5 + 1))
                act.activation(m.xt[:, 0, :, i * P:(i + 1) * P], tile3(m.ps[:, i, 0:256].bitcast(F16)), ACT.Copy).then_inc(self.bank_free[i], 1)
            for st in range(T + 2):
                i = st
                if i < T:
                    act.wait_ge(*self.at(self.bank_free[3], b * 5 + 2 + i))
                    act.activation(self.h[:, i % 3, :], self.h[:, i % 3, :], ACT.Gelu).then_inc(self.gelu_done, 1)
                    act.wait_ge(*self.at(self.gelu_done, b * T + i + 1))
                    act.wait_ge(*self.at(self.ss_done, b * T + i))
                    if i == 0:
                        act.wait_ge(*self.at(self.abs_done, 8))
                    act.activation(self.junk, self.h[:, i % 3, :], ACT.Square,
                                   accum_out=self.ms[:, T + i:T + i + 1]).then_inc(self.ss_done, 1)
                i = st - 2
                if i >= 0:
                    for k in range(2):
                        act.wait_ge(*self.at(self.t_full[k], b * T + i + 1))
                        act.activation(self.q2t[:, i % 2, k * 1024:(k + 1) * 1024], m.ps[:, 4 + k, :].bitcast(F16), ACT.Copy).then_inc(self.t_free[k], 1)

    def row_factors(self, v, ch, cols, dim, which, powers):
        ch.wait(v)
        v.wait_ge(*self.at(self.powered, powers))
        c = cols
        d = dim ** -0.5
        ch.put(v.scalar_tensor_tensor(out=self.top[:, c], in0=self.r[:, c], scalar=d, in1=self.am[:, c], op0=ALU.mult, op1=ALU.mult))
        ch.wait(v)
        ch.put(v.tensor_scalar(self.top[:, c], self.top[:, c], 1e-5, None, ALU.max))
        ch.wait(v)
        ch.put(v.reciprocal(self.inv[:, c], self.top[:, c]))
        ch.put(v.tensor_scalar(self.alpha[:, c], self.top[:, c], self.negmean[:, which:which + 1], 1.0 / 127.0, ALU.mult, ALU.mult))
        ch.wait(v)
        ch.put(v.scalar_tensor_tensor(out=self.f[:, c], in0=self.inv[:, c], scalar=127.0 * d, in1=self.r[:, c], op0=ALU.mult, op1=ALU.mult))
        ch.wait(v)

    def quantise(self, v, ch, src, tmp, dst, factor, done):
        ch.put(v.tensor_scalar(tmp, src, factor, 127.0, ALU.mult, ALU.min))
        ch.wait(v)
        ch.put(v.tensor_scalar(tmp, tmp, -128.0, MAGIC, ALU.max, ALU.add))
        ch.wait(v)
        v.tensor_scalar(dst, tmp, -MAGIC, None, ALU.add).then_inc(done, 1)

    def dve(self, v):
        m = self.m
        for n in range(8):
            v.wait_ge(*self.at(self.raw_loaded[n % 2], 16 * (n // 2 + 1)))
            if n:
                v.wait_ge(*self.at(self.sign_done, n))
            v.tensor_scalar(self.h[:, 0, :], flat(m.raw[:, n % 2]), 0.0, None, ALU.is_gt).then_inc(self.pos_done, 1)
            v.wait_ge(*self.at(self.pos_done, n + 1))
            v.scalar_tensor_tensor(out=self.signs[:, n * INNER:(n + 1) * INNER], in0=flat(m.raw[:, n % 2]), scalar=0.0,
                                   in1=self.h[:, 0, :], op0=ALU.is_lt, op1=ALU.subtract).then_inc(self.sign_done, 1)
        v.wait_ge(*self.at(self.abs_done, 8))
        v.wait_ge(*self.at(self.sign_done, 8))
        v.tensor_reduce(self.absum2, self.absum.rearrange("p (a n) -> p a n", a=2), AX.X, ALU.add).then_inc(self.abs2, 1)
        v.wait_ge(*self.at(self.allred, 1))
        v.tensor_scalar(self.negmean, self.negmean, -1.0 / (INNER * D), None, ALU.mult).then_inc(self.mean_done, 1)
        v.wait_ge(*self.at(self.mean_done, 1))
        v.wait_ge(*self.at(self.const, 32))
        with v.Fori(0, NB) as b:
            ch = Chain(self, self.chain, self.per, b)
            c4 = slice(0, T)
            ch.wait(v)
            ch.put(v.tensor_reduce(self.am[:, c4], m.xn[:], AX.X, ALU.max, apply_absolute_value=True))
            var = m.mv[:, :, 1:2].rearrange("p t a -> p (t a)")
            ch.put(v.tensor_tensor(self.ms[:, c4], var, m.rstd[:], ALU.mult))
            ch.wait(v)
            ch.put(v.tensor_tensor(self.ms[:, c4], self.ms[:, c4], m.rstd[:], ALU.mult))
            ch.wait(v)
            ch.put(v.tensor_scalar(self.r[:, c4], self.ms[:, c4], 1e-6, None, ALU.add))
            ch.wait(v)
            v.tensor_copy(self.f[:, c4], self.r[:, c4]).then_inc(self.power, 1)
            v.wait_ge(*self.at(self.power, b * (T + 1) + 1))
            self.row_factors(v, ch, c4, D, 0, b * (T + 1) + 1)
            for i in range(T):
                self.quantise(v, ch, m.xn[:, i, :], self.q1f[:, i, :], self.q1[:, i, :], self.f[:, i:i + 1], self.q1_done)
            for st in range(T + 2):
                i = st
                if i < T:
                    if i == 3:
                        v.wait_ge(*self.at(self.q2_done, b * T + 1))
                    for n in range(4):
                        v.wait_ge(*self.at(self.bank_full[n], b * 5 + 2 + i))
                        v.scalar_tensor_tensor(out=self.h[:, i % 3, n * 512:(n + 1) * 512], in0=m.ps[:, n, :], scalar=self.alpha[:, i:i + 1],
                                               in1=self.b1[:, n * 512:(n + 1) * 512], op0=ALU.mult, op1=ALU.add).then_inc(self.bank_free[n], 1)
                i = st - 1
                if 0 <= i < T:
                    col = slice(T + i, T + i + 1)
                    v.wait_ge(*self.at(self.gelu_done, b * T + i + 1))
                    ch.put(v.tensor_reduce(self.am[:, col], self.h[:, i % 3, :], AX.X, ALU.max, apply_absolute_value=True))
                    v.wait_ge(*self.at(self.ss_done, b * T + i + 1))
                    ch.put(v.tensor_scalar(self.r[:, col], self.ms[:, col], 1.0 / INNER, 1e-6, ALU.mult, ALU.add))
                    ch.wait(v)
                    v.tensor_copy(self.f[:, col], self.r[:, col]).then_inc(self.power, 1)
                    v.wait_ge(*self.at(self.power, b * (T + 1) + i + 2))
                    self.row_factors(v, ch, col, INNER, 1, b * (T + 1) + i + 2)
                    self.quantise(v, ch, self.h[:, i % 3, :], self.h[:, i % 3, :], self.q2[:, i % 2, :], self.f[:, T + i:T + i + 1], self.q2_done)
                i = st - 2
                if i >= 0:
                    v.wait_ge(*self.at(self.y_full[i % 2], b * 2 + i // 2 + 1))
                    v.wait_ge(*self.at(self.bias_added, b * T + i + 1))
                    xs = slot(m.x, b * T + i)
                    v.scalar_tensor_tensor(out=xs, in0=m.ps[:, 6 + i % 2, :], scalar=self.alpha[:, T + i:T + i + 1], in1=xs,
                                           op0=ALU.mult, op1=ALU.add).then_inc(self.y_free[i % 2], 1)
                if st == T - 1:
                    v.wait_ge(*self.at(self.q1_done, b * T + T))
                    nb = (b + 1) % NB
                    self.norm.dve(v, b, lambda i: slot(m.x, nb * T + i), lambda i: m.xn[:, i, :])
            for k in range(2):
                v.wait_ge(*self.at(self.y_free[k], b * 2 + 2))
            v.wait_ge(*self.at(self.norm.xn_ready, b * T + T))
            v.wait_ge(*self.at(self.q2_done, b * T + T))
            ch.close()

    def pool(self, g):
        m = self.m
        g.wait_ge(*self.at(self.abs2, 1))
        g.partition_all_reduce(self.negmean, self.absum2, P, RADD).then_inc(self.allred, 1)
        g.wait_ge(*self.at(self.const, 32))

        def inverse_root(k, b, cols):
            g.wait_ge(*self.at(self.power, b * (T + 1) + k + 1))
            g.tensor_tensor(self.r[:, cols], self.f[:, cols], m.mhalf[:, 0:cols.stop - cols.start], ALU.pow).then_inc(self.powered, 1)

        with g.Fori(0, NB) as b:
            g.wait_ge(*self.at(self.norm.xn_ready, b * T))
            inverse_root(0, b, slice(0, T))
            for i in range(T):
                xs = slot(m.x, b * T + i)
                g.tensor_tensor(xs, xs, self.b2, ALU.add).then_inc(self.bias_added, 1)
            for i in range(3):
                inverse_root(1 + i, b, slice(T + i, T + i + 1))
                if i == 2:
                    self.norm.pool(g, b)
            inverse_root(T, b, slice(2 * T - 1, 2 * T))


class Fp8Linear(Phase):

    def __init__(self, m, name):
        super().__init__(m, name)
        take = m.take
        self.y = take(NB * T * D).rearrange("p (t d) -> p t d", t=NB * T)
        self.v = take(2 * T * D).rearrange("p (n d) -> p n d", n=2)
        self.p2 = take(2 * T * D).rearrange("p (n d) -> p n d", n=2)
        self.q = take(2 * T * D, F16).rearrange("p (n d) -> p n d", n=2)
        self.bias = take(D)
        self.am, self.top, self.ws, self.ws64 = take(NB), take(4), take(1), take(1)
        s = self.sem
        self.const, self.wdone, self.normed, self.peak = s("const_loaded", 48), s("weight_split", 3), Norm(m, "norm", NB), s("peaks", NB + 1)
        self.allred, self.scale, self.chain, self.q_done = s("peak_all", 1), s("scale_ready", 3), s("chain", 4 * NB), s("q_done", NB)
        self.bank_full, self.bank_free = self.sems("bank_full", 4, NB), self.sems("bank_free", 4, NB)
        self.y_full, self.y_free = self.sems("y_full", 4, NB), self.sems("y_free", 4, NB)
        self.bias_added, self.stored = s("bias_added", NB * T), s("stored", 16 * NB * T)

    def sp(self, sp):
        io, m = self.io, self.m
        row = lambda a, n: a.rearrange("(a n) -> a n", a=1).broadcast_to([P, n])
        sp.dma_start(m.raw[:, 0], io["L1_ffn_weightT"].rearrange("(c p) o -> p c o", p=P)).then_inc(self.const, 16)
        sp.dma_start(self.bias, row(io["L1_ffn_bias"], D)).then_inc(self.const, 16)
        sp.dma_start(self.ws, row(io["L1_ffn_weight_scale"], 1)).then_inc(self.const, 16)
        sp.wait_ge(*self.at(self.const, 48))
        with sp.Fori(0, NB) as b:
            for i in range(T):
                sp.wait_ge(*self.at(self.y_free[i], b + 1))
                sp.dma_start(io["out"][bass.ds(b, 1), i * P:(i + 1) * P, :].rearrange("b p d -> p (b d)"),
                             slot(m.x, b * T + i)).then_inc(self.stored, 16)
        sp.wait_ge(*self.at(self.stored, 16 * NB * T))

    def pe(self, pe):
        m = self.m
        pe.wait_ge(*self.at(self.wdone, 3))
        with pe.Fori(0, NB) as b:
            pe.wait_ge(*self.at(self.q_done, b + 1))
            for i in range(T):
                pe.wait_ge(*self.at(self.bank_free[i], b))
                for c in range(C):
                    last = pe.transpose(m.ps[:, i, 0:256].bitcast(F16)[:, c * P:(c + 1) * P],
                                        self.q[:, 0, i * D + c * P:i * D + (c + 1) * P], m.ident16[:])
                last.then_inc(self.bank_full[i], 1)
            for i in range(T):
                pe.wait_ge(*self.at(self.bank_free[i], b + 1))
                pe.wait_ge(*self.at(self.y_free[i], b))
                for c in range(C):
                    for a in range(2):
                        last = pe.matmul(m.ps[:, 4 + i, :], m.xt[:, 0, c, i * P:(i + 1) * P], m.w[:, 0, a, c, :],
                                         start=c == 0 and a == 0, stop=c == C - 1 and a == 1)
                last.then_inc(self.y_full[i], 1)

    def act(self, act):
        m = self.m
        with act.Fori(0, NB) as b:
            for i in range(T):
                act.wait_ge(*self.at(self.bank_full[i], b + 1))
                act.activation(m.xt[:, 0, :, i * P:(i + 1) * P], tile3(m.ps[:, i, 0:256].bitcast(F16)), ACT.Copy).then_inc(self.bank_free[i], 1)

    def dve(self, v):
        m = self.m
        v.wait_ge(*self.at(self.const, 48))
        v.tensor_scalar(self.ws64, self.ws, WSCALE, None, ALU.mult).then_inc(self.scale, 1)
        v.wait_ge(*self.at(self.scale, 1))
        v.tensor_scalar(flat(m.raw[:, 1]), flat(m.raw[:, 0]), self.ws64, None, ALU.mult).then_inc(self.wdone, 1)
        v.wait_ge(*self.at(self.wdone, 1))
        v.tensor_copy(flat(m.w[:, 0, 0]), flat(m.raw[:, 1])).then_inc(self.wdone, 1)
        v.wait_ge(*self.at(self.wdone, 2))
        v.tensor_tensor(flat(m.w[:, 0, 1]), flat(m.raw[:, 1]), flat(m.w[:, 0, 0]), ALU.subtract).then_inc(self.wdone, 1)
        with v.Fori(0, NB) as b:
            self.normed.dve(v, b, lambda i: slot(m.x, b * T + i), lambda i: slot(self.y, b * T + i))
            v.wait_ge(*self.at(self.normed.xn_ready, b * T + T))
            v.tensor_reduce(slot_col(self.am, b), self.y[:, bass.ds(b * T, T), :].rearrange("p t d -> p (t d)"), AX.X, ALU.max,
                            apply_absolute_value=True).then_inc(self.peak, 1)
        v.wait_ge(*self.at(self.peak, NB))
        v.tensor_reduce(self.top[:, 0:1], self.am, AX.X, ALU.max).then_inc(self.peak, 1)
        v.wait_ge(*self.at(self.allred, 1))
        v.tensor_scalar(self.top[:, 2:3], self.top[:, 1:2], 1.0 / 448.0, 1e-7, ALU.mult, ALU.max).then_inc(self.scale, 1)
        v.wait_ge(*self.at(self.scale, 2))
        v.reciprocal(self.top[:, 3:4], self.top[:, 2:3]).then_inc(self.scale, 1)
        v.wait_ge(*self.at(self.scale, 3))
        val, pw = self.v[:, 0, :], self.p2[:, 0, :]
        with v.Fori(0, NB) as b:
            ch = Chain(self, self.chain, 4, b)
            v.wait_ge(*self.at(self.q_done, b))
            ch.put(v.tensor_scalar(val, self.y[:, bass.ds(b * T, T), :].rearrange("p t d -> p (t d)"), self.top[:, 3:4], None, ALU.mult))
            ch.wait(v)
            ch.put(v.tensor_scalar(pw.bitcast(I32), val.bitcast(I32), 0x7F800000, None, ALU.bitwise_and))
            ch.wait(v)
            ch.put(v.tensor_scalar(pw, pw, 2.0 ** -6, 1.5 * 2.0 ** 20, ALU.max, ALU.mult))
            ch.wait(v)
            ch.put(v.tensor_tensor(val, val, pw, ALU.add))
            ch.wait(v)
            for i in range(T):
                v.wait_ge(*self.at(self.bank_full[i], b))
            v.tensor_tensor(self.q[:, 0, :], val, pw, ALU.subtract).then_inc(self.q_done, 1)
            ch.close()
            for i in range(T):
                v.wait_ge(*self.at(self.y_full[i], b + 1))
                v.wait_ge(*self.at(self.bias_added, b * T + i + 1))
                xs = slot(m.x, b * T + i)
                v.scalar_tensor_tensor(out=xs, in0=m.ps[:, 4 + i, :], scalar=1.0 / WSCALE, in1=xs,
                                       op0=ALU.mult, op1=ALU.add).then_inc(self.y_free[i], 1)

    def pool(self, g):
        m = self.m
        g.wait_ge(*self.at(self.const, 48))
        with g.Fori(0, NB) as b:
            self.normed.pool(g, b)
        g.wait_ge(*self.at(self.peak, NB + 1))
        g.partition_all_reduce(self.top[:, 1:2], self.top[:, 0:1], P, RMAX).then_inc(self.allred, 1)
        with g.Fori(0, NB) as b:
            for i in range(T):
                xs = slot(m.x, b * T + i)
                g.tensor_tensor(xs, xs, self.bias, ALU.add).then_inc(self.bias_added, 1)


class Finish(Phase):

    def __init__(self, m):
        super().__init__(m, "finish")
        self.stored = self.sem("stored", 16)

    def sp(self, sp):
        sp.dma_start(self.io["out"].rearrange("b (t p) d -> p (b t) d", p=P), self.m.x[:]).then_inc(self.stored, 16)
        sp.wait_ge(*self.at(self.stored, 16))


def program(nc, io, stages):
    with ExitStack() as ctx:
        m = Machine(nc, ctx, io)
        phases = stages(m, io)
        block = ctx.enter_context(nc.Block())

        @block.tensor
        def _(pe):
            m.barrier(pe, 0)
            for k, ph in enumerate(phases):
                ph.pe(pe)
                m.barrier(pe, k + 1)

        @block.scalar
        def _(act):
            m.barrier(act, 0)
            for k, ph in enumerate(phases):
                ph.act(act)
                m.barrier(act, k + 1)

        @block.vector
        def _(v):
            m.barrier(v, 0)
            for k, ph in enumerate(phases):
                ph.dve(v)
                m.barrier(v, k + 1)

        @block.gpsimd
        def _(g):
            m.barrier(g, 0)
            for k, ph in enumerate(phases):
                ph.pool(g)
                m.barrier(g, k + 1)

        @block.sync
        def _(sp):
            for sem in m.sems.values():
                sp.sem_inc(sem, 1)
            m.barrier(sp, 0)
            for k, ph in enumerate(phases):
                ph.sp(sp)
                m.barrier(sp, k + 1)


def decoder(nc, io):
    def stages(m, t):
        qkv = t["L1_attn_w_qkvT"]
        return [Start(m),
                Weights(m, "w_attn0", [t["L0_attn_k_wT"], t["L0_attn_q_wT"], t["L0_attn_v_wT"], t["L0_attn_out_wT"]]),
                Attention(m, "attn0", t["L0_attn_q_b_cols"], t["L0_attn_k_b_cols"], t["L0_attn_v_b"], t["L0_attn_out_b"], rope=True),
                Weights(m, "w_experts", [t["ctxT"][e * D:(e + 1) * D, :] for e in range(NE)]),
                Experts(m, "experts"),
                BitMlp(m, "bit"),
                Weights(m, "w_attn1", [qkv[:, D:2 * D], qkv[:, 0:D], qkv[:, 2 * D:3 * D], t["L1_attn_w_outT"]]),
                Attention(m, "attn1", t["L1_attn_q_b_cols"], t["L1_attn_k_b_cols"], t["L1_attn_v_b"], t["L1_attn_b_out"]),
                Weights(m, "w_xattn", [t["L1_xattn_WkT"], t["L1_xattn_WqT"], t["L1_xattn_WvT"], t["L1_xattn_WoT"]]),
                Attention(m, "xattn", t["L1_xattn_bq_cols"], t["L1_xattn_bk_cols"], t["L1_xattn_bv"], t["L1_xattn_bo"], cross=True),
                Fp8Linear(m, "fp8")]
    program(nc, io, stages)


def layout(inputs):
    import numpy as np
    a = {k: np.ascontiguousarray(v) for k, v in inputs.items()}
    for k in ("L0_attn_q_w", "L0_attn_k_w", "L0_attn_v_w", "L0_attn_out_w", "L0_ffn_w1", "L0_ffn_w2", "L1_attn_w_qkv",
              "L1_attn_w_out", "L1_xattn_Wq", "L1_xattn_Wk", "L1_xattn_Wv", "L1_xattn_Wo", "L1_ffn_weight"):
        a[k + "T"] = np.ascontiguousarray(a.pop(k).T)
    a["ctxT"] = np.ascontiguousarray(a.pop("ctx_2048").transpose(0, 2, 1)).reshape(NB * D, S)
    for k in ("L1_xattn_residual_scale", "L1_ffn_weight_scale"):
        a[k] = a[k].reshape(1)
    cols = lambda v: np.ascontiguousarray(v.reshape(-1, P).T)
    b1 = a["L1_attn_b_qkv"]
    a["L1_attn_q_b_cols"], a["L1_attn_k_b_cols"], a["L1_attn_v_b"] = cols(b1[0:D]), cols(b1[D:2 * D]), np.ascontiguousarray(b1[2 * D:])
    for k in ("L0_attn_q_b", "L0_attn_k_b", "L1_xattn_bq", "L1_xattn_bk"):
        a[k + "_cols"] = cols(a.pop(k))
    a["mask_cols"] = cols(a.pop("mask_BxS2_ik0"))
    a["itok"] = a.pop("itok_BxS_13_99985").reshape(-1)
    a["ident"] = np.eye(P, dtype=np.float32)
    half = HD // 2
    inv = (np.float32(1.0) / np.float32(10000.0) ** (np.arange(0, HD, 2, dtype=np.float32) / np.float32(HD))).astype(np.float32)
    angle = (np.arange(S, dtype=np.float32)[None, :] * inv[:, None]).astype(np.float32)
    angle = np.tile(angle, (2 * HG, 1))
    a["rope_cos"], a["rope_sin"] = np.cos(angle).astype(np.float32), np.sin(angle).astype(np.float32)
    rot = np.zeros((P, P), np.float32)
    for o in range(P):
        first = o % HD < half
        rot[o + half if first else o - half, o] = -1.0 if first else 1.0
    a["rope_rot"] = rot
    return a


def kernel(**inputs):
    import concourse.bacc as bacc
    from concourse import mybir as _mybir
    from concourse.bass_utils import run_bass_kernel_spmd as run

    nc = bacc.Bacc("TRN2", target_bir_lowering=False, num_devices=1)
    arrays = layout(inputs)
    io = {k: nc.dram_tensor(f"in_{k}", v.shape, _mybir.dt.from_np(v.dtype), kind="ExternalInput").ap() for k, v in arrays.items()}
    io["out"] = nc.dram_tensor("out", (NB, S, D), F32, kind="ExternalOutput").ap()
    decoder(nc, io)
    r = run(nc, [{f"in_{k}": v for k, v in arrays.items()}], core_ids=[0])
    return r.results[0]["out"]
```

```python
from contextlib import ExitStack

import concourse.bass as bass
from concourse import mybir

P = 128
NB = 4
S = 512
D = 512
NH = 16
HD = D // NH
T = S // P
C = D // P
HG = P // HD
NE = 4
INNER = 2048
NI = INNER // P
WSCALE = 64.0
MSCALE = 64.0
ARENA = 27 * 1024 + 600
SIGN_PARTS = 8
SIGN_PART = D * INNER // P // SIGN_PARTS
NSLOT = NB * T + NE - 1
EPS = 1e-5
MAGIC = 1.5 * 2.0 ** 23
VOCAB_PER_EXPERT = 25000 // NE

ALU = mybir.AluOpType
ACT = mybir.ActivationFunctionType
AX = mybir.AxisListType
F32 = mybir.dt.float32
F16 = mybir.dt.float16
I32 = mybir.dt.int32
RMAX = bass.bass_isa.ReduceOp.max
RADD = bass.bass_isa.ReduceOp.add
SOFTMAX_SCALE = HD ** -0.5


def tile3(ap):
    return ap.rearrange("p (c t) -> p c t", t=P)


class Chain:

    def __init__(self, phase, sem, per, b):
        self.at, self.sem, self.per, self.base, self.n = phase.at, sem, per, b * per, 0

    def put(self, ins):
        ins.then_inc(self.sem, 1)
        self.n += 1

    def wait(self, eng):
        eng.wait_ge(*self.at(self.sem, self.base + self.n))

    def close(self):
        assert self.n == self.per, (self.sem, self.n, self.per)


class Machine:

    def __init__(self, nc, ctx, io):
        self.nc, self.ctx, self.io = nc, ctx, io
        sb = lambda name, shape, dt: ctx.enter_context(nc.sbuf_tensor(name, shape, dt))
        self.x = sb("x", [P, NB * T, D], F32)
        self.xn = sb("xn", [P, T, D], F32)
        self.xt = sb("xt", [P, 2, C, S], F16)
        self.w = sb("w", [P, 4, 2, C, D], F16)
        self.raw = sb("raw", [P, 2, C, D], F32)
        self.arena = sb("arena", [P, ARENA], F32)
        matrix = lambda a: a.rearrange("p (c o) -> p c o", c=C)
        self.tails = [matrix(self.arena[:, ARENA - (k + 1) * C * D:ARENA - k * C * D]) for k in (1, 0)]
        self.signs = self.arena[:, ARENA - C * INNER:].bitcast(F16)
        self.abs_sums = sb("abs_sums", [P, 2 * SIGN_PARTS], F32)
        self.turned = self.xt[:].rearrange("p a c t -> p (a c t)").bitcast(F32).rearrange("p (c o) -> p c o", c=C)
        self.raws = [self.raw[:, 0], self.raw[:, 1]]
        self.ident = sb("ident", [P, P], F32)
        self.ident16 = sb("ident16", [P, P], F16)
        self.place = sb("place", [P, NB * T], I32)
        self.slot_expert = sb("slot_expert", [P, NSLOT], I32)
        self.mhalf = sb("mhalf", [P, T], F32)
        self.carrier = sb("carrier", [P, 1], F32)
        self.eps = sb("eps", [P, T], F32)
        self.stats = sb("stats", [P, T, 6], F32)
        self.mv = sb("mv", [P, T, 2], F32)
        self.rstd = sb("rstd", [P, T], F32)
        self.final_mean, self.final_rstd = sb("final_mean", [P, NB * T], F32), sb("final_rstd", [P, NB * T], F32)
        self.final_peak = sb("final_peak", [P, NB], F32)
        self.ps = ctx.enter_context(nc.psum_tensor("ps", [P, 8, 512], F32))
        self.phase_end = ctx.enter_context(nc.semaphore("phase_end"))
        self.sems, self.count, self.first = {}, {}, {}
        self.used = 0

    def sem(self, name, total, first=1):
        if name not in self.sems:
            self.sems[name] = self.ctx.enter_context(self.nc.semaphore(name))
            self.first[name] = self.count[name] = first
        self.taken.append(name)
        assert self.taken.count(name) == 1, name
        self.start[name] = self.count[name]
        self.count[name] += total
        return self.sems[name]

    def next_phase(self):
        self.used, self.taken, self.start = 0, [], {}
        return self.start

    def take(self, n, dt=F32):
        words = (n + 1) // 2 if dt == F16 else n
        a = self.arena[:, self.used:self.used + words]
        self.used += words
        assert self.used <= ARENA, self.used
        return a if dt == F32 else a.bitcast(dt)

    def take_back(self, g, b):
        for t in range(b * T, (b + 1) * T):
            g.indirect_dma_start(self.x[:, t, :], None, self.io["sorted_y"][:, :], bass.IndirectOffsetOnAxis(self.place[:, t:t + 1], 0),
                                 compute_op=ALU.add).then_inc(self.gathered[b], 16)

    def wait_back(self, eng, *batches):
        for b in batches:
            eng.wait_ge(self.gathered[b], 16 * T)

    def barrier(self, eng, k):
        eng.drain().then_inc(self.phase_end, 1)
        eng.wait_ge(self.phase_end, 5 * (k + 1))


def counter(start):
    return lambda sem, n: (sem, start[sem.name] + n)


def slot(ap, i):
    return ap[:, bass.ds(i, 1), :].rearrange("p a n -> p (a n)")


class Norm:

    def __init__(self, m, name, calls):
        self.m = m
        self.sums = m.sem(f"{name}_bn_sums", calls * T)
        self.moments = m.sem(f"{name}_moments", calls * T)
        self.rstd_ready = m.sem(f"{name}_rstd_ready", calls)
        self.eps_added = m.sem(f"{name}_eps_added", calls)
        self.xn_ready = m.sem(f"{name}_xn_ready", calls * T)
        self.at = counter(m.start)

    def dve_moments(self, v, b, src):
        m = self.m
        for i in range(T):
            v.bn_stats(m.stats[:, i, :], src(i)).then_inc(self.sums, 1)
        v.wait_ge(*self.at(self.sums, b * T + T))
        v.memset(m.carrier[:], 0.0)
        for i in range(T):
            v.bn_aggr(m.mv[:, i, :], m.stats[:, i, :]).then_inc(self.moments, 1)

    def dve_apply(self, v, b, src, dst):
        m = self.m
        v.wait_ge(*self.at(self.moments, b * T + T))
        v.wait_ge(*self.at(self.rstd_ready, b + 1))
        for i in range(T):
            v.tensor_scalar(dst(i), src(i), m.mv[:, i, 0:1], m.rstd[:, i:i + 1],
                            ALU.subtract, ALU.mult).then_inc(self.xn_ready, 1)

    def dve(self, v, b, src, dst):
        self.dve_moments(v, b, src)
        self.dve_apply(v, b, src, dst)

    def pool(self, g, b):
        m = self.m
        g.wait_ge(*self.at(self.moments, b * T + T))
        g.tensor_tensor(m.rstd[:], m.mv[:, :, 1:2].rearrange("p t a -> p (t a)"), m.eps[:],
                        ALU.add).then_inc(self.eps_added, 1)
        g.wait_ge(*self.at(self.eps_added, b + 1))
        g.tensor_tensor(m.rstd[:], m.rstd[:], m.mhalf[:], ALU.pow).then_inc(self.rstd_ready, 1)


class Phase:
    def __init__(self, m, name):
        self.m, self.name = m, name
        self.following = None
        self.at = counter(m.next_phase())
        self.io = m.io

    def sem(self, name, total):
        return self.m.sem(name, total)

    def sem_from_zero(self, name, total):
        return self.m.sem(name, total, first=0)

    def sems(self, name, n, total):
        return [self.sem(f"{name}{i}", total) for i in range(n)]

    def sp_following(self, sp):
        if self.following:
            self.following.sp_early(sp)

    def sp_early(self, sp): pass

    def pe(self, pe): pass
    def act(self, act): pass
    def dve(self, v): pass
    def pool(self, g): pass
    def sp(self, sp): pass


class Start(Phase):

    def __init__(self, m):
        super().__init__(m, "start")
        s, take = self.sem, m.take
        self.x_loaded, self.const = self.sems("x_loaded", 2, 16), s("const_loaded", 16 * 4)
        self.norm = Norm(m, "norm", 1)
        self.consts, self.memsets, self.filled = s("consts_done", 2), s("ones_and_zero", 2), s("zero_filled", 16)
        n = NE * NB * T
        e_t = lambda a: a.rearrange("p (e t) -> p e t", e=NE)
        self.ids = take(NB * T, I32)
        self.own, self.total, self.before, self.rank = (e_t(take(n)) for _ in range(4))
        self.tri, self.ones, self.starts = take(P), take(P), take(NSLOT)
        self.cut = e_t(take(n))
        self.n, self.tiles, self.base = take(NE), take(NE), take(NE)
        self.placef, self.expertf = take(NB * T), take(NSLOT)
        self.zero = m.arena[:, ARENA - D:]
        self.own_made, self.counted, self.chain = s("experts_known", 1), s("tokens_counted", 1), s("chain", 60)
        m.zero_filled, m.x_all = self.at(self.filled, 16), self.at(self.x_loaded[1], 16)

    def sp(self, sp):
        m, io = self.m, self.io
        for dst, src in ((self.ids, io["itok_cols"]), (m.ident[:], io["ident"]), (self.tri, io["triangle"]), (self.starts, io["slot_starts"])):
            sp.dma_start(dst, src).then_inc(self.const, 16)
        for k, b in ((0, slice(0, 1)), (1, slice(1, NB))):
            sp.dma_start(m.x[:, b.start * T:b.stop * T, :], io["x"][b].rearrange("b (t p) d -> p (b t) d", p=P)).then_inc(self.x_loaded[k], 16)
            if k == 0:
                self.sp_following(sp)
        sp.wait_ge(*self.at(self.memsets, 2))
        sp.dma_start(io["sorted_x"].rearrange("(s p) d -> p s d", p=P),
                     self.zero.rearrange("p (a d) -> p a d", a=1).broadcast_to([P, NSLOT, D])).then_inc(self.filled, 16)

    def pool(self, g):
        g.memset(self.m.mhalf[:], -0.5).then_inc(self.consts, 1)
        g.memset(self.m.eps[:], EPS).then_inc(self.consts, 1)
        g.wait_ge(*self.at(self.consts, 2))
        self.norm.pool(g, 0)

    def pe(self, pe):
        m = self.m
        pe.wait_ge(*self.at(self.own_made, 1))
        pe.wait_ge(*self.at(self.memsets, 2))
        n = NE * NB * T
        pe.matmul(m.ps[:, 0, 0:n], self.tri, flat(self.own), start=True, stop=True)
        pe.matmul(m.ps[:, 1, 0:n], self.ones, flat(self.own), start=True, stop=True).then_inc(self.counted, 1)

    def dve(self, v):
        m = self.m
        v.memset(self.ones, 1.0).then_inc(self.memsets, 1)
        v.memset(self.zero, 0.0).then_inc(self.memsets, 1)
        v.wait_ge(*self.at(self.const, 16 * 4))
        v.tensor_copy(m.ident16[:], m.ident[:])
        ch = Chain(self, self.chain, 60, 0)
        k = VOCAB_PER_EXPERT
        ch.put(v.tensor_scalar(self.own[:, 0, :], self.ids, float(k), None, ALU.is_lt))
        for e in range(1, NE):
            ch.put(v.tensor_scalar(self.own[:, e, :], self.ids, float(e * k), None, ALU.is_ge))
        ch.wait(v)
        for e in range(1, NE - 1):
            ch.put(v.scalar_tensor_tensor(out=self.own[:, e, :], in0=self.ids, scalar=float((e + 1) * k), in1=self.own[:, e, :],
                                          op0=ALU.is_lt, op1=ALU.mult))
        ch.wait(v)
        v.memset(self.before[:, :, 0:1], 0.0).then_inc(self.own_made, 1)
        v.wait_ge(*self.at(self.x_loaded[0], 16))
        self.norm.dve(v, 0, lambda i: m.x[:, i, :], lambda i: m.xn[:, i, :])
        n = NE * NB * T
        v.wait_ge(*self.at(self.counted, 1))
        ch.put(v.tensor_copy(flat(self.total), m.ps[:, 1, 0:n]))
        for t in range(1, NB * T):
            ch.wait(v)
            ch.put(v.tensor_tensor(self.before[:, :, t:t + 1], self.before[:, :, t - 1:t], self.total[:, :, t - 1:t], ALU.add))
        ch.wait(v)
        last = slice(NB * T - 1, NB * T)
        ch.put(v.tensor_tensor(self.n.rearrange("p (e a) -> p e a", a=1), self.before[:, :, last], self.total[:, :, last], ALU.add))
        ch.wait(v)
        shape = [P, NE, NB * T]
        ch.put(v.tensor_tensor(self.cut, self.n.rearrange("p (e a) -> p e a", a=1).broadcast_to(shape),
                               self.starts[:, 0:NB * T].rearrange("p (a t) -> p a t", a=1).broadcast_to(shape), ALU.is_gt))
        ch.wait(v)
        ch.put(v.tensor_reduce(self.tiles, self.cut, AX.X, ALU.add))
        ch.put(v.memset(self.base[:, 0:1], 0.0))
        for e in range(1, NE):
            ch.wait(v)
            ch.put(v.scalar_tensor_tensor(out=self.base[:, e:e + 1], in0=self.tiles[:, e - 1:e], scalar=float(P),
                                          in1=self.base[:, e - 1:e], op0=ALU.mult, op1=ALU.add))
        ch.put(v.tensor_tensor(flat(self.rank), m.ps[:, 0, 0:n], flat(self.before), ALU.add))
        ch.wait(v)
        ch.put(v.tensor_tensor(self.rank, self.rank, self.base.rearrange("p (e a) -> p e a", a=1).broadcast_to(shape), ALU.add))
        ch.wait(v)
        ch.put(v.tensor_tensor(flat(self.rank), flat(self.rank), flat(self.own), ALU.mult))
        ch.wait(v)
        ch.put(v.tensor_reduce(self.placef, self.rank.rearrange("p e t -> p t e"), AX.X, ALU.add))
        ch.put(v.tensor_scalar(self.expertf, self.starts, self.base[:, 1:2], None, ALU.is_ge))
        for e in range(2, NE):
            ch.wait(v)
            ch.put(v.scalar_tensor_tensor(out=self.expertf, in0=self.starts, scalar=self.base[:, e:e + 1], in1=self.expertf,
                                          op0=ALU.is_ge, op1=ALU.add))
        ch.wait(v)
        v.tensor_copy(m.place[:], self.placef)
        v.tensor_copy(m.slot_expert[:], self.expertf)


class Weights:

    def __init__(self, phase, mats, bufs, early):
        self.m, self.at, self.mats, self.bufs, self.early = phase.m, phase.at, mats, bufs, early
        n = len(mats)
        self.loaded = [phase.sem(f"weight_loaded{k}", 16) for k in range(n)]
        self.high_done, self.low_done = phase.sem("weight_high", n), phase.sem("weight_low", n)

    def buf(self, n):
        return self.bufs[n]

    def load(self, sp, n):
        sp.dma_start(self.buf(n), self.mats[n].rearrange("(c p) o -> p c o", p=P)).then_inc(self.loaded[n], 16)

    def sp_early(self, sp):
        for n in range(self.early):
            self.load(sp, n)

    def sp_rest(self, sp):
        for n in range(self.early, len(self.mats)):
            for k in range(n - 1, -1, -1):
                if self.bufs[k] is self.bufs[n]:
                    self.wait(sp, k)
                    break
            self.load(sp, n)

    def act(self, act, n):
        act.wait_ge(*self.at(self.loaded[n], 16))
        act.activation(self.m.w[:, n, 0], self.buf(n), ACT.Copy, scale=WSCALE).then_inc(self.high_done, 1)

    def dve(self, v, n):
        v.wait_ge(*self.at(self.high_done, n + 1))
        v.scalar_tensor_tensor(out=flat(self.m.w[:, n, 1]), in0=flat(self.buf(n)), scalar=WSCALE,
                               in1=flat(self.m.w[:, n, 0]), op0=ALU.mult, op1=ALU.subtract).then_inc(self.low_done, 1)

    def wait(self, eng, n):
        eng.wait_ge(*self.at(self.low_done, n + 1))


def three_passes(pe, out, left, right, cl, cr, start=True, stop=True):
    n = len(cl)
    for k in range(n):
        for a, (l, r) in enumerate(((0, 0), (0, 1), (1, 0))):
            last = pe.matmul(out, left[l](cl[k]), right[r](cr[k]), start=start and k == 0 and a == 0,
                             stop=stop and k == n - 1 and a == 2)
    return last


class Attention(Phase):

    NPROJ = 2 * C

    def __init__(self, m, name, mats, bufs, early, q_bias, k_bias, v_bias, out_bias, rope=False, cross=False):
        super().__init__(m, name)
        self.weights = Weights(self, mats, bufs, early)
        self.rope, self.cross = rope, cross
        self.biases = (k_bias, q_bias)
        self.v_bias, self.out_bias = v_bias, out_bias
        take = m.take
        self.qst = take(NH * S, F16).rearrange("p (h t) -> p h t", h=NH)
        self.kst = take(NH * S, F16).rearrange("p (h t) -> p h t", h=NH)
        self.qf = take(4 * C * S, F16).rearrange("p (w a c t) -> p w a c t", w=2, a=2, c=C)
        self.v = take(T * D).rearrange("p (t d) -> p t d", t=T)
        self.ct = take(2 * C * S, F16).rearrange("p (a c t) -> p a c t", a=2, c=C)
        self.qb = take(2 * S).rearrange("p (n t) -> p n t", n=2)
        if rope:
            self.t1 = take(2 * S).rearrange("p (n t) -> p n t", n=2)
            self.t2 = take(S)
            self.qr = take(2 * S).rearrange("p (n t) -> p n t", n=2)
            self.cos, self.sin, self.rot = take(S), take(S), take(P)
        self.ctxn, self.sums = take(S), take(S)
        self.vb, self.ob = take(D), take(D)
        self.pb = take(2 * C)
        self.mx = take(HG * T)
        self.mt = take(P, F16)
        self.ones = take(HD)
        s = self.sem
        if cross:
            self.cth = m.raw[:, 1].rearrange("p c o -> p (c o)").bitcast(F16).rearrange("p (a c t) -> p a c t", a=2, c=C)
            self.gamma, self.beta = take(D), take(D)
            self.rs, self.rs64 = take(1), take(1)
            self.mask, self.hi = take(NB * T, I32), take(NB * T)
            self.audio_loaded, self.audio_high, self.audio_low = s("audio_loaded", 16 * (NB + 1)), s("audio_high", NB + 1), s("audio_low", NB + 1)
            self.audio_scaled = s("audio_scaled", NB + 1)
            self.clipped = self.sems("clipped", 2, NB * NH)
            self.dnorm = Norm(m, "delta", NB)
            self.peak = s("peaks", NB)
            self.kept = s("final_kept", 2 * NB)
        if cross or rope:
            self.ynorm = Norm(m, "final_norm", NB)
        if rope:
            self.place_now, self.pool_carrier = take(T, I32), take(1)
            self.place_ready, self.xn_sent = s("place_ready", NB), s("xn_sent", NB)
            self.scattered = self.sem_from_zero("scattered", 16 * NB * T)
        self.pt = take(2 * HG * S).rearrange("p (n t) -> p n t", n=2)
        if cross:
            self.delta = take(T * D).rearrange("p (t d) -> p t d", t=T)
        seq = []
        for n in range(self.NPROJ):
            seq.append(("proj", n))
            if rope and n:
                seq.append(("rot", n - 1))
        if rope:
            seq.append(("rot", self.NPROJ - 1))
        seq += [("v", i) for i in range(T)] + [("out", i) for i in range(T)]
        self.place = {it: (n % 4, n // 4) for n, it in enumerate(seq)}
        self.uses = len(seq) // 4
        assert len(seq) % 4 == 0 and self.place["v", 0][0] == 0
        u = NB * self.uses
        self.bank_full, self.bank_free = self.sems("bank_full", 4, u), self.sems("bank_free", 4, u)
        self.row_items = (0 if cross else self.ROWS * C) + T
        u = T // 2 + NB * self.row_items // 2
        self.row_full, self.row_free = self.sems("rowmax_full", 2, u), self.sems("rowmax_free", 2, u)
        self.norm = Norm(m, "norm", NB)
        self.xt_high, self.fh, self.fl = s("xt_high", (NB + 1) * T), s("qk_high", NB * self.NPROJ), s("qk_low", NB * self.NPROJ)
        self.stacked = self.sems("stacked", 2, NB * 24 * 16)
        self.mdma = s("max_stacked", 0 if cross else NB * C * 16)
        self.t1_ready, self.rotated = s("cos_part", rope * NB * self.NPROJ), s("rotated", rope * NB * self.NPROJ)
        self.st_full, self.exp_done = self.sems("scores_full", 2, NB * NH), self.sems("exp_done", 2, NB * NH)
        self.pv_done, self.ctx_free, self.inverted = s("pv_done", NB * NH), s("ctx_free", NB * (C - 1) * 2), s("sums_inverted", NB * C * 4)
        self.normed, self.ch, self.cl = (s(n, NB * C) for n in ("ctx_normed", "ctx_high", "ctx_low"))
        self.bias_added, self.scaled = s("bias_added", NB * T), s("gamma_applied", cross * NB * T)
        self.x_done = s("x_done", cross * NB * T)
        self.nconst = 16 * (4 + 3 * rope + 4 * cross)
        self.const, self.consts_done = s("const_loaded", self.nconst), s("consts_done", 2 + 5 * cross)

    def wait_free(self, eng, item, b):
        k, u = self.place[item]
        eng.wait_ge(*self.at(self.bank_free[k], b * self.uses + u))

    def wait_full(self, eng, item, b):
        k, u = self.place[item]
        eng.wait_ge(*self.at(self.bank_full[k], b * self.uses + u + 1))

    def wait_read(self, eng, item, b):
        k, u = self.place[item]
        eng.wait_ge(*self.at(self.bank_free[k], b * self.uses + u + 1))

    def bank(self, item):
        return self.m.ps[:, self.place[item][0], :]

    def proj_of(self, n):
        w = n // 2 % 2
        return (1 - w if self.cross else w), 2 * (n // 4) + n % 2

    ROWS = HG * T + 1

    def row(self, g, j):
        n = self.ROWS * g + j
        return n % 2, n // 2

    def xt_row(self, i):
        n = self.row_items - T + i
        return n % 2, n // 2

    def row_wait(self, eng, sem, place, b, done):
        k, u = place
        eng.wait_ge(*self.at(sem[k], u % (T // 2) + done if b is None else T // 2 + b * (self.row_items // 2) + u + done))

    def row_bank(self, place):
        return self.m.ps[:, 4 + place[0], :]

    WITH_V = [(2, 1, 2, 1), (1, 1, 2, 1), (1, 2, 1, 1), (0, 0, 0, 0)]
    WITH_UNIT = [(2, 1, 1, 2, 1), (1, 1, 1, 1, 0), (2, 1, 1, 1, 0), (0, 0, 0, 0, 0)]
    INVERT = [(), (0, 1), (2,), (3,)]

    def first(self, table, i):
        return sum(sum(r) for r in table[:i])

    def sp(self, sp):
        m, io = self.m, self.io
        row = lambda a: a.rearrange("(a n) -> a n", a=1).broadcast_to([P, D])
        loads = [(self.vb, row(self.v_bias)), (self.ob, row(self.out_bias)),
                 (self.pb[:, 0:C], self.biases[0]),
                 (self.pb[:, C:2 * C], self.biases[1])]
        if self.rope:
            loads += [(self.cos, io["rope_cos"]), (self.sin, io["rope_sin"]), (self.rot, io["rope_rot"])]
        if self.cross:
            loads += [(self.gamma, row(io["L1_xattn_ln_gamma"])), (self.beta, row(io["L1_xattn_ln_beta"])),
                      (self.rs, io["L1_xattn_residual_scale"].rearrange("(a n) -> a n", a=1).broadcast_to([P, 1])),
                      (self.mask, io["mask_cols"])]
        for dst, src in loads:
            sp.dma_start(dst, src).then_inc(self.const, 16)
        self.weights.sp_rest(sp)
        sp.wait_ge(*self.at(self.const, 16 * len(loads)))
        with sp.Fori(0, NB) as b:
            if self.cross:
                nb = (b + 1) % NB
                sp.wait_ge(*self.at(self.audio_low, b + 1))
                sp.dma_start(m.raw[:, 0],
                             io["ctxT"][bass.ds(nb * D, D), :].rearrange("(c p) o -> p c o", p=P)).then_inc(self.audio_loaded, 16)
            for half in range(2):
                order = ((0, self.kst, (0, 0, 1)), (1, self.qst, (0, 1, 0)))
                for n, (w, stack, parts) in enumerate(reversed(order) if self.cross else order):
                    sp.wait_ge(*self.at(self.fl, b * self.NPROJ + 4 * half + 2 * (n + 1)))
                    for r, part in enumerate(parts):
                        for j in range(HG):
                            sp.dma_start(stack[HD * r:HD * (r + 1)].rearrange("p (c j) t -> p c j t", j=HG)[:, 2 * half:2 * half + 2, j, :],
                                         self.qf[HD * j:HD * (j + 1), w, part, 2 * half:2 * half + 2]).then_inc(self.stacked[half], 16)
            if not self.cross:
                for g in range(C):
                    self.row_wait(sp, self.row_free, self.row(g, self.ROWS - 1), b, 1)
                    sp.dma_start(self.qst[3 * HD:3 * HD + 1, HG * g:HG * (g + 1), :].rearrange("p h t -> p (h t)"),
                                 self.mt[0:HG * T, :]).then_inc(self.mdma, 16)
        if self.cross:
            sp.wait_ge(*self.at(self.audio_low, NB + 1))
        else:
            self.weights.wait(sp, len(self.weights.mats) - 1)
        if self.rope:
            for k in range(2):
                sp.wait_ge(*self.at(self.row_free[k], T // 2 + NB * (self.row_items // 2)))
        self.sp_following(sp)
        if self.rope:
            self.following.weights.sp_rest(sp)

    def sp_early(self, sp):
        self.weights.sp_early(sp)
        if self.cross:
            sp.dma_start(self.m.raw[:, 0], self.io["ctxT"][0:D, :].rearrange("(c p) o -> p c o", p=P)).then_inc(self.audio_loaded, 16)

    def scores_rows(self):
        return 3 * HD if self.cross else 3 * HD + 1

    def pe_rowmax(self, pe, g, js, b):
        for j in js:
            head, t = HG * g + j // T, j % T
            at = self.row(g, j)
            self.row_wait(pe, self.row_free, at, b, 0)
            pe.matmul(self.row_bank(at), self.qst[0:3 * HD, head, t * P:(t + 1) * P],
                      self.kst[0:3 * HD, head, :], start=True, stop=True).then_inc(self.row_full[at[0]], 1)

    def pe_turn_max(self, pe, g, b):
        self.row_wait(pe, self.row_free, self.row(g, self.ROWS - 2), b, 1)
        at = self.row(g, self.ROWS - 1)
        self.row_wait(pe, self.row_free, at, b, 0)
        pe.transpose(self.row_bank(at)[0:HG * T, 0:P], self.mx, self.m.ident[:]).then_inc(self.row_full[at[0]], 1)

    def pe_turn_x(self, pe, i, b):
        m = self.m
        at = self.xt_row(i)
        self.row_wait(pe, self.row_free, at, b, 0)
        if i == 0 and b is not None:
            pe.wait_ge(*self.at(self.norm.xn_ready, b * T + T))
        for c in range(C):
            last = pe.transpose(self.row_bank(at)[:, c * P:(c + 1) * P], m.xn[:, i, c * P:(c + 1) * P], m.ident[:])
        last.then_inc(self.row_full[at[0]], 1)

    def pe_values(self, pe, u, b, ones):
        g, kb = divmod(u, T)
        if not ones:
            for h in range(2):
                pe.wait_ge(*self.at(self.exp_done[h], b * NH + u + 1))
            if kb == 0 and g:
                pe.wait_ge(*self.at(self.ctx_free, (b * (C - 1) + g) * 2))
            if u == 0:
                pe.wait_ge(*self.at(self.normed, b * C))
        for j in range(HG):
            left = self.ones if ones else self.v[:, kb, HD * (HG * g + j):HD * (HG * g + j + 1)]
            last = pe.matmul(self.m.ps[HD * j:HD * (j + 1), 7 if ones else 6, :], left,
                             self.pt[:, u % 2, j * S:(j + 1) * S], start=kb == 0, stop=kb == T - 1,
                             tile_position=(0, HD * j))
        if ones:
            last.then_inc(self.pv_done, 1)

    def pe_proj(self, pe, n, b):
        m = self.m
        w, chunk = self.proj_of(n)
        item, c0 = ("proj", n), chunk * P
        if chunk == 0:
            self.weights.wait(pe, w)
        src = self.cth if self.cross and w == 0 else m.xt
        self.wait_free(pe, item, b)
        three_passes(pe, self.bank(item), [lambda c: m.w[:, w, 0, c, c0:c0 + P], lambda c: m.w[:, w, 1, c, c0:c0 + P]],
                     [lambda c: src[:, 0, c, :], lambda c: src[:, 1, c, :]], range(C), range(C)).then_inc(self.bank_full[self.place[item][0]], 1)

    def pe_rotate(self, pe, n, b):
        item = ("rot", n)
        self.wait_free(pe, item, b)
        self.wait_read(pe, ("proj", n), b)
        pe.matmul(self.bank(item), self.rot, self.qb[:, n % 2, :], start=True, stop=True).then_inc(self.bank_full[self.place[item][0]], 1)

    def pe(self, pe):
        m = self.m
        for i in range(T):
            self.pe_turn_x(pe, i, None)
        pe.wait_ge(*self.at(self.const, self.nconst))
        pe.wait_ge(*self.at(self.consts_done, 2 + self.cross * 5))
        with pe.Fori(0, NB) as b:
            for k in range(2):
                pe.wait_ge(*self.at(self.row_free[k], T // 2 + b * (self.row_items // 2)))
            for n in range(self.NPROJ):
                if self.cross and n == 2:
                    pe.wait_ge(*self.at(self.audio_low, b + 1))
                self.pe_proj(pe, n, b)
                if self.rope and n:
                    self.pe_rotate(pe, n - 1, b)
            if self.rope:
                self.pe_rotate(pe, self.NPROJ - 1, b)
            a = self.cth if self.cross else m.xt
            self.weights.wait(pe, 2)
            for i in range(T):
                item = ("v", i)
                self.wait_free(pe, item, b)
                j = self.first(self.WITH_V, i)
                for c in range(C):
                    last = three_passes(pe, self.bank(item), [lambda c: a[:, 0, c, i * P:(i + 1) * P], lambda c: a[:, 1, c, i * P:(i + 1) * P]],
                                        [lambda c: m.w[:, 2, 0, c, :], lambda c: m.w[:, 2, 1, c, :]], [c], [c], start=c == 0, stop=c == C - 1)
                    if c == C - 1:
                        last.then_inc(self.bank_full[self.place[item][0]], 1)
                    if not self.cross:
                        if i == 0 and c == 0:
                            pe.wait_ge(*self.at(self.stacked[0], (b + 1) * 24 * 16))
                        self.pe_rowmax(pe, 0, range(j, j + self.WITH_V[i][c]), b)
                        j += self.WITH_V[i][c]
                        if i == T - 1 and c == 0:
                            self.pe_turn_max(pe, 0, b)
            self.pe_heads(pe, b)
            self.weights.wait(pe, 3)
            for c in range(C):
                if c == 0:
                    pe.wait_ge(*self.at(self.cl, b * C + C - 1))
                if c == C - 1:
                    pe.wait_ge(*self.at(self.cl, b * C + C))
                for i in range(T):
                    item = ("out", i)
                    if c == 0:
                        self.wait_free(pe, item, b)
                    last = three_passes(pe, self.bank(item), [lambda c: self.ct[:, 0, c, i * P:(i + 1) * P], lambda c: self.ct[:, 1, c, i * P:(i + 1) * P]],
                                        [lambda c: m.w[:, 3, 0, c, :], lambda c: m.w[:, 3, 1, c, :]], [c], [c], start=c == 0, stop=c == C - 1)
                    if c == C - 1:
                        last.then_inc(self.bank_full[self.place[item][0]], 1)

    def pe_heads(self, pe, b):
        if self.cross:
            pe.wait_ge(*self.at(self.stacked[0], (b + 1) * 24 * 16))
        R = self.scores_rows()
        for u in range(NH):
            g, kb = divmod(u, T)
            if u == (2 * T if self.cross else T):
                pe.wait_ge(*self.at(self.stacked[1], (b + 1) * 24 * 16))
            slots, j = self.WITH_UNIT[kb], self.first(self.WITH_UNIT, kb)
            for step in range(5):
                if not self.cross and g + 1 < C:
                    self.pe_rowmax(pe, g + 1, range(j, j + slots[step]), b)
                    j += slots[step]
                    if kb == T - 1 and step == 0:
                        self.pe_turn_max(pe, g + 1, b)
                if step == 0 and kb == 0 and not self.cross:
                    pe.wait_ge(*self.at(self.mdma, (b * C + g + 1) * 16))
                if step < 2:
                    h = step
                    if u == 0:
                        for i in (2 * h, 2 * h + 1):
                            self.wait_read(pe, ("v", i), b)
                    else:
                        pe.wait_ge(*self.at((self.clipped if self.cross else self.exp_done)[h], b * NH + u))
                    for j4 in (2 * h, 2 * h + 1):
                        last = pe.matmul(self.m.ps[:, j4, :], self.kst[0:R, HG * g + j4, kb * P:(kb + 1) * P],
                                         self.qst[0:R, HG * g + j4, :], start=True, stop=True)
                    last.then_inc(self.st_full[h], 1)
                elif step < 4 and u:
                    self.pe_values(pe, u - 1, b, ones=step == 3)
                elif step == 4 and g == C - 1:
                    self.pe_turn_x(pe, kb, b)
        for i in range(T):
            self.wait_read(pe, ("v", i), b)
        self.pe_values(pe, NH - 1, b, ones=False)
        self.pe_values(pe, NH - 1, b, ones=True)

    def act_turn_x(self, act, i, b):
        at = self.xt_row(i)
        self.row_wait(act, self.row_full, at, b, 1)
        act.activation(self.m.xt[:, 0, :, i * P:(i + 1) * P], tile3(self.row_bank(at)), ACT.Copy).then_inc(self.xt_high, 1)

    def act_audio(self, act, n):
        raw = self.m.raw[:, 0]
        act.wait_ge(*self.at(self.audio_loaded, n * 16 + 16))
        act.activation(raw, raw, ACT.Copy, scale=WSCALE).then_inc(self.audio_scaled, 1)
        act.wait_ge(*self.at(self.audio_scaled, n + 1))
        act.activation(self.cth[:, 0], raw, ACT.Copy).then_inc(self.audio_high, 1)

    def act_context(self, act, g, b):
        act.wait_ge(*self.at(self.pv_done, b * NH + T * (g + 1)))
        act.wait_ge(*self.at(self.cl, b * C + g))
        act.activation(self.sums, self.m.ps[:, 7, :], ACT.Copy).then_inc(self.ctx_free, 1)
        act.activation(self.ctxn, self.m.ps[:, 6, :], ACT.Copy).then_inc(self.ctx_free, 1)

    def act_context_high(self, act, g, b):
        act.wait_ge(*self.at(self.normed, b * C + g + 1))
        act.activation(self.ct[:, 0, g, :], self.ctxn, ACT.Copy).then_inc(self.ch, 1)

    def act(self, act):
        descale = 1.0 / WSCALE
        for i in range(T):
            self.act_turn_x(act, i, None)
        for n in range(4):
            self.weights.act(act, n)
            if self.cross and n == 1:
                self.weights.wait(act, 0)
                self.act_audio(act, 0)
        act.wait_ge(*self.at(self.const, self.nconst))
        act.wait_ge(*self.at(self.consts_done, 2 + self.cross * 5))
        with act.Fori(0, NB) as b:
            for n in range(self.NPROJ):
                item = ("proj", n)
                w, c = self.proj_of(n)
                self.wait_full(act, item, b)
                if self.rope:
                    act.wait_ge(*self.at(self.t1_ready, b * self.NPROJ + max(n - 1, 0)))
                    if n >= 2:
                        self.wait_full(act, ("rot", n - 2), b)
                    elif n == 0:
                        act.wait_ge(*self.at(self.exp_done[0], b * NH))
                else:
                    act.wait_ge(*self.at(self.fl, b * self.NPROJ + max(n - 1, 0)))
                s = descale if w or not self.cross else descale / WSCALE
                act.activation(self.qb[:, n % 2, :], self.bank(item), ACT.Identity, scale=s,
                               bias=self.pb[:, C * w + c:C * w + c + 1]).then_inc(self.bank_free[self.place[item][0]], 1)
                if not self.rope:
                    self.wait_read(act, item, b)
                    act.activation(self.qf[:, w, 0, c, :], self.qb[:, n % 2, :], ACT.Copy).then_inc(self.fh, 1)
            for u in range(NH):
                g, kb = divmod(u, T)
                for h in range(2):
                    out = self.pt[:, u % 2, 2 * h * S:(2 * h + 2) * S]
                    if self.cross:
                        act.wait_ge(*self.at(self.clipped[h], b * NH + u + 1))
                        src = out
                    else:
                        act.wait_ge(*self.at(self.st_full[h], b * NH + u + 1))
                        act.wait_ge(*self.at(self.pv_done, b * NH + max(u - 1, 0)))
                        src = flat(self.m.ps[:, 2 * h:2 * h + 2, :])
                    act.activation(out, src, ACT.Exp, scale=SOFTMAX_SCALE).then_inc(self.exp_done[h], 1)
                if kb == 0 and g:
                    self.act_context(act, g - 1, b)
                if kb == T - 1 and g:
                    self.act_context_high(act, g - 1, b)
                if g == C - 1:
                    self.act_turn_x(act, kb, b)
                if self.cross and u == NH // 2:
                    self.act_audio(act, b + 1)
            self.act_context_high(act, C - 1, b)
        if self.rope:
            self.wait_full(act, ("out", T - 1), NB - 1)
            for n in range(NE):
                self.following.weights.act(act, n)

    def dve_rowmax(self, v, g, js, b):
        for j in js:
            at = self.row(g, j)
            self.row_wait(v, self.row_full, at, b, 1)
            v.tensor_reduce(self.mx[:, j:j + 1], self.row_bank(at), AX.X, ALU.max).then_inc(self.row_free[at[0]], 1)

    def dve_turn_max(self, v, g, b):
        at = self.row(g, self.ROWS - 1)
        self.row_wait(v, self.row_full, at, b, 1)
        v.wait_ge(*self.at(self.mdma, (b * C + g) * 16))
        v.tensor_scalar(self.mt[0:HG * T, :], self.row_bank(at)[0:HG * T, 0:P], 1.0 / MSCALE, None,
                        ALU.mult).then_inc(self.row_free[at[0]], 1)

    def dve_turn_x(self, v, i, b):
        m = self.m
        at = self.xt_row(i)
        v.wait_ge(*self.at(self.xt_high, (i if b is None else (b + 1) * T + i) + 1))
        v.tensor_tensor(m.xt[:, 1, :, i * P:(i + 1) * P], tile3(self.row_bank(at)), m.xt[:, 0, :, i * P:(i + 1) * P],
                        ALU.subtract).then_inc(self.row_free[at[0]], 1)

    def dve_invert(self, v, g, k, b):
        v.wait_ge(*self.at(self.ctx_free, (b * (C - 1) + g) * 2 + 1))
        part = self.sums[:, k * P:(k + 1) * P]
        v.reciprocal(part, part).then_inc(self.inverted, 1)

    def dve_last_context(self, v, b):
        g = C - 1
        v.wait_ge(*self.at(self.pv_done, (b + 1) * NH))
        v.wait_ge(*self.at(self.cl, b * C + g))
        v.reciprocal(self.sums, self.m.ps[:, 7, :]).then_inc(self.inverted, 4)
        v.wait_ge(*self.at(self.inverted, (b * C + C) * 4))
        v.tensor_tensor(self.ctxn, self.m.ps[:, 6, :], self.sums, ALU.mult).then_inc(self.normed, 1)
        v.wait_ge(*self.at(self.ch, b * C + C))
        v.tensor_tensor(self.ct[:, 1, g, :], self.ctxn, self.ct[:, 0, g, :], ALU.subtract).then_inc(self.cl, 1)

    def dve(self, v):
        m = self.m
        n = self.nconst
        v.memset(self.ones, 1.0).then_inc(self.consts_done, 1)
        for i in range(T):
            self.dve_turn_x(v, i, None)
        for k in range(4):
            self.weights.dve(v, k)
        if self.cross:
            v.wait_ge(*self.at(self.const, n))
            v.wait_ge(*self.at(self.consts_done, 2))
            top = 50.0 / SOFTMAX_SCALE
            v.tensor_scalar(self.hi, self.mask, 0.5, 2.0 * top, ALU.is_gt, ALU.mult).then_inc(self.consts_done, 1)
            v.tensor_scalar(self.rs, self.rs, 0.0, 0.3, ALU.max, ALU.min).then_inc(self.consts_done, 1)
            v.wait_ge(*self.at(self.consts_done, 4))
            v.tensor_scalar(self.hi, self.hi, -top, None, ALU.add).then_inc(self.consts_done, 1)
            v.tensor_scalar(self.rs64, self.rs, 1.0 / WSCALE, None, ALU.mult).then_inc(self.consts_done, 1)
            v.tensor_scalar(self.ob, self.ob, self.rs, None, ALU.mult).then_inc(self.consts_done, 1)
            v.wait_ge(*self.at(self.consts_done, 7))
        with v.Fori(0, NB) as b:
            if self.cross:
                nb = (b + 1) % NB
                self.norm.dve(v, b, lambda i: slot(m.x, nb * T + i), lambda i: m.xn[:, i, :])
            if self.rope:
                for n in range(self.NPROJ):
                    self.dve_rotate(v, n, b)
            if not self.cross:
                self.dve_rowmax(v, 0, range(HG * T), b)
                self.dve_turn_max(v, 0, b)
            for i in range(T):
                item = ("v", i)
                self.wait_full(v, item, b)
                v.scalar_tensor_tensor(out=self.v[:, i, :], in0=self.bank(item),
                                       scalar=1.0 / WSCALE / (WSCALE if self.cross else 1.0),
                                       in1=self.vb, op0=ALU.mult, op1=ALU.add).then_inc(self.bank_free[self.place[item][0]], 1)
            self.dve_heads(v, b)
            for i in range(T):
                item = ("out", i)
                self.wait_full(v, item, b)
                if self.cross:
                    v.scalar_tensor_tensor(out=self.delta[:, i, :], in0=self.bank(item), scalar=self.rs64, in1=self.ob,
                                           op0=ALU.mult, op1=ALU.add).then_inc(self.bank_free[self.place[item][0]], 1)
                else:
                    v.wait_ge(*self.at(self.bias_added, b * T + i + 1))
                    xs = slot(m.x, b * T + i)
                    v.scalar_tensor_tensor(out=xs, in0=self.bank(item), scalar=1.0 / WSCALE, in1=xs,
                                           op0=ALU.mult, op1=ALU.add).then_inc(self.bank_free[self.place[item][0]], 1)
            for i in range(T):
                self.wait_read(v, ("out", i), b)
            if self.cross:
                self.dve_delta(v, b)
            if self.rope:
                final = lambda i: slot(m.x, b * T + i)
                v.wait_ge(*self.at(self.xn_sent, b))
                v.tensor_copy(self.place_now, m.place[:, bass.ds(b * T, T)]).then_inc(self.place_ready, 1)
                self.ynorm.dve_moments(v, b, final)
                self.ynorm.dve_apply(v, b, final, lambda i: m.xn[:, i, :])
        if self.rope:
            for n in range(NE):
                self.following.weights.dve(v, n)

    def dve_rotate(self, v, n, b):
        item = ("rot", n)
        w, c = self.proj_of(n)
        self.wait_full(v, item, b)
        v.wait_ge(*self.at(self.rotated, b * self.NPROJ + n))
        v.tensor_tensor(self.t2, self.bank(item), self.sin, ALU.mult).then_inc(self.bank_free[self.place[item][0]], 1)
        self.wait_read(v, item, b)
        v.wait_ge(*self.at(self.t1_ready, b * self.NPROJ + n + 1))
        v.wait_ge(*self.at(self.fl, b * self.NPROJ + max(n - 1, 0)))
        v.tensor_tensor(self.qr[:, n % 2, :], self.t1[:, n % 2, :], self.t2, ALU.add).then_inc(self.rotated, 1)
        v.wait_ge(*self.at(self.rotated, b * self.NPROJ + n + 1))
        v.tensor_copy(self.qf[:, w, 0, c, :], self.qr[:, n % 2, :]).then_inc(self.fh, 1)

    def dve_delta(self, v, b):
        m = self.m
        self.dnorm.dve_moments(v, b, lambda i: self.delta[:, i, :])
        v.wait_ge(*self.at(self.dnorm.moments, b * T + T))
        for i in range(T):
            d = self.delta[:, i, :]
            v.scalar_tensor_tensor(out=d, in0=d, scalar=m.mv[:, i, 0:1], in1=self.gamma,
                                   op0=ALU.subtract, op1=ALU.mult).then_inc(self.scaled, 1)
        v.wait_ge(*self.at(self.dnorm.rstd_ready, b + 1))
        v.wait_ge(*self.at(self.bias_added, b * T + T))
        v.wait_ge(*self.at(self.scaled, b * T + T))
        for i in range(T):
            xs = slot(m.x, b * T + i)
            v.scalar_tensor_tensor(out=xs, in0=self.delta[:, i, :], scalar=m.rstd[:, i:i + 1], in1=xs,
                                   op0=ALU.mult, op1=ALU.add).then_inc(self.x_done, 1)
        v.wait_ge(*self.at(self.x_done, b * T + T))
        v.memset(m.carrier[:], 0.0)
        final = lambda i: slot(m.x, b * T + i)
        self.ynorm.dve_moments(v, b, final)
        self.ynorm.dve_apply(v, b, final, lambda i: m.xn[:, i, :])
        v.tensor_copy(m.final_mean[:, bass.ds(b * T, T)], m.mv[:, :, 0:1].rearrange("p t a -> p (t a)")).then_inc(self.kept, 1)
        v.tensor_copy(m.final_rstd[:, bass.ds(b * T, T)], m.rstd[:]).then_inc(self.kept, 1)
        v.wait_ge(*self.at(self.ynorm.xn_ready, b * T + T))
        v.tensor_reduce(slot_col(m.final_peak, b), flat(m.xn[:]), AX.X, ALU.max, apply_absolute_value=True).then_inc(self.peak, 1)
        v.wait_ge(*self.at(self.peak, b + 1))

    def dve_heads(self, v, b):
        m = self.m
        for u in range(NH):
            g, kb = divmod(u, T)
            if self.cross:
                for h in range(2):
                    v.wait_ge(*self.at(self.st_full[h], b * NH + u + 1))
                    v.wait_ge(*self.at(self.pv_done, b * NH + max(u - 1, 0)))
                    v.tensor_scalar(self.pt[:, u % 2, 2 * h * S:(2 * h + 2) * S], flat(m.ps[:, 2 * h:2 * h + 2, :]),
                                    slot_col(self.hi, b * T + kb), -50.0 / SOFTMAX_SCALE, ALU.min, ALU.max).then_inc(self.clipped[h], 1)
                    if g and kb in (1, 2):
                        self.dve_invert(v, g - 1, 2 * (kb - 1) + h, b)
            elif g + 1 < C:
                j = self.first(self.WITH_UNIT, kb)
                for n in range(sum(self.WITH_UNIT[kb])):
                    self.dve_rowmax(v, g + 1, [j + n], b)
                    if g and n % 2 and n // 2 < len(self.INVERT[kb]):
                        self.dve_invert(v, g - 1, self.INVERT[kb][n // 2], b)
                if kb == T - 1:
                    self.dve_turn_max(v, g + 1, b)
                    if g:
                        self.dve_invert(v, g - 1, T - 1, b)
            elif kb == 1:
                for n in range(4):
                    self.dve_invert(v, g - 1, n, b)
            if g == C - 1:
                self.dve_turn_x(v, kb, b)
            nb = (b + 1) % NB
            if u == T - 1 and not self.cross:
                if self.rope:
                    v.wait_ge(*m.x_all)
                self.norm.dve_moments(v, b, lambda i: slot(m.x, nb * T + i))
            if u == 2 * T - 1 and not self.cross:
                if self.rope:
                    v.wait_ge(*self.at(self.xn_sent, b))
                self.norm.dve_apply(v, b, lambda i: slot(m.x, nb * T + i), lambda i: m.xn[:, i, :])
        self.dve_last_context(v, b)

    def pool_context(self, g, c, b):
        g.wait_ge(*self.at(self.inverted, (b * C + c + 1) * 4))
        g.wait_ge(*self.at(self.ctx_free, (b * (C - 1) + c + 1) * 2))
        g.tensor_tensor(self.ctxn, self.ctxn, self.sums, ALU.mult).then_inc(self.normed, 1)
        g.wait_ge(*self.at(self.ch, b * C + c + 1))
        g.tensor_tensor(self.ct[:, 1, c, :], self.ctxn, self.ct[:, 0, c, :], ALU.subtract).then_inc(self.cl, 1)

    def pool(self, g):
        m = self.m
        g.memset(self.kst[3 * HD:3 * HD + 1].rearrange("p h t -> p (h t)"), -MSCALE).then_inc(self.consts_done, 1)
        g.wait_ge(*self.at(self.const, self.nconst))
        g.wait_ge(*self.at(self.consts_done, 2 + self.cross * 5))
        if self.cross:
            self.pool_audio(g, 0)
        if self.rope:
            g.wait_ge(*m.zero_filled)
        with g.Fori(0, NB) as b:
            if self.cross:
                self.norm.pool(g, b)
            g.wait_ge(*self.at(self.norm.xn_ready, b * T))
            for n in range(self.NPROJ):
                if self.rope:
                    self.wait_read(g, ("proj", n), b)
                    g.wait_ge(*self.at(self.rotated, b * self.NPROJ + max(n - 1, 0)))
                    g.tensor_tensor(self.t1[:, n % 2, :], self.qb[:, n % 2, :], self.cos, ALU.mult).then_inc(self.t1_ready, 1)
                    if n:
                        self.pool_low(g, n - 1, b)
                else:
                    self.pool_low(g, n, b)
            if self.rope:
                self.pool_low(g, self.NPROJ - 1, b)
                g.wait_ge(*m.x_all)
            for i in range(T):
                xs = slot(m.x, b * T + i)
                g.tensor_tensor(xs, xs, self.beta if self.cross else self.ob, ALU.add).then_inc(self.bias_added, 1)
            if not self.cross:
                self.norm.pool(g, b)
            for c in range(C - 1):
                if c == C - 2 and self.cross:
                    self.pool_audio(g, b + 1)
                self.pool_context(g, c, b)
            if self.cross:
                self.dnorm.pool(g, b)
                self.ynorm.pool(g, b)
            if self.rope:
                self.ynorm.pool(g, b)
                g.wait_ge(*self.at(self.ynorm.xn_ready, b * T + T))
                g.wait_ge(*self.at(self.place_ready, b + 1))
                g.tensor_tensor(self.pool_carrier, m.eps[:, 0:1], m.eps[:, 1:2], ALU.add)
                for i in range(T):
                    g.indirect_dma_start(self.io["sorted_x"][:, :], bass.IndirectOffsetOnAxis(self.place_now[:, i:i + 1], 0),
                                         m.xn[:, i, :], None).then_inc(self.scattered, 16)
                g.wait_ge(self.scattered, (b + 1) * (16 * T))
                g.sem_inc(self.xn_sent, 1)

    def pool_audio(self, g, n):
        g.wait_ge(*self.at(self.audio_high, n + 1))
        g.tensor_tensor(flat(self.cth[:, 1]), flat(self.m.raw[:, 0]), flat(self.cth[:, 0]), ALU.subtract).then_inc(self.audio_low, 1)

    def pool_low(self, g, n, b):
        src = self.qr if self.rope else self.qb
        w, c = self.proj_of(n)
        g.wait_ge(*self.at(self.fh, b * self.NPROJ + n + 1))
        g.tensor_tensor(self.qf[:, w, 1, c, :], src[:, n % 2, :], self.qf[:, w, 0, c, :],
                        ALU.subtract).then_inc(self.fl, 1)


def slot_col(ap, i):
    return ap[:, bass.ds(i, 1)]


def flat(ap):
    return ap.rearrange("p a b -> p (a b)")


class Experts(Phase):

    DEPTH = 3

    def __init__(self, m, name, mats, bufs, early):
        super().__init__(m, name)
        self.weights = Weights(self, mats, bufs, early)
        take = m.take
        self.positive, self.junk = take(SIGN_PART), take(SIGN_PART)
        pair = lambda dt=F32: take(2 * D, dt).rearrange("p (n d) -> p n d", n=2)
        self.xs, self.gate, self.a, self.ys = pair(), pair(), pair(), pair()
        self.ahl = take(4 * D, F16).rearrange("p (n a d) -> p n a d", n=2, a=2)
        assert m.used <= ARENA - C * INNER
        self.norm = Norm(m, "norm", 1)
        s = self.sem
        self.part_loaded = self.sems("part_loaded", 2, 16 * SIGN_PARTS)
        self.pos_done, self.sign_done, self.abs_done = s("positive", 2 * SIGN_PARTS), self.sems("signs_made", 2, SIGN_PARTS), self.sems("abs_summed", 2, SIGN_PARTS)
        n = [(NSLOT + 1) // 2, NSLOT // 2]
        by2 = lambda name, per=1: [s(f"{name}{k}", per * n[k]) for k in range(2)]
        m.gathered = [self.sem_from_zero(f"gathered{b}", 16 * T) for b in range(NB)]
        self.slot_loaded, self.slot_stored = by2("slot_loaded", 16), by2("slot_stored", 16)
        self.turned, self.x_high, self.x_low = by2("slot_turned"), by2("slot_high"), by2("slot_low")
        self.up_full, self.gated, self.multiplied = by2("up_full"), by2("silu_done"), by2("act_made")
        self.a_high, self.a_low, self.y_full, self.y_out = by2("act_high"), by2("act_low"), by2("y_full"), by2("y_out")

    def steps(self, step, eng):
        def one(s):
            step(eng, s // 2, s % 2, lambda d: 0 <= s - d < NSLOT)
        peeled, last = 4, NSLOT // 2 * 2
        for s in range(peeled):
            one(s)
        with eng.Fori(peeled // 2, last // 2) as r:
            for j in range(2):
                step(eng, r, j, lambda d: True)
        for s in range(last, NSLOT + self.DEPTH):
            one(s)

    @staticmethod
    def behind(r, j, d):
        return (j - d) % 2, r + (j - d) // 2

    def rows(self, name, s):
        return self.io[name][bass.ds(s * P, P), :] if not isinstance(s, int) else self.io[name][s * P:(s + 1) * P, :]

    def part(self, r, j):
        q = (r - 2) * 2 + j
        return q if not isinstance(q, int) or 0 <= q < 2 * SIGN_PARTS else None

    def load_part(self, sp, r, j):
        sp.wait_ge(*self.at(self.sign_done[j], r - 2))
        sp.wait_ge(*self.at(self.abs_done[j], r - 2))
        sp.dma_start(flat(self.m.raw[:, j])[:, 0:SIGN_PART], self.rows("ffn_parts", (r - 2) * 2 + j)).then_inc(self.part_loaded[j], 16)

    def act_part(self, act, r, j):
        act.wait_ge(*self.at(self.part_loaded[j], 16 * (r - 1)))
        act.wait_ge(*self.at(self.abs_done[1 - j], r - 2 + j))
        q = (r - 2) * 2 + j
        act.activation(self.junk, flat(self.m.raw[:, j])[:, 0:SIGN_PART], ACT.Abs,
                       accum_out=self.m.abs_sums[:, q:q + 1] if isinstance(q, int) else slot_col(self.m.abs_sums, q)).then_inc(self.abs_done[j], 1)

    def dve_part(self, v, r, j):
        raw = flat(self.m.raw[:, j])[:, 0:SIGN_PART]
        q = (r - 2) * 2 + j
        v.wait_ge(*self.at(self.part_loaded[j], 16 * (r - 1)))
        v.wait_ge(*self.at(self.sign_done[1 - j], r - 2 + j))
        v.tensor_scalar(self.positive, raw, 0.0, None, ALU.is_gt).then_inc(self.pos_done, 1)
        v.wait_ge(*self.at(self.pos_done, q + 1))
        v.scalar_tensor_tensor(out=self.m.signs[:, bass.ds(q * SIGN_PART, SIGN_PART)], in0=raw, scalar=0.0,
                               in1=self.positive, op0=ALU.is_lt, op1=ALU.subtract).then_inc(self.sign_done[j], 1)

    def sp_step(self, sp, r, j, has):
        if has(0):
            sp.wait_ge(*self.at(self.turned[j], r))
            sp.dma_start(self.xs[:, j, :], self.rows("sorted_x", r * 2 + j)).then_inc(self.slot_loaded[j], 16)
        if has(3):
            k, n = self.behind(r, j, 3)
            sp.wait_ge(*self.at(self.y_out[k], n + 1))
            sp.dma_start(self.rows("sorted_y", r * 2 + j - 3), self.ys[:, k, :]).then_inc(self.slot_stored[k], 16)
        if self.part(r, j) is not None:
            self.load_part(sp, r, j)

    def sp(self, sp):
        self.steps(self.sp_step, sp)
        for k in range(2):
            sp.wait_ge(*self.at(self.sign_done[k], SIGN_PARTS))
            sp.wait_ge(*self.at(self.abs_done[k], SIGN_PARTS))
        self.sp_following(sp)

    def sp_early(self, sp):
        self.weights.sp_early(sp)

    def expert_of(self, pe, s):
        at = self.m.slot_expert[0:1, s:s + 1] if isinstance(s, int) else self.m.slot_expert[0:1, bass.ds(s, 1)]
        return pe.value_load(at, min_val=0, max_val=NE - 1)

    def pe_step(self, pe, r, j, has):
        m = self.m
        if has(0):
            pe.wait_ge(*self.at(self.slot_loaded[j], 16 * (r + 1)))
            pe.wait_ge(*self.at(self.x_low[j], r))
            for c in range(C):
                last = pe.transpose(m.ps[:, j, c * P:(c + 1) * P], self.xs[:, j, c * P:(c + 1) * P], m.ident[:])
            last.then_inc(self.turned[j], 1)
        if has(1):
            k, n = self.behind(r, j, 1)
            e = self.expert_of(pe, r * 2 + j - 1)
            w = lambda a, c, cols: m.w[:, bass.ds(e, 1), a, c, cols].rearrange("p e o -> p (e o)")
            pe.wait_ge(*self.at(self.x_low[k], n + 1))
            pe.wait_ge(*self.at(self.multiplied[k], n))
            for f in range(C):
                cols = slice(f * P, (f + 1) * P)
                last = three_passes(pe, m.ps[:, 2 + k, cols], [lambda c: w(0, c, cols), lambda c: w(1, c, cols)],
                                    [lambda c: m.xt[:, 0, c, k * P:(k + 1) * P], lambda c: m.xt[:, 1, c, k * P:(k + 1) * P]],
                                    range(C), range(C))
            last.then_inc(self.up_full[k], 1)
        if has(2):
            k, n = self.behind(r, j, 2)
            e = self.expert_of(pe, r * 2 + j - 2)
            w2 = lambda a, f: m.w[:, bass.ds(e, 1), a, f, :].rearrange("p e o -> p (e o)")
            pe.wait_ge(*self.at(self.a_low[k], n + 1))
            pe.wait_ge(*self.at(self.y_out[k], n))
            three_passes(pe, m.ps[:, 4 + k, :], [lambda f: self.ahl[:, k, 0, f * P:(f + 1) * P], lambda f: self.ahl[:, k, 1, f * P:(f + 1) * P]],
                         [lambda f: w2(0, f), lambda f: w2(1, f)], range(C), range(C)).then_inc(self.y_full[k], 1)

    def pe(self, pe):
        self.steps(self.pe_step, pe)

    def act_step(self, act, r, j, has):
        m = self.m
        if has(0):
            act.wait_ge(*self.at(self.turned[j], r + 1))
            act.wait_ge(*self.at(self.up_full[j], r))
            act.activation(m.xt[:, 0, :, j * P:(j + 1) * P], tile3(m.ps[:, j, :]), ACT.Copy).then_inc(self.x_high[j], 1)
        if has(1):
            k, n = self.behind(r, j, 1)
            act.wait_ge(*self.at(self.up_full[k], n + 1))
            act.wait_ge(*self.at(self.multiplied[k], n))
            act.activation(self.gate[:, k, :], m.ps[:, 2 + k, :], ACT.Silu, scale=1.0 / WSCALE).then_inc(self.gated[k], 1)
        if has(2):
            k, n = self.behind(r, j, 2)
            act.wait_ge(*self.at(self.y_full[k], n + 1))
            act.wait_ge(*self.at(self.slot_stored[k], 16 * n))
            act.activation(self.ys[:, k, :], m.ps[:, 4 + k, :], ACT.Copy, scale=1.0 / WSCALE).then_inc(self.y_out[k], 1)
        if self.part(r, j) is not None:
            self.act_part(act, r, j)

    def act(self, act):
        self.steps(self.act_step, act)

    def dve_step(self, v, r, j, has):
        m = self.m
        if has(0):
            v.wait_ge(*self.at(self.x_high[j], r + 1))
            v.tensor_tensor(m.xt[:, 1, :, j * P:(j + 1) * P], tile3(m.ps[:, j, :]), m.xt[:, 0, :, j * P:(j + 1) * P],
                            ALU.subtract).then_inc(self.x_low[j], 1)
        if has(1):
            k, n = self.behind(r, j, 1)
            v.wait_ge(*self.at(self.gated[k], n + 1))
            v.wait_ge(*self.at(self.a_low[k], n))
            v.scalar_tensor_tensor(out=self.a[:, k, :], in0=m.ps[:, 2 + k, :], scalar=1.0 / WSCALE, in1=self.gate[:, k, :],
                                   op0=ALU.mult, op1=ALU.mult).then_inc(self.multiplied[k], 1)
            v.wait_ge(*self.at(self.multiplied[k], n + 1))
            v.wait_ge(*self.at(self.y_full[k], n))
            v.tensor_copy(self.ahl[:, k, 0, :], self.a[:, k, :]).then_inc(self.a_high[k], 1)
            v.wait_ge(*self.at(self.a_high[k], n + 1))
            v.tensor_tensor(self.ahl[:, k, 1, :], self.a[:, k, :], self.ahl[:, k, 0, :], ALU.subtract).then_inc(self.a_low[k], 1)
        if self.part(r, j) is not None:
            self.dve_part(v, r, j)

    def dve(self, v):
        m = self.m
        self.steps(self.dve_step, v)
        m.wait_back(v, 0)
        self.norm.dve_moments(v, 0, lambda i: m.x[:, i, :])
        self.norm.dve_apply(v, 0, lambda i: m.x[:, i, :], lambda i: m.xn[:, i, :])

    def pool(self, g):
        m = self.m
        for k in range(2):
            g.wait_ge(*self.at(self.slot_stored[k], 16 * ((NSLOT + 1 - k) // 2)))
        m.take_back(g, 0)
        self.norm.pool(g, 0)


class BitMlp(Phase):

    DEPTH = 4

    def __init__(self, m, name):
        super().__init__(m, name)
        take = m.take
        self.b1, self.b2 = take(INNER), take(D)
        self.h = take(4 * INNER).rearrange("p (n f) -> p n f", n=4)
        self.q2 = take(2 * INNER, F16).rearrange("p (n f) -> p n f", n=2)
        self.q2t = take(2 * INNER, F16).rearrange("p (n f) -> p n f", n=2)
        self.junk = take(INNER)
        self.q1f = take(T * D).rearrange("p (t d) -> p t d", t=T)
        self.q1 = take(T * D, F16).rearrange("p (t d) -> p t d", t=T)
        self.ms, self.am, self.r, self.top, self.inv, self.f, self.alpha = (take(2 * T) for _ in range(7))
        self.alpha1 = take(T)
        self.negmean, self.absum2 = take(2), take(2)
        assert m.used <= ARENA - C * INNER
        self.signs = m.signs
        s = self.sem
        self.const = s("const_loaded", 32)
        self.abs2, self.allred, self.mean_done = s("abs_totalled", 1), s("abs_all", 1), s("means_ready", 1)
        self.norm = Norm(m, "norm", NB)
        u = 1 + NB * (T + 1)
        self.bank_full, self.bank_free = self.sems("bank_full", 4, u), self.sems("bank_free", 4, u)
        self.t_full, self.t_free = self.sems("turn_full", 2, NB * T), self.sems("turn_free", 2, NB * T)
        self.y_full, self.y_free = self.sems("y_full", 2, NB * 2), self.sems("y_free", 2, NB * 2)
        self.input_chain = s("input_chain", (NB + 1) * self.INPUT)
        self.factor_chain, self.rounded = s("factor_chain", NB * T * self.FACTOR), s("rounded", NB * T)
        self.power1, self.powered1 = s("power1_wanted", NB + 1), s("power1_ready", NB + 1)
        self.power2, self.powered2 = s("power2_wanted", NB * T), s("power2_ready", NB * T)
        self.input_scaled, self.input_rounded = s("input_scaled", (NB + 1) * T), s("input_rounded", NB + 1)
        self.alpha1_ready = s("alpha1_ready", NB + 1)
        self.q1_done = s("q1_done", (NB + 1) * T)
        self.gelu_done, self.ss_done, self.scaled, self.q2_done = (s(n, NB * T) for n in ("gelu_done", "squares_summed", "scaled", "q2_done"))
        self.bias_added = s("bias_added", NB * T)

    INPUT = 3 + 5
    FACTOR = 1 + 5

    def sp(self, sp):
        io, m = self.io, self.m
        row = lambda a, n: a.rearrange("(a n) -> a n", a=1).broadcast_to([P, n])
        sp.dma_start(self.b1, row(io["L0_ffn_b1"], INNER)).then_inc(self.const, 16)
        sp.dma_start(self.b2, row(io["L0_ffn_b2"], D)).then_inc(self.const, 16)
        self.sp_following(sp)
        sp.wait_ge(*self.at(self.const, 32))

    def steps(self, step, eng):
        for i in range(T):
            step(eng, 0, i, lambda k: i >= k, first=True)
        with eng.Fori(1, NB) as b:
            for i in range(T):
                step(eng, b, i, lambda k: True)
        for i in range(self.DEPTH):
            step(eng, NB, i, lambda k: i < k)

    def pe_turn_input(self, pe, turn):
        m = self.m
        for i in range(T):
            pe.wait_ge(*self.at(self.q1_done, turn * T + i + 1))
            pe.wait_ge(*self.at(self.bank_free[i], turn * (T + 1)))
            for c in range(C):
                last = pe.transpose(m.ps[:, i, 0:256].bitcast(F16)[:, c * P:(c + 1) * P], self.q1[:, i, c * P:(c + 1) * P], m.ident16[:])
            last.then_inc(self.bank_full[i], 1)

    def pe_step(self, pe, b, i, has, first=False):
        m, sg = self.m, self.signs
        tile, k3 = b * T + i - 3, (i - 3) % 2
        if has(3):
            pe.wait_ge(*self.at(self.q2_done, tile + 1))
            for k in range(2):
                pe.wait_ge(*self.at(self.t_free[k], tile))
                for c in range(8):
                    last = pe.transpose(m.ps[:, 4 + k, :].bitcast(F16)[:, c * P:(c + 1) * P],
                                        self.q2[:, k3, (8 * k + c) * P:(8 * k + c + 1) * P], m.ident16[:])
                last.then_inc(self.t_full[k], 1)
        if has(0):
            pe.wait_ge(*self.at(self.bank_free[i], b * (T + 1) + 1))
            for n in range(4):
                pe.wait_ge(*self.at(self.bank_free[n], b * (T + 1) + 1 + i))
                for c in range(C):
                    last = pe.matmul(m.ps[:, n, :], m.xt[:, 0, c, i * P:(i + 1) * P],
                                     sg[:, c * INNER + n * 512:c * INNER + (n + 1) * 512], start=c == 0, stop=c == C - 1)
                last.then_inc(self.bank_full[n], 1)
        if has(3):
            pe.wait_ge(*self.at(self.y_free[k3], b * 2 + (i - 3) // 2))
            for c in range(NI):
                if c % 8 == 0:
                    pe.wait_ge(*self.at(self.t_free[c // 8], tile + 1))
                last = pe.matmul(m.ps[:, 6 + k3, :], self.q2t[:, k3, c * P:(c + 1) * P],
                                 sg[:, C * INNER + c * D:C * INNER + (c + 1) * D], start=c == 0, stop=c == NI - 1)
            last.then_inc(self.y_full[k3], 1)
        if has(0) and i == T - 1:
            self.pe_turn_input(pe, b + 1)

    def pe(self, pe):
        self.pe_turn_input(pe, 0)
        self.steps(self.pe_step, pe)

    def act_turn_input(self, act, turn):
        m = self.m
        for i in range(T):
            act.wait_ge(*self.at(self.bank_full[i], turn * (T + 1) + 1))
            act.activation(m.xt[:, 0, :, i * P:(i + 1) * P], tile3(m.ps[:, i, 0:256].bitcast(F16)), ACT.Copy).then_inc(self.bank_free[i], 1)

    def act_scale_input(self, act, turn):
        for i in range(T):
            act.wait_ge(*self.at(self.input_chain, (turn + 1) * self.INPUT))
            act.activation(self.q1f[:, i, :], self.m.xn[:, i, :], ACT.Copy, scale=self.f[:, i:i + 1]).then_inc(self.input_scaled, 1)

    def act_step(self, act, b, i, has, first=False):
        m = self.m
        tile = b * T + i
        if has(3):
            for k in range(2):
                act.wait_ge(*self.at(self.t_full[k], tile - 3 + 1))
                act.activation(self.q2t[:, (i - 3) % 2, k * 1024:(k + 1) * 1024], m.ps[:, 4 + k, :].bitcast(F16), ACT.Copy).then_inc(self.t_free[k], 1)
        if has(0):
            h = self.h[:, i, :]
            act.wait_ge(*self.at(self.bank_free[3], b * (T + 1) + 2 + i))
            act.activation(h, h, ACT.Gelu).then_inc(self.gelu_done, 1)
            if i == T - 1:
                self.act_turn_input(act, b + 1)
            act.wait_ge(*self.at(self.gelu_done, tile + 1))
            act.wait_ge(*self.at(self.ss_done, tile))
            act.activation(self.junk, h, ACT.Square, accum_out=self.ms[:, T + i:T + i + 1]).then_inc(self.ss_done, 1)
        if has(1):
            k = (i - 1) % T
            h = self.h[:, k, :]
            act.wait_ge(*self.at(self.factor_chain, tile * self.FACTOR))
            act.activation(h, h, ACT.Copy, scale=self.f[:, T + k:T + k + 1]).then_inc(self.scaled, 1)
        if has(0) and i == 2:
            self.act_scale_input(act, b + 1)

    def act(self, act):
        self.act_scale_input(act, 0)
        self.act_turn_input(act, 0)
        self.steps(self.act_step, act)

    def row_factors(self, v, ch, cols, dim, which):
        c = cols
        d = dim ** -0.5
        ch.put(v.scalar_tensor_tensor(out=self.top[:, c], in0=self.r[:, c], scalar=d, in1=self.am[:, c], op0=ALU.mult, op1=ALU.mult))
        ch.wait(v)
        ch.put(v.tensor_scalar(self.top[:, c], self.top[:, c], 1e-5, None, ALU.max))
        ch.wait(v)
        ch.put(v.reciprocal(self.inv[:, c], self.top[:, c]))
        ch.put(v.tensor_scalar(self.alpha[:, c], self.top[:, c], self.negmean[:, which:which + 1], 1.0 / 127.0, ALU.mult, ALU.mult))
        ch.wait(v)
        ch.put(v.scalar_tensor_tensor(out=self.f[:, c], in0=self.inv[:, c], scalar=127.0 * d, in1=self.r[:, c], op0=ALU.mult, op1=ALU.mult))

    def dve_input_rows(self, v, ch, turn):
        m, c4 = self.m, slice(0, T)
        ch.put(v.tensor_reduce(self.am[:, c4], m.xn[:], AX.X, ALU.max, apply_absolute_value=True))
        ch.put(v.tensor_tensor(self.ms[:, c4], m.mv[:, :, 1:2].rearrange("p t a -> p (t a)"), m.rstd[:], ALU.mult))
        ch.wait(v)
        ch.put(v.tensor_tensor(self.ms[:, c4], self.ms[:, c4], m.rstd[:], ALU.mult))
        ch.wait(v)
        v.tensor_scalar(self.f[:, c4], self.ms[:, c4], 1e-6, None, ALU.add).then_inc(self.power1, 1)

    def dve_input_factors(self, v, ch, turn):
        v.wait_ge(*self.at(self.powered1, turn + 1))
        self.row_factors(v, ch, slice(0, T), D, 0)
        ch.wait(v)
        ch.close()

    def dve_input_round(self, v, turn):
        q1f = flat(self.q1f)
        v.wait_ge(*self.at(self.input_scaled, (turn + 1) * T))
        v.tensor_scalar(q1f, q1f, 127.0, MAGIC, ALU.min, ALU.add).then_inc(self.input_rounded, 1)
        v.wait_ge(*self.at(self.input_rounded, turn + 1))
        for i in range(T):
            v.tensor_scalar(self.q1[:, i, :], self.q1f[:, i, :], MAGIC - 128.0, MAGIC, ALU.max, ALU.subtract).then_inc(self.q1_done, 1)

    def dve_step(self, v, b, i, has, first=False):
        m = self.m
        tile = b * T + i
        if has(1):
            k = (i - 1) % T
            col = slice(T + k, T + k + 1)
            ch1 = Chain(self, self.factor_chain, self.FACTOR, tile - 1)
            v.wait_ge(*self.at(self.gelu_done, tile))
            ch1.put(v.tensor_reduce(self.am[:, col], self.h[:, k, :], AX.X, ALU.max, apply_absolute_value=True))
            v.wait_ge(*self.at(self.ss_done, tile))
            v.tensor_scalar(self.f[:, col], self.ms[:, col], 1.0 / INNER, 1e-6, ALU.mult, ALU.add).then_inc(self.power2, 1)
        if has(0):
            for n in range(4):
                v.wait_ge(*self.at(self.bank_full[n], b * (T + 1) + 2 + i))
                if n == 0 and i == 0:
                    v.wait_ge(*self.at(self.alpha1_ready, b + 1))
                v.scalar_tensor_tensor(out=self.h[:, i, n * 512:(n + 1) * 512], in0=m.ps[:, n, :], scalar=self.alpha1[:, i:i + 1],
                                       in1=self.b1[:, n * 512:(n + 1) * 512], op0=ALU.mult, op1=ALU.add).then_inc(self.bank_free[n], 1)
        if has(1):
            v.wait_ge(*self.at(self.powered2, tile))
            ch1.wait(v)
            self.row_factors(v, ch1, col, INNER, 1)
            ch1.close()
        if has(2):
            k = (i - 2) % T
            h = self.h[:, k, :]
            v.wait_ge(*self.at(self.scaled, tile - 1))
            v.tensor_scalar(h, h, 127.0, MAGIC, ALU.min, ALU.add).then_inc(self.rounded, 1)
            v.wait_ge(*self.at(self.rounded, tile - 1))
            v.tensor_scalar(self.q2[:, k % 2, :], h, MAGIC - 128.0, MAGIC, ALU.max, ALU.subtract).then_inc(self.q2_done, 1)
        if has(4):
            k = i % 2
            v.wait_ge(*self.at(self.y_full[k], (b - 1) * 2 + i // 2 + 1))
            v.wait_ge(*self.at(self.bias_added, tile - 3))
            xs = slot(m.x, (b - 1) * T + i)
            v.scalar_tensor_tensor(out=xs, in0=m.ps[:, 6 + k, :], scalar=self.alpha[:, T + i:T + i + 1], in1=xs,
                                   op0=ALU.mult, op1=ALU.add).then_inc(self.y_free[k], 1)
        if has(0):
            nb = (b + 1) % NB
            if i == 0:
                if first:
                    m.wait_back(v, 1)
                self.norm.dve_moments(v, b, lambda i: slot(m.x, nb * T + i))
            if i == 1:
                self.norm.dve_apply(v, b, lambda i: slot(m.x, nb * T + i), lambda i: m.xn[:, i, :])
                v.wait_ge(*self.at(self.norm.xn_ready, b * T + T))
                self.chi = Chain(self, self.input_chain, self.INPUT, b + 1)
                self.dve_input_rows(v, self.chi, b + 1)
            if i == 2:
                self.dve_input_factors(v, self.chi, b + 1)
            if i == T - 1:
                self.dve_input_round(v, b + 1)
            if i == T - 1 and first:
                m.wait_back(v, 2, 3)
            if i == T - 1:
                v.wait_ge(*self.at(self.bank_free[3], b * (T + 1) + 2 + i))
                v.tensor_copy(self.alpha1, self.alpha[:, 0:T]).then_inc(self.alpha1_ready, 1)

    def dve(self, v):
        m = self.m
        v.tensor_reduce(self.absum2, m.abs_sums[:].rearrange("p (a n) -> p a n", a=2), AX.X, ALU.add).then_inc(self.abs2, 1)
        ch = Chain(self, self.input_chain, self.INPUT, 0)
        self.dve_input_rows(v, ch, 0)
        v.wait_ge(*self.at(self.allred, 1))
        v.tensor_scalar(self.negmean, self.negmean, -1.0 / (INNER * D), None, ALU.mult).then_inc(self.mean_done, 1)
        v.wait_ge(*self.at(self.mean_done, 1))
        self.dve_input_factors(v, ch, 0)
        self.dve_input_round(v, 0)
        v.tensor_copy(self.alpha1, self.alpha[:, 0:T]).then_inc(self.alpha1_ready, 1)
        v.wait_ge(*self.at(self.const, 32))
        self.steps(self.dve_step, v)

    def pool_root1(self, g, turn):
        g.wait_ge(*self.at(self.power1, turn + 1))
        g.tensor_tensor(self.r[:, 0:T], self.f[:, 0:T], self.m.mhalf[:], ALU.pow).then_inc(self.powered1, 1)

    def pool_step(self, g, b, i, has, first=False):
        m = self.m
        if has(1):
            col = slice(T + (i - 1) % T, T + (i - 1) % T + 1)
            g.wait_ge(*self.at(self.power2, b * T + i))
            g.tensor_tensor(self.r[:, col], self.f[:, col], m.mhalf[:, 0:1], ALU.pow).then_inc(self.powered2, 1)
        if has(0):
            if i == 0:
                if first:
                    m.take_back(g, 2)
                self.norm.pool(g, b)
            if i == 1:
                self.pool_root1(g, b + 1)
            xs = slot(m.x, b * T + i)
            g.tensor_tensor(xs, xs, self.b2, ALU.add).then_inc(self.bias_added, 1)
            if i == 2 and first:
                m.take_back(g, 3)
            if i == 3 and first:
                m.wait_back(g, 1, 2, 3)

    def pool(self, g):
        m = self.m
        g.wait_ge(*self.at(self.abs2, 1))
        g.partition_all_reduce(self.negmean, self.absum2, P, RADD).then_inc(self.allred, 1)
        self.pool_root1(g, 0)
        m.take_back(g, 1)
        g.wait_ge(*self.at(self.const, 32))
        self.steps(self.pool_step, g)


class Fp8Linear(Phase):

    def __init__(self, m, name):
        super().__init__(m, name)
        take = m.take
        tiles = lambda a: a.rearrange("p (n d) -> p n d", n=T)
        self.val, self.pw, self.q = tiles(take(T * D)), tiles(take(T * D)), tiles(take(T * D, F16))
        self.bias = take(D)
        self.top, self.ws, self.ws64 = take(4), take(1), take(1)
        self.factor, self.shift = take(NB * T), take(NB * T)
        s = self.sem
        self.weight_loaded, self.const = s("weight_loaded0", 16), s("const_loaded", 32)
        self.whigh, self.wlow, self.peak = s("weight_high", 1), s("weight_low", 1), s("peaks", 1)
        self.allred, self.scale = s("peak_all", 1), s("scale_ready", 5)
        self.val_done, self.power_cut, self.power_done, self.summed = (s(n, NB * T) for n in ("val_done", "power_cut", "power_done", "summed"))
        self.q_done = self.sems("q_done", 4, NB)
        self.bank_full, self.bank_free = self.sems("bank_full", 4, NB), self.sems("bank_free", 4, NB)
        self.y_full, self.y_free = self.sems("y_full", 4, NB), self.sems("y_free", 4, NB)
        self.bias_added, self.stored = s("bias_added", NB * T), s("stored", 16 * NB * T)

    def sp_early(self, sp):
        sp.dma_start(self.m.raw[:, 0], self.io["L1_ffn_weightT"].rearrange("(c p) o -> p c o", p=P)).then_inc(self.weight_loaded, 16)

    def sp(self, sp):
        io, m = self.io, self.m
        row = lambda a, n: a.rearrange("(a n) -> a n", a=1).broadcast_to([P, n])
        sp.dma_start(self.ws, row(io["L1_ffn_weight_scale"], 1)).then_inc(self.const, 16)
        sp.dma_start(self.bias, row(io["L1_ffn_bias"], D)).then_inc(self.const, 16)
        sp.wait_ge(*self.at(self.const, 32))
        with sp.Fori(0, NB) as b:
            for i in range(T):
                sp.wait_ge(*self.at(self.y_free[i], b + 1))
                sp.dma_start(io["out"][bass.ds(b, 1), i * P:(i + 1) * P, :].rearrange("b p d -> p (b d)"),
                             slot(m.x, b * T + i)).then_inc(self.stored, 16)
        sp.wait_ge(*self.at(self.stored, 16 * NB * T))

    def pe(self, pe):
        m = self.m
        with pe.Fori(0, NB) as b:
            for i in range(T):
                pe.wait_ge(*self.at(self.q_done[i], b + 1))
                pe.wait_ge(*self.at(self.bank_free[i], b))
                for c in range(C):
                    last = pe.transpose(m.ps[:, i, 0:256].bitcast(F16)[:, c * P:(c + 1) * P],
                                        self.q[:, i, c * P:(c + 1) * P], m.ident16[:])
                last.then_inc(self.bank_full[i], 1)
            for i in range(T):
                pe.wait_ge(*self.at(self.bank_free[i], b + 1))
                pe.wait_ge(*self.at(self.y_free[i], b))
                if i == 0:
                    pe.wait_ge(*self.at(self.wlow, 1))
                for c in range(C):
                    for a in range(2):
                        last = pe.matmul(m.ps[:, 4 + i, :], m.xt[:, 0, c, i * P:(i + 1) * P], m.w[:, 0, a, c, :],
                                         start=c == 0 and a == 0, stop=c == C - 1 and a == 1)
                last.then_inc(self.y_full[i], 1)

    def act_values(self, act, b):
        for i in range(T):
            act.wait_ge(*self.at(self.q_done[i], b))
            tile = b * T + i
            act.activation(self.val[:, i, :], slot(self.m.x, tile), ACT.Identity, scale=slot_col(self.factor, tile),
                           bias=slot_col(self.shift, tile)).then_inc(self.val_done, 1)

    def act_turned(self, act, b):
        m = self.m
        for i in range(T):
            act.wait_ge(*self.at(self.bank_full[i], b + 1))
            act.activation(m.xt[:, 0, :, i * P:(i + 1) * P], tile3(m.ps[:, i, 0:256].bitcast(F16)), ACT.Copy).then_inc(self.bank_free[i], 1)

    def act(self, act):
        m = self.m
        act.wait_ge(*self.at(self.scale, 1))
        act.wait_ge(*self.at(self.weight_loaded, 16))
        act.activation(m.w[:, 0, 0], m.raw[:, 0], ACT.Copy, scale=self.ws64).then_inc(self.whigh, 1)
        act.wait_ge(*self.at(self.scale, 5))
        self.act_values(act, 0)
        with act.Fori(1, NB) as b:
            self.act_values(act, b)
            self.act_turned(act, b - 1)
        self.act_turned(act, NB - 1)

    def dve_round(self, v, b):
        tile = b * T
        val, pw = (lambda i: self.val[:, i, :]), (lambda i: self.pw[:, i, :])
        for i in range(T):
            v.wait_ge(*self.at(self.val_done, tile + i + 1))
            v.wait_ge(*self.at(self.q_done[i], b))
            v.tensor_scalar(pw(i).bitcast(I32), val(i).bitcast(I32), 0x7F800000, None, ALU.bitwise_and).then_inc(self.power_cut, 1)
        for i in range(T):
            v.wait_ge(*self.at(self.power_cut, tile + i + 1))
            v.tensor_scalar(pw(i), pw(i), 2.0 ** -6, 1.5 * 2.0 ** 20, ALU.max, ALU.mult).then_inc(self.power_done, 1)
        for i in range(T):
            v.wait_ge(*self.at(self.power_done, tile + i + 1))
            v.tensor_tensor(val(i), val(i), pw(i), ALU.add).then_inc(self.summed, 1)
        for i in range(T):
            v.wait_ge(*self.at(self.summed, tile + i + 1))
            v.wait_ge(*self.at(self.bank_full[i], b))
            v.tensor_tensor(self.q[:, i, :], val(i), pw(i), ALU.subtract).then_inc(self.q_done[i], 1)

    def dve_sum(self, v, b):
        for i in range(T):
            v.wait_ge(*self.at(self.y_full[i], b + 1))
            v.wait_ge(*self.at(self.bias_added, b * T + i + 1))
            xs = slot(self.m.x, b * T + i)
            v.scalar_tensor_tensor(out=xs, in0=self.m.ps[:, 4 + i, :], scalar=1.0 / WSCALE, in1=xs,
                                   op0=ALU.mult, op1=ALU.add).then_inc(self.y_free[i], 1)

    def dve(self, v):
        m = self.m
        v.tensor_reduce(self.top[:, 0:1], m.final_peak[:], AX.X, ALU.max).then_inc(self.peak, 1)
        v.wait_ge(*self.at(self.const, 32))
        v.tensor_scalar(self.ws64, self.ws, WSCALE, None, ALU.mult).then_inc(self.scale, 1)
        v.wait_ge(*self.at(self.allred, 1))
        v.tensor_scalar(self.top[:, 2:3], self.top[:, 1:2], 1.0 / 448.0, 1e-7, ALU.mult, ALU.max).then_inc(self.scale, 1)
        v.wait_ge(*self.at(self.scale, 2))
        v.reciprocal(self.top[:, 3:4], self.top[:, 2:3]).then_inc(self.scale, 1)
        v.wait_ge(*self.at(self.scale, 3))
        v.tensor_scalar(self.factor, m.final_rstd[:], self.top[:, 3:4], None, ALU.mult).then_inc(self.scale, 1)
        v.wait_ge(*self.at(self.scale, 4))
        v.scalar_tensor_tensor(out=self.shift, in0=m.final_mean[:], scalar=-1.0, in1=self.factor,
                               op0=ALU.mult, op1=ALU.mult).then_inc(self.scale, 1)
        self.dve_round(v, 0)
        v.wait_ge(*self.at(self.whigh, 1))
        v.scalar_tensor_tensor(out=flat(m.w[:, 0, 1]), in0=flat(m.raw[:, 0]), scalar=self.ws64,
                               in1=flat(m.w[:, 0, 0]), op0=ALU.mult, op1=ALU.subtract).then_inc(self.wlow, 1)
        with v.Fori(1, NB) as b:
            self.dve_round(v, b)
            self.dve_sum(v, b - 1)
        self.dve_sum(v, NB - 1)

    def pool(self, g):
        m = self.m
        g.wait_ge(*self.at(self.peak, 1))
        g.partition_all_reduce(self.top[:, 1:2], self.top[:, 0:1], P, RMAX).then_inc(self.allred, 1)
        g.wait_ge(*self.at(self.const, 32))
        with g.Fori(0, NB) as b:
            for i in range(T):
                g.wait_ge(*self.at(self.val_done, b * T + i + 1))
                xs = slot(m.x, b * T + i)
                g.tensor_tensor(xs, xs, self.bias, ALU.add).then_inc(self.bias_added, 1)


def program(nc, io, stages):
    with ExitStack() as ctx:
        m = Machine(nc, ctx, io)
        phases = stages(m, io)
        for ph, following in zip(phases, phases[1:]):
            ph.following = following
        block = ctx.enter_context(nc.Block())

        @block.tensor
        def _(pe):
            m.barrier(pe, 0)
            for k, ph in enumerate(phases):
                ph.pe(pe)
                m.barrier(pe, k + 1)

        @block.scalar
        def _(act):
            m.barrier(act, 0)
            for k, ph in enumerate(phases):
                ph.act(act)
                m.barrier(act, k + 1)

        @block.vector
        def _(v):
            m.barrier(v, 0)
            for k, ph in enumerate(phases):
                ph.dve(v)
                m.barrier(v, k + 1)

        @block.gpsimd
        def _(g):
            m.barrier(g, 0)
            for k, ph in enumerate(phases):
                ph.pool(g)
                m.barrier(g, k + 1)

        @block.sync
        def _(sp):
            for name, sem in m.sems.items():
                if m.first[name]:
                    sp.sem_inc(sem, 1)
            m.barrier(sp, 0)
            for k, ph in enumerate(phases):
                ph.sp(sp)
                m.barrier(sp, k + 1)


def decoder(nc, io):
    def stages(m, t):
        qkv = t["L1_attn_w_qkvT"]
        k, q, v = qkv[:, D:2 * D], qkv[:, 0:D], qkv[:, 2 * D:3 * D]
        return [Start(m),
                Attention(m, "attn0", [t["L0_attn_k_wT"], t["L0_attn_q_wT"], t["L0_attn_v_wT"], t["L0_attn_out_wT"]], m.raws * 2, 2,
                          t["L0_attn_q_b_cols"], t["L0_attn_k_b_cols"], t["L0_attn_v_b"], t["L0_attn_out_b"], rope=True),
                Experts(m, "experts", [t["ctxT"][e * D:(e + 1) * D, :] for e in range(NE)], m.raws + [m.turned, m.raws[0]], 3),
                BitMlp(m, "bit"),
                Attention(m, "attn1", [k, q, v, t["L1_attn_w_outT"]], m.raws * 2, 2,
                          t["L1_attn_q_b_cols"], t["L1_attn_k_b_cols"], t["L1_attn_v_b"], t["L1_attn_b_out"]),
                Attention(m, "xattn", [t["L1_xattn_WkT"], t["L1_xattn_WqT"], t["L1_xattn_WvT"], t["L1_xattn_WoT"]], [m.raws[1], *m.tails, m.tails[0]], 3,
                          t["L1_xattn_bq_cols"], t["L1_xattn_bk_cols"], t["L1_xattn_bv"], t["L1_xattn_bo"], cross=True),
                Fp8Linear(m, "fp8")]
    program(nc, io, stages)


def layout(inputs):
    import numpy as np
    a = {k: np.ascontiguousarray(v) for k, v in inputs.items()}
    for k in ("L0_attn_q_w", "L0_attn_k_w", "L0_attn_v_w", "L0_attn_out_w", "L0_ffn_w1", "L0_ffn_w2", "L1_attn_w_qkv",
              "L1_attn_w_out", "L1_xattn_Wq", "L1_xattn_Wk", "L1_xattn_Wv", "L1_xattn_Wo", "L1_ffn_weight"):
        a[k + "T"] = np.ascontiguousarray(a.pop(k).T)
    a["ctxT"] = np.ascontiguousarray(a.pop("ctx_2048").transpose(0, 2, 1)).reshape(NB * D, S)
    w1 = a.pop("L0_ffn_w1T").reshape(C, P, INNER // SIGN_PART, SIGN_PART).transpose(0, 2, 1, 3)
    w2 = a.pop("L0_ffn_w2T").reshape(NI * D // SIGN_PART, SIGN_PART // D, P, D).transpose(0, 2, 1, 3)
    a["ffn_parts"] = np.ascontiguousarray(np.concatenate([w1.reshape(-1, SIGN_PART), w2.reshape(-1, SIGN_PART)]))
    for k in ("L1_xattn_residual_scale", "L1_ffn_weight_scale"):
        a[k] = a[k].reshape(1)
    cols = lambda v: np.ascontiguousarray(v.reshape(-1, P).T)
    b1 = a["L1_attn_b_qkv"]
    a["L1_attn_q_b_cols"], a["L1_attn_k_b_cols"], a["L1_attn_v_b"] = cols(b1[0:D]), cols(b1[D:2 * D]), np.ascontiguousarray(b1[2 * D:])
    for k in ("L0_attn_q_b", "L0_attn_k_b", "L1_xattn_bq", "L1_xattn_bk"):
        a[k + "_cols"] = cols(a.pop(k))
    a["mask_cols"] = cols(a.pop("mask_BxS2_ik0"))
    a["itok_cols"] = cols(a.pop("itok_BxS_13_99985"))
    a["triangle"] = np.triu(np.ones((P, P), np.float32), 1)
    a["slot_starts"] = np.tile(P * np.arange(NSLOT, dtype=np.float32), (P, 1))
    a["ident"] = np.eye(P, dtype=np.float32)
    half = HD // 2
    inv = (np.float32(1.0) / np.float32(10000.0) ** (np.arange(0, HD, 2, dtype=np.float32) / np.float32(HD))).astype(np.float32)
    angle = (np.arange(S, dtype=np.float32)[None, :] * inv[:, None]).astype(np.float32)
    angle = np.tile(angle, (2 * HG, 1))
    a["rope_cos"], a["rope_sin"] = np.cos(angle).astype(np.float32), np.sin(angle).astype(np.float32)
    rot = np.zeros((P, P), np.float32)
    for o in range(P):
        first = o % HD < half
        rot[o + half if first else o - half, o] = -1.0 if first else 1.0
    a["rope_rot"] = rot
    return a


def kernel(**inputs):
    import concourse.bacc as bacc
    from concourse import mybir as _mybir
    from concourse.bass_utils import run_bass_kernel_spmd as run

    nc = bacc.Bacc("TRN2", target_bir_lowering=False, num_devices=1)
    arrays = layout(inputs)
    io = {k: nc.dram_tensor(f"in_{k}", v.shape, _mybir.dt.from_np(v.dtype), kind="ExternalInput").ap() for k, v in arrays.items()}
    for name in ("sorted_x", "sorted_y"):
        io[name] = nc.dram_tensor(name, (NSLOT * P, D), F32, kind="Internal").ap()
    io["out"] = nc.dram_tensor("out", (NB, S, D), F32, kind="ExternalOutput").ap()
    decoder(nc, io)
    r = run(nc, [{f"in_{k}": v for k, v in arrays.items()}], core_ids=[0])
    return r.results[0]["out"]
```
